# Optimizing a Trainium2 kernel written in Bass

```python
import numpy as np
import jax
import jax.numpy as jnp

def _softmax(x, axis=-1):
    return jax.nn.softmax(x, axis=axis)

def _gelu(x):
    return jax.nn.gelu(x, approximate=True)

def _silu(x):
    return jax.nn.silu(x)

def _sigmoid(x):
    return jax.nn.sigmoid(x)

def _layernorm(x, axis=-1, eps=1e-05):
    m = jnp.mean(x, axis=axis, keepdims=True)
    v = jnp.var(x, axis=axis, keepdims=True)
    return (x - m) / jnp.sqrt(v + eps)

def _scatter_add(tgt, idx, src, axis=0):
    return tgt.at[idx].add(src)

def _segment_sum(src, seg, n):
    return jax.ops.segment_sum(src, seg, n)
kernel_name = 'mk_recurrent_d2_jaxref_r8_963ed3'

def setup_inputs(seed: int=0):
    np.random.seed(seed)
    _w = jnp.asarray

    def _L0_attn_setup():
        import jax, jax.numpy as jnp
        import numpy as np
        B, S, D_MODEL, H, D = (2, 256, 128, 16, 64)
        SCALE = 1.0 / float(np.sqrt(D))

        def _rope(t, c, s):
            d2 = t.shape[-1] // 2
            t1, t2 = (t[..., :d2], t[..., d2:])
            return jnp.concatenate([t1 * c - t2 * s, t1 * s + t2 * c], axis=-1)
        key = jax.random.key(seed)
        ks = jax.random.split(key, 5)
        x = jax.random.normal(ks[0], (B, S, D_MODEL), jnp.float32)
        qkv_w = jax.random.normal(ks[1], (3 * H * D, D_MODEL), jnp.float32) * 0.02
        out_w = jax.random.normal(ks[2], (D_MODEL, H * D), jnp.float32) * 0.02
        bias_p = jax.random.uniform(ks[3], (H, 1, 1), jnp.float32) * 2.0
        bias_a = jax.random.uniform(ks[4], (H, 1, 1), jnp.float32)
        rope_freqs = 10000.0 ** (-jnp.arange(D // 2, dtype=jnp.float32) / (D // 2))
        return {'x': x, 'qkv_w': qkv_w, 'out_w': out_w, 'bias_p': bias_p, 'bias_a': bias_a, 'rope_freqs': rope_freqs}
    _L0_attn_in = _L0_attn_setup()

    def _L0_ffn_setup():
        import math
        import jax, jax.numpy as jnp
        import numpy as np
        HIDDEN = 128
        INTER = 512
        EXPERTS = 8
        B, T = (4, 256)
        EPS = 1e-12
        CAP_FACTOR = 1.0
        MIN_CAP = 4

        def layer_norm(x, g, b, eps=EPS):
            m = jnp.mean(x, axis=-1, keepdims=True)
            v = jnp.var(x, axis=-1, keepdims=True)
            return (x - m) * jax.lax.rsqrt(v + eps) * g + b

        def top1_gate(x, wg, capacity):
            logits = x @ wg
            gates = jax.nn.softmax(logits, axis=-1)
            E = wg.shape[-1]
            idx = jnp.argmax(gates, axis=-1)
            mask1 = jax.nn.one_hot(idx, E, dtype=gates.dtype)
            locations = jnp.cumsum(mask1, axis=0) - mask1
            mask1 = mask1 * (locations < capacity).astype(gates.dtype)
            gates1_s = jnp.sum(gates * mask1, axis=-1)
            loc_s = jnp.sum(locations * mask1, axis=-1).astype(jnp.int32)
            loc_oh = jax.nn.one_hot(loc_s, capacity, dtype=gates.dtype)
            combine = gates1_s[:, None, None] * mask1[:, :, None] * loc_oh[:, None, :]
            dispatch = jax.lax.stop_gradient((combine > 0).astype(x.dtype))
            return (combine, dispatch)
        key = jax.random.key(seed)
        ks = jax.random.split(key, 8)
        s = 0.02
        return {'x': jax.random.normal(ks[0], (B, T, HIDDEN), jnp.float32), 'attn_nw': jnp.ones((HIDDEN,), jnp.float32), 'attn_nb': jnp.zeros((HIDDEN,), jnp.float32), 'wg': jax.random.normal(ks[1], (HIDDEN, EXPERTS), jnp.float32) * s, 'inter_w': jax.random.normal(ks[2], (EXPERTS, HIDDEN, INTER), jnp.float32) * s, 'inter_b': jnp.zeros((EXPERTS, INTER), jnp.float32), 'output_w': jax.random.normal(ks[3], (EXPERTS, INTER, HIDDEN), jnp.float32) * s, 'output_b': jnp.zeros((EXPERTS, HIDDEN), jnp.float32), 'res_inter_w': jax.random.normal(ks[4], (HIDDEN, INTER), jnp.float32) * s, 'res_inter_b': jnp.zeros((INTER,), jnp.float32), 'res_output_w': jax.random.normal(ks[5], (INTER, HIDDEN), jnp.float32) * s, 'res_output_b': jnp.zeros((HIDDEN,), jnp.float32), 'res_coef': jax.random.normal(ks[6], (HIDDEN, 2), jnp.float32) * s}
    _L0_ffn_in = _L0_ffn_setup()

    def _L1_attn_setup():
        import jax, jax.numpy as jnp
        import numpy as np
        B, T, D, H = (4, 256, 128, 16)
        E = D // H
        DH = D // 4
        key = jax.random.key(seed)
        ks = jax.random.split(key, 9)
        s = D ** (-0.5)
        return {'x': jax.random.normal(ks[0], (B, T, D), jnp.float32), 'q_w': jax.random.normal(ks[1], (D, D), jnp.float32) * s, 'k_w': jax.random.normal(ks[2], (D, D), jnp.float32) * s, 'v_w': jax.random.normal(ks[3], (D, D), jnp.float32) * s, 'o_w': jax.random.normal(ks[4], (D, D), jnp.float32) * s, 'cs_w1': jax.random.normal(ks[5], (DH, D), jnp.float32) * s, 'cs_b1': jnp.zeros((DH,), jnp.float32), 'cs_w2': jax.random.normal(ks[6], (H, DH), jnp.float32) * DH ** (-0.5), 'cs_b2': jnp.zeros((H,), jnp.float32), 'decay_params': jax.random.normal(ks[7], (H, E), jnp.float32) + 3.0}
    _L1_attn_in = _L1_attn_setup()

    def _L1_ffn_setup():
        import jax, jax.numpy as jnp
        import numpy as np
        B, S, D, F, E, R = (4, 256, 128, 512, 8, 4)
        key = jax.random.key(seed)
        ks = jax.random.split(key, 8)
        s_in = 1.0 / np.sqrt(D)
        s_ff = 1.0 / np.sqrt(F)
        return {'hidden_states': jax.random.normal(ks[0], (B, S, D), jnp.float32), 'gate_W': jax.random.normal(ks[1], (E, D), jnp.float32) * s_in, 'gate_b': jnp.zeros((E,), jnp.float32), 'wi_W': jax.random.normal(ks[2], (F, D), jnp.float32) * s_in, 'wi_b': jnp.zeros((F,), jnp.float32), 'wo_W': jax.random.normal(ks[3], (D, F), jnp.float32) * s_ff, 'wo_b': jnp.zeros((D,), jnp.float32), 'lora_A': jax.random.normal(ks[4], (E, R, D), jnp.float32) * s_in, 'lora_B': jax.random.normal(ks[5], (E, F, R), jnp.float32) * 0.02}
    _L1_ffn_in = _L1_ffn_setup()
    _d = {'L0_attn_x': _L0_attn_in['x'], 'L0_attn_qkv_w': _L0_attn_in['qkv_w'], 'L0_attn_out_w': _L0_attn_in['out_w'], 'L0_attn_bias_p': _L0_attn_in['bias_p'], 'L0_attn_bias_a': _L0_attn_in['bias_a'], 'L0_attn_rope_freqs': _L0_attn_in['rope_freqs'], 'L0_ffn_attn_nw': _L0_ffn_in['attn_nw'], 'L0_ffn_attn_nb': _L0_ffn_in['attn_nb'], 'L0_ffn_wg': _L0_ffn_in['wg'], 'L0_ffn_inter_w': _L0_ffn_in['inter_w'], 'L0_ffn_inter_b': _L0_ffn_in['inter_b'], 'L0_ffn_output_w': _L0_ffn_in['output_w'], 'L0_ffn_output_b': _L0_ffn_in['output_b'], 'L0_ffn_res_inter_w': _L0_ffn_in['res_inter_w'], 'L0_ffn_res_inter_b': _L0_ffn_in['res_inter_b'], 'L0_ffn_res_output_w': _L0_ffn_in['res_output_w'], 'L0_ffn_res_output_b': _L0_ffn_in['res_output_b'], 'L0_ffn_res_coef': _L0_ffn_in['res_coef'], 'L1_attn_q_w': _L1_attn_in['q_w'], 'L1_attn_k_w': _L1_attn_in['k_w'], 'L1_attn_v_w': _L1_attn_in['v_w'], 'L1_attn_o_w': _L1_attn_in['o_w'], 'L1_attn_cs_w1': _L1_attn_in['cs_w1'], 'L1_attn_cs_b1': _L1_attn_in['cs_b1'], 'L1_attn_cs_w2': _L1_attn_in['cs_w2'], 'L1_attn_cs_b2': _L1_attn_in['cs_b2'], 'L1_attn_decay_params': _L1_attn_in['decay_params'], 'L1_ffn_gate_W': _L1_ffn_in['gate_W'], 'L1_ffn_gate_b': _L1_ffn_in['gate_b'], 'L1_ffn_wi_W': _L1_ffn_in['wi_W'], 'L1_ffn_wi_b': _L1_ffn_in['wi_b'], 'L1_ffn_wo_W': _L1_ffn_in['wo_W'], 'L1_ffn_wo_b': _L1_ffn_in['wo_b'], 'L1_ffn_lora_A': _L1_ffn_in['lora_A'], 'L1_ffn_lora_B': _L1_ffn_in['lora_B']}
    _x0 = _d['L0_attn_x']
    _d['L0_attn_x'] = jax.random.normal(jax.random.fold_in(jax.random.key(seed), 1), (4, 1024, 128), dtype=_x0.dtype)
    del _x0
    return _d

def reference(L0_attn_x, L0_attn_qkv_w, L0_attn_out_w, L0_attn_bias_p, L0_attn_bias_a, L0_attn_rope_freqs, L0_ffn_attn_nw, L0_ffn_attn_nb, L0_ffn_wg, L0_ffn_inter_w, L0_ffn_inter_b, L0_ffn_output_w, L0_ffn_output_b, L0_ffn_res_inter_w, L0_ffn_res_inter_b, L0_ffn_res_output_w, L0_ffn_res_output_b, L0_ffn_res_coef, L1_attn_q_w, L1_attn_k_w, L1_attn_v_w, L1_attn_o_w, L1_attn_cs_w1, L1_attn_cs_b1, L1_attn_cs_w2, L1_attn_cs_b2, L1_attn_decay_params, L1_ffn_gate_W, L1_ffn_gate_b, L1_ffn_wi_W, L1_ffn_wi_b, L1_ffn_wo_W, L1_ffn_wo_b, L1_ffn_lora_A, L1_ffn_lora_B):

    def _L0_attn_ref(x, qkv_w, out_w, bias_p, bias_a, rope_freqs):
        import jax, jax.numpy as jnp
        import numpy as np
        B, S, D_MODEL, H, D = (2, 256, 128, 16, 64)
        SCALE = 1.0 / float(np.sqrt(D))

        def _rope(t, c, s):
            d2 = t.shape[-1] // 2
            t1, t2 = (t[..., :d2], t[..., d2:])
            return jnp.concatenate([t1 * c - t2 * s, t1 * s + t2 * c], axis=-1)
        Bb, Ss, _ = x.shape
        qkv = (x @ qkv_w.T).reshape(Bb, Ss, 3, H, D)
        q = qkv[:, :, 0].transpose(0, 2, 1, 3)
        k = qkv[:, :, 1].transpose(0, 2, 1, 3)
        v = qkv[:, :, 2].transpose(0, 2, 1, 3)
        pos = jnp.arange(Ss, dtype=jnp.float32)
        ang = pos[:, None] * rope_freqs[None, :]
        c = jnp.cos(ang)[None, None]
        s = jnp.sin(ang)[None, None]
        q = _rope(q, c, s)
        k = _rope(k, c, s)
        scores = jnp.einsum('bhqd,bhkd->bhqk', q, k) * SCALE
        p = jnp.maximum(bias_p, 0.01)
        a = jnp.maximum(bias_a, 0.01)
        dist = jnp.abs(pos[None, :] - pos[:, None])
        kb = -p * jnp.log1p(a * dist)
        attn = jax.nn.softmax(scores + kb[None], axis=-1)
        out = jnp.einsum('bhqk,bhkd->bhqd', attn, v)
        out = out.transpose(0, 2, 1, 3).reshape(Bb, Ss, H * D)
        return out @ out_w.T

    def _L0_ffn_ref(x, attn_nw, attn_nb, wg, inter_w, inter_b, output_w, output_b, res_inter_w, res_inter_b, res_output_w, res_output_b, res_coef):
        import math
        import jax, jax.numpy as jnp
        import numpy as np
        HIDDEN = 128
        INTER = 512
        EXPERTS = 8
        B, T = (4, 256)
        EPS = 1e-12
        CAP_FACTOR = 1.0
        MIN_CAP = 4

        def layer_norm(x, g, b, eps=EPS):
            m = jnp.mean(x, axis=-1, keepdims=True)
            v = jnp.var(x, axis=-1, keepdims=True)
            return (x - m) * jax.lax.rsqrt(v + eps) * g + b

        def top1_gate(x, wg, capacity):
            logits = x @ wg
            gates = jax.nn.softmax(logits, axis=-1)
            E = wg.shape[-1]
            idx = jnp.argmax(gates, axis=-1)
            mask1 = jax.nn.one_hot(idx, E, dtype=gates.dtype)
            locations = jnp.cumsum(mask1, axis=0) - mask1
            mask1 = mask1 * (locations < capacity).astype(gates.dtype)
            gates1_s = jnp.sum(gates * mask1, axis=-1)
            loc_s = jnp.sum(locations * mask1, axis=-1).astype(jnp.int32)
            loc_oh = jax.nn.one_hot(loc_s, capacity, dtype=gates.dtype)
            combine = gates1_s[:, None, None] * mask1[:, :, None] * loc_oh[:, None, :]
            dispatch = jax.lax.stop_gradient((combine > 0).astype(x.dtype))
            return (combine, dispatch)
        Bx, Tx, M = x.shape
        S = Bx * Tx
        E = wg.shape[-1]
        capacity = max(MIN_CAP, math.ceil(S / E * CAP_FACTOR))
        residual = x.reshape(S, M)
        attn_out = layer_norm(residual, attn_nw, attn_nb)
        combine, dispatch = top1_gate(attn_out, wg, capacity)
        dispatched = jnp.einsum('sec,sm->ecm', dispatch, attn_out)
        h = jax.nn.gelu(jnp.einsum('ecm,emi->eci', dispatched, inter_w) + inter_b[:, None, :], approximate=True)
        expert_out = jnp.einsum('eci,eim->ecm', h, output_w) + output_b[:, None, :]
        moe_out = jnp.einsum('sec,ecm->sm', combine, expert_out)
        rh = jax.nn.gelu(attn_out @ res_inter_w + res_inter_b, approximate=True)
        res_mlp_out = rh @ res_output_w + res_output_b
        coef = jax.nn.softmax(attn_out @ res_coef, axis=-1)
        out = res_mlp_out * coef[:, :1] + moe_out * coef[:, 1:]
        out = out + residual
        return out.reshape(Bx, Tx, M)

    def _L1_attn_ref(x, q_w, k_w, v_w, o_w, cs_w1, cs_b1, cs_w2, cs_b2, decay_params):
        import jax, jax.numpy as jnp
        import numpy as np
        B, T, D, H = (4, 256, 128, 16)
        E = D // H
        DH = D // 4
        Bx, Tx, Dx = x.shape
        q = (x @ q_w.T).reshape(Bx, Tx, H, E)
        k = (x @ k_w.T).reshape(Bx, Tx, H, E)
        v = (x @ v_w.T).reshape(Bx, Tx, H, E)
        lc = jax.nn.sigmoid(jnp.tanh(x @ cs_w1.T + cs_b1) @ cs_w2.T + cs_b2)
        base = jax.nn.sigmoid(decay_params)[None, None]
        lam = jnp.clip(base * (1.0 + 0.2 * lc[..., None]), 0.0, 0.9995)

        def step(state, inp):
            qt, kt, vt, dt = inp
            state = state * dt[..., None] + kt[..., None] * vt[:, :, None, :]
            out_t = jnp.einsum('bhe,bhef->bhf', qt, state)
            return (state, out_t)
        init = jnp.zeros((Bx, H, E, E), x.dtype)
        xs = (jnp.swapaxes(q, 0, 1), jnp.swapaxes(k, 0, 1), jnp.swapaxes(v, 0, 1), jnp.swapaxes(lam, 0, 1))
        _, ys = jax.lax.scan(step, init, xs)
        y = jnp.swapaxes(ys, 0, 1).reshape(Bx, Tx, Dx)
        return y @ o_w.T

    def _L1_ffn_ref(hidden_states, gate_W, gate_b, wi_W, wi_b, wo_W, wo_b, lora_A, lora_B):
        import jax, jax.numpy as jnp
        import numpy as np
        B, S, D, F, E, R = (4, 256, 128, 512, 8, 4)
        x = hidden_states
        logits = jnp.einsum('bsd,ed->bse', x, gate_W) + gate_b
        top1 = jnp.argmax(jax.nn.softmax(logits, axis=-1), axis=-1)
        base = jnp.einsum('bsd,fd->bsf', x, wi_W) + wi_b
        out = jnp.zeros_like(x)
        for i in range(lora_A.shape[0]):
            lora = jnp.einsum('bsr,fr->bsf', jnp.einsum('bsd,rd->bsr', x, lora_A[i]), lora_B[i])
            inter = jax.nn.relu(base + lora)
            expert_out = jnp.einsum('bsf,df->bsd', inter, wo_W) + wo_b
            mask = (top1 == i).astype(x.dtype)[..., None]
            out = out + mask * expert_out
        return out
    x = L0_attn_x
    xn = _layernorm(x, axis=-1)
    s = _L0_attn_ref(xn, L0_attn_qkv_w, L0_attn_out_w, L0_attn_bias_p, L0_attn_bias_a, L0_attn_rope_freqs)
    g = _silu(_L0_ffn_ref(xn, L0_ffn_attn_nw, L0_ffn_attn_nb, L0_ffn_wg, L0_ffn_inter_w, L0_ffn_inter_b, L0_ffn_output_w, L0_ffn_output_b, L0_ffn_res_inter_w, L0_ffn_res_inter_b, L0_ffn_res_output_w, L0_ffn_res_output_b, L0_ffn_res_coef))
    x = x + s * g
    xn = _layernorm(x, axis=-1)
    s = _L1_attn_ref(xn, L1_attn_q_w, L1_attn_k_w, L1_attn_v_w, L1_attn_o_w, L1_attn_cs_w1, L1_attn_cs_b1, L1_attn_cs_w2, L1_attn_cs_b2, L1_attn_decay_params)
    g = _silu(_L1_ffn_ref(xn, L1_ffn_gate_W, L1_ffn_gate_b, L1_ffn_wi_W, L1_ffn_wi_b, L1_ffn_wo_W, L1_ffn_wo_b, L1_ffn_lora_A, L1_ffn_lora_B))
    x = x + s * g
    return x

_drawn_inputs = setup_inputs


def setup_inputs(seed=0):
    import zlib

    import numpy as np

    out = dict(_drawn_inputs(seed))
    spreads = {'L0_ffn_attn_nw': (1.0, 0.6),
     'L0_ffn_attn_nb': (0.0, 0.8),
     'L0_ffn_inter_b': (0.0, 0.8),
     'L0_ffn_output_b': (0.0, 0.8),
     'L0_ffn_res_inter_b': (0.0, 0.8),
     'L0_ffn_res_output_b': (0.0, 0.8),
     'L1_attn_cs_b1': (0.0, 0.1),
     'L1_attn_cs_b2': (0.0, 0.1),
     'L1_ffn_gate_b': (0.0, 1.704),
     'L1_ffn_wi_b': (0.0, 0.1),
     'L1_ffn_wo_b': (0.0, 0.1)}
    factors = {'L0_attn_bias_p': 3.171,
     'L0_attn_bias_a': 3.803,
     'L0_attn_rope_freqs': 64.0,
     'L0_ffn_wg': 8.0,
     'L0_ffn_inter_w': 8.0,
     'L0_ffn_output_w': 8.0,
     'L0_ffn_res_inter_w': 8.0,
     'L0_ffn_res_output_w': 8.0,
     'L0_ffn_res_coef': 8.0}
    for name, (base, spread) in spreads.items():
        noise = np.random.default_rng([zlib.crc32(name.encode()), seed]).standard_normal(out[name].shape)
        drawn = base * np.exp(spread * noise) if base else spread * noise
        out[name] = jnp.asarray(drawn.astype(out[name].dtype))
    for name, factor in factors.items():
        out[name] = (out[name] * factor).astype(out[name].dtype)
    return out
```

```python
from contextlib import ExitStack
import math

import concourse.bass as bass
from concourse import mybir

ALU = mybir.AluOpType
ACT = mybir.ActivationFunctionType
AX_X = mybir.AxisListType.X
F32 = mybir.dt.float32
BF16 = mybir.dt.bfloat16
I32 = mybir.dt.int32
U32 = mybir.dt.uint32

P = 128
B, S, D = 4, 1024, 128
NT = B * S // P
BT = S // P
H, DH = 16, 64
G = H // 2
E, F, R = 8, 512, 4
FT = F // P
CAP = B * S // E
SCALE = 1.0 / math.sqrt(DH)
DMA = 16
CH = 512
MAGIC = 12582912.0
TWO_PI_1 = 6.28125
TWO_PI_2 = 0.00193500518798828125
TWO_PI_3 = 2.0 * math.pi - TWO_PI_1 - TWO_PI_2
TAB = 2 * S - P
FLEN = 2 * S


class Shared:
    pass


class Chain:

    def __init__(self, eng, sem):
        self.eng, self.sem, self.count = eng, sem, 0

    def link(self, ins):
        self.count += 1
        ins.then_inc(self.sem, 1)
        self.eng.wait_ge(self.sem, self.count)


def last_axis(ap, n):
    return ap.unsqueeze(2).to_broadcast([ap.shape[0], ap.shape[1], n])


def mid_axis(ap, n):
    return ap.unsqueeze(1).to_broadcast([ap.shape[0], n, ap.shape[1]])


def norm_batch(v, ch, src, dst, tmp, st, b, eps, sem_var, sem_rstd, nth):
    n = slice(b * BT, b * BT + BT)
    ch.link(v.tensor_reduce(st[:, 0, n], src[:, n, :], AX_X, ALU.add))
    ch.link(v.tensor_scalar(st[:, 1, n], st[:, 0, n], 1.0 / D, None, ALU.mult))
    ch.link(v.tensor_tensor(dst[:, n, :], src[:, n, :], last_axis(st[:, 1, n], D), ALU.subtract))
    ch.link(v.tensor_tensor(tmp[:, n, :], dst[:, n, :], dst[:, n, :], ALU.mult))
    ch.link(v.tensor_reduce(st[:, 2, n], tmp[:, n, :], AX_X, ALU.add))
    v.tensor_scalar(st[:, 3, n], st[:, 2, n], 1.0 / D, eps, ALU.mult, ALU.add).then_inc(sem_var, 1)
    v.wait_ge(sem_rstd, nth)
    ch.link(v.tensor_tensor(dst[:, n, :], dst[:, n, :], last_axis(st[:, 4, n], D), ALU.mult))


def prepare(nc, K, io, sb, ps, sem):
    x_in = [sem(f"x_in{b}") for b in range(B)]
    par_in, wg_in, zero_ready, zero_out = sem("par_in"), sem("wg_in"), sem("zero_ready"), sem("zero_out")
    var_ready, rstd_ready, half_ready = sem("var_ready"), sem("rstd_ready"), sem("half_ready")
    xn_ready, a_ready, tr_ready, tr_out = sem("xn_ready"), sem("a_ready"), sem("tr_ready"), sem("tr_out")
    ident_ready, logit_ready, max_sub, exp_ready = sem("ident_ready"), sem("logit_ready"), sem("max_sub"), sem("exp_ready")
    hot_ready, pos_ready, tri_ready, iota_ready = sem("hot_ready"), sem("pos_ready"), sem("tri_ready"), sem("iota_ready")
    dve_own, pool_own = sem("prep_dve"), sem("prep_pool")

    st = sb("ln_stats", [P, 5, NT])
    neg_half = sb("neg_half", [P, NT])
    gbc, bbc = sb("attn_nw_rows", [P, D]), sb("attn_nb_rows", [P, D])
    wgc = sb("wgc", [P, E + 2])
    tri, ones = sb("tri", [P, P]), sb("ones_sq", [P, P])
    lg = sb("logits0", [P, NT, E + 2])
    big = sb("ln_tmp", [P, NT, D])
    r1, r2 = sb("route1", [P, NT, E]), sb("route2", [P, NT, E])
    hot = sb("onehot", [P, NT, E])
    io8 = sb("iota8", [P, NT, E])
    col = sb("route_cols", [P, 12, NT])
    one_row = sb("one_row", [P, NT])
    tp = [ps(f"prep_t{i}", [P, 2 * CH]) for i in range(2)]
    lps, pre, tot = ps("logit_ps", [P, NT, E + 2]), ps("prefix_ps", [P, NT, E]), ps("total_ps", [P, NT, E])
    X, XN, A = K.X, K.XN, K.A

    with nc.Block() as block:

        @block.sync
        def _(sp):
            for b in range(B):
                sp.dma_start(X[:, b * BT:b * BT + BT, :],
                             io["x"][b].rearrange("(t p) d -> p t d", p=P)).then_inc(x_in[b], DMA)
            sp.dma_start(gbc[:], io["attn_nw"].partition_broadcast(P)).then_inc(par_in, DMA)
            sp.dma_start(bbc[:], io["attn_nb"].partition_broadcast(P)).then_inc(par_in, DMA)
            sp.dma_start(wgc[:, 0:E], io["wg"]).then_inc(wg_in, DMA)
            sp.dma_start(wgc[:, E:E + 2], io["res_coef"]).then_inc(wg_in, DMA)
            sp.wait_ge(zero_ready, 1)
            sp.dma_start(K.disp.rearrange("(p t) d -> p (t d)", p=P), K.Z[:]).then_inc(zero_out, DMA)
            sp.wait_ge(zero_out, DMA)

        @block.gpsimd
        def _(g):
            g.memset(K.ident[:], 0.0).then_inc(pool_own, 1)
            g.memset(neg_half[:], -0.5).then_inc(half_ready, 1)
            g.wait_ge(pool_own, 1)
            g.affine_select(out=K.ident[:], in_=K.ident[:], compare_op=ALU.not_equal, fill=1.0, base=0,
                            pattern=[[-1, P]], channel_multiplier=1).then_inc(ident_ready, 1)
            g.memset(K.Z[:], 0.0).then_inc(zero_ready, 1)
            g.memset(ones[:], 1.0).then_inc(pool_own, 1)
            g.wait_ge(pool_own, 2)
            g.affine_select(out=tri[:], in_=ones[:], compare_op=ALU.is_gt, fill=0.0, base=0,
                            pattern=[[1, P]], channel_multiplier=-1).then_inc(tri_ready, 1)
            g.memset(one_row[:], 1.0).then_inc(tri_ready, 1)
            g.iota(io8[:], pattern=[[0, NT], [1, E]], base=0, channel_multiplier=0,
                   allow_small_or_imprecise_dtypes=True).then_inc(iota_ready, 1)
            g.wait_ge(half_ready, 1)
            for n in range(2 * B):
                b = n // 2
                g.wait_ge(var_ready, n + 1)
                g.tensor_tensor(st[:, 4, b * BT:b * BT + BT], st[:, 3, b * BT:b * BT + BT],
                                neg_half[:, b * BT:b * BT + BT], ALU.pow).then_inc(rstd_ready, 1)

        @block.vector
        def _(v):
            ch = Chain(v, dve_own)
            for b in range(B):
                n = slice(b * BT, b * BT + BT)
                v.wait_ge(x_in[b], DMA)
                norm_batch(v, ch, X, XN, big, st, b, 1e-5, var_ready, rstd_ready, 2 * b + 1)
                v.nop().then_inc(xn_ready, 1)
                norm_batch(v, ch, XN, A, big, st, b, 1e-12, var_ready, rstd_ready, 2 * b + 2)
                if b == 0:
                    v.wait_ge(par_in, 2 * DMA)
                ch.link(v.tensor_tensor(big[:, n, :], A[:, n, :], mid_axis(gbc[:], BT), ALU.mult))
                ch.link(v.tensor_tensor(A[:, n, :], big[:, n, :], mid_axis(bbc[:], BT), ALU.add))
                v.nop().then_inc(a_ready, 1)
            v.wait_ge(logit_ready, 1)
            ch.link(v.tensor_copy(lg[:], lps[:]))
            ch.link(v.tensor_reduce(col[:, 0, :], lg[:, :, 0:E], AX_X, ALU.max))
            ch.link(v.tensor_reduce(col[:, 1, :], lg[:, :, E:E + 2], AX_X, ALU.max))
            ch.link(v.tensor_tensor(lg[:, :, 0:E], lg[:, :, 0:E], last_axis(col[:, 0, :], E), ALU.subtract))
            v.tensor_tensor(lg[:, :, E:E + 2], lg[:, :, E:E + 2], last_axis(col[:, 1, :], 2),
                            ALU.subtract).then_inc(max_sub, 1)
            v.wait_ge(exp_ready, 1)
            ch.link(v.tensor_reduce(col[:, 2, :], lg[:, :, 0:E], AX_X, ALU.add))
            ch.link(v.reciprocal(col[:, 3, :], col[:, 2, :]))
            ch.link(v.tensor_reduce(col[:, 4, :], lg[:, :, E:E + 2], AX_X, ALU.add))
            ch.link(v.reciprocal(col[:, 5, :], col[:, 4, :]))
            ch.link(v.tensor_tensor(K.coef_res[:], lg[:, :, E], col[:, 5, :], ALU.mult))
            ch.link(v.tensor_tensor(col[:, 6, :], lg[:, :, E + 1], col[:, 5, :], ALU.mult))
            v.wait_ge(iota_ready, 1)
            ch.link(v.tensor_scalar(r1[:], lg[:, :, 0:E], 1.0, float(E), ALU.is_lt, ALU.mult))
            ch.link(v.tensor_tensor(r1[:], r1[:], io8[:], ALU.add))
            ch.link(v.tensor_reduce(col[:, 7, :], r1[:], AX_X, ALU.min))
            v.tensor_tensor(hot[:], io8[:], last_axis(col[:, 7, :], E), ALU.is_equal).then_inc(hot_ready, 1)
            v.wait_ge(pos_ready, 1)
            ch.link(v.tensor_copy(r2[:], tot[:]))
            v.wait_ge(tri_ready, 2)
            for e in range(E):
                ins = v.tensor_tensor_scan(r1[:, :, e], one_row[:], r2[:, :, e], 0.0, ALU.mult, ALU.add)
            ch.link(ins)
            ch.link(v.tensor_tensor(r1[:], r1[:], r2[:], ALU.subtract))
            ch.link(v.tensor_tensor(r1[:], pre[:], r1[:], ALU.add))
            ch.link(v.tensor_tensor(r1[:], r1[:], hot[:], ALU.mult))
            ch.link(v.tensor_reduce(col[:, 8, :], r1[:], AX_X, ALU.add))
            ch.link(v.tensor_scalar(col[:, 9, :], col[:, 8, :], float(CAP), None, ALU.is_lt))
            ch.link(v.tensor_tensor(K.coef_moe[:], col[:, 6, :], col[:, 3, :], ALU.mult))
            ch.link(v.tensor_tensor(K.coef_moe[:], K.coef_moe[:], col[:, 9, :], ALU.mult))
            ch.link(v.scalar_tensor_tensor(out=col[:, 10, :], in0=col[:, 7, :], scalar=float(CAP),
                                           in1=col[:, 8, :], op0=ALU.mult, op1=ALU.add))
            ch.link(v.tensor_tensor(col[:, 10, :], col[:, 10, :], col[:, 9, :], ALU.mult))
            ch.link(v.tensor_copy(K.gather_idx[:], col[:, 10, :]))
            ch.link(v.tensor_scalar(col[:, 11, :], col[:, 9, :], -float(2 * E * CAP), float(2 * E * CAP),
                                    ALU.mult, ALU.add))
            ch.link(v.tensor_tensor(col[:, 11, :], col[:, 11, :], col[:, 10, :], ALU.add))
            ch.link(v.tensor_copy(K.scatter_idx[:], col[:, 11, :]))

        @block.tensor
        def _(pe):
            pe.wait_ge(ident_ready, 1)
            for n in range(2 * B):
                b, src = n // 2, (XN, A)[n % 2]
                pe.wait_ge((xn_ready, a_ready)[n % 2], b + 1)
                if n >= 2:
                    pe.wait_ge(tr_out, n - 1)
                for t in range(BT):
                    mm = pe.transpose(tp[n % 2][:, t * P:t * P + P], src[:, b * BT + t, :], K.ident[:])
                mm.then_inc(tr_ready, 1)
            pe.wait_ge(wg_in, 2 * DMA)
            pe.wait_ge(tr_out, 2 * B)
            for t in range(NT):
                mm = pe.matmul(lps[:, t, :], K.AT[:, t * P:t * P + P], wgc[:], start=True, stop=True)
            mm.then_inc(logit_ready, 1)
            pe.wait_ge(hot_ready, 1)
            pe.wait_ge(tri_ready, 1)
            pe.matmul(pre[:], tri[:], hot[:], start=True, stop=True)
            pe.matmul(tot[:], ones[:], hot[:], start=True, stop=True).then_inc(pos_ready, 1)

        @block.scalar
        def _(act):
            for n in range(2 * B):
                b, dst = n // 2, (K.XNT, K.AT)[n % 2]
                act.wait_ge(tr_ready, n + 1)
                act.copy(dst[:, b * S:b * S + S], tp[n % 2][:]).then_inc(tr_out, 1)
            act.wait_ge(max_sub, 1)
            act.activation(lg[:], lg[:], ACT.Exp).then_inc(exp_ready, 1)


def experts(nc, K, io, sb, ps, sem):
    res_in, w_in = sem("res_in"), [sem("w_in0"), sem("w_in1")]
    bias_in, scat, d_in = sem("bias_in"), sem("scattered"), [sem("d_in0"), sem("d_in1")]
    dt_ready, dt_out = sem("dt_ready"), sem("dt_out")
    h_ready, h_out, o_ready, o_out = sem("h_ready"), sem("h_out"), sem("o_ready"), sem("o_out")
    e_wr = [sem("e_wr0"), sem("e_wr1")]
    gath, mix_ready, g0_ready, own = sem("gathered"), sem("mix_ready"), sem("g0_ready"), sem("exp_dve")

    w1 = [sb(f"w1_{i}", [P, F]) for i in range(2)]
    w2 = [sb(f"w2_{i}", [P, FT, D]) for i in range(2)]
    w1r, w2r = sb("w1_res", [P, F]), sb("w2_res", [P, FT, D])
    b1, b1r = sb("b1_cols", [P, E, FT]), sb("b1_res_cols", [P, FT])
    b2, b2r = sb("b2_rows", [P, E * D]), sb("b2_res_rows", [P, D])
    dx = [sb(f"dispatched{i}", [P, CAP // P, D]) for i in range(2)]
    dT = [sb(f"dispatched_t{i}", [P, CAP]) for i in range(2)]
    hT = [sb(f"hidden_t{i}", [P, FT, CAP]) for i in range(2)]
    eo = [sb(f"expert_out{i}", [P, CAP // P, D]) for i in range(2)]
    RES, MOE = K.RES, K.MOE
    hp = [ps(f"hid_ps{i}", [P, CH]) for i in range(4)]
    op = [ps(f"out_ps{i}", [P, CAP // P, D]) for i in range(2)]
    tp = [ps(f"dt_ps{i}", [P, CH]) for i in range(2)]
    CT = CAP // P

    with nc.Block() as block:

        @block.sync
        def _(sp):
            sp.dma_start(w1r[:], io["res_inter_w"]).then_inc(res_in, DMA)
            sp.dma_start(w2r[:], io["res_output_w"].rearrange("(i p) d -> p i d", p=P)).then_inc(res_in, DMA)
            sp.dma_start(b1r[:], io["res_inter_b"]).then_inc(bias_in, DMA)
            sp.dma_start(b2r[:], io["res_output_b"].partition_broadcast(P)).then_inc(bias_in, DMA)
            sp.dma_start(b1[:], io["inter_b"]).then_inc(bias_in, DMA)
            sp.dma_start(b2[:], io["output_b"].rearrange("e d -> (e d)").partition_broadcast(P)).then_inc(bias_in, DMA)

            def load(e, s):
                sp.dma_start(w1[s][:], io["inter_w"][e]).then_inc(w_in[s], DMA)
                sp.dma_start(w2[s][:], io["output_w"][e].rearrange("(i p) d -> p i d", p=P)).then_inc(w_in[s], DMA)
                sp.dma_start(dx[s][:], K.disp[bass.ts(e, CAP), :].rearrange("(c p) d -> p c d", p=P)).then_inc(d_in[s], DMA)

            sp.wait_ge(scat, DMA * NT)
            load(0, 0)
            load(1, 1)
            for e in range(E):
                s = e % 2
                sp.wait_ge(o_out, NT // CT + e + 1)
                sp.dma_start(K.eout[bass.ts(e, CAP), :].rearrange("(c p) d -> p c d", p=P), eo[s][:]).then_inc(e_wr[s], DMA)
                if e + 2 < E:
                    load(e + 2, s)
            for s in range(2):
                sp.wait_ge(e_wr[s], DMA * E // 2)

        @block.gpsimd
        def _(g):
            for t in range(NT):
                g.indirect_dma_start(out=K.disp, out_offset=bass.IndirectOffsetOnAxis(K.scatter_idx[:, t:t + 1], 0),
                                     in_=K.A[:, t, :], in_offset=None, bounds_check=E * CAP - 1,
                                     oob_is_err=False).then_inc(scat, DMA)
            for s in range(2):
                g.wait_ge(e_wr[s], DMA * E // 2)
            for t in range(NT):
                g.indirect_dma_start(out=MOE[:, t, :], out_offset=None, in_=K.eout,
                                     in_offset=bass.IndirectOffsetOnAxis(K.gather_idx[:, t:t + 1], 0),
                                     bounds_check=E * CAP - 1, oob_is_err=False).then_inc(gath, DMA)

        NR = NT // CT
        JOBS = NR + E

        @block.tensor
        def _(pe):
            pe.wait_ge(res_in, 2 * DMA)

            def hidden(j):
                e, s = j - NR, j % 2
                if e >= 0:
                    pe.wait_ge(w_in[s], 2 * DMA * (e // 2 + 1))
                    pe.wait_ge(dt_out, e + 1)
                for i in range(FT):
                    if j >= 1:
                        pe.wait_ge(h_out, FT * (j - 1) + i + 1)
                    w = w1r if e < 0 else w1[s]
                    rhs = K.AT[:, j * CAP:j * CAP + CAP] if e < 0 else dT[s][:]
                    pe.matmul(hp[i][:], w[:, i * P:i * P + P], rhs, start=True, stop=True).then_inc(h_ready, 1)

            def out(j):
                e, s = j - NR, j % 2
                w = w2r if e < 0 else w2[s]
                if j >= 2:
                    pe.wait_ge(o_out, j - 1)
                for i in range(FT):
                    pe.wait_ge(h_out, FT * j + i + 1)
                    for c in range(CT):
                        mm = pe.matmul(op[s][:, c, :], hT[s][:, i, c * P:c * P + P], w[:, i, :],
                                       start=(i == 0 and c == 0), stop=(i == FT - 1), skip_group_check=True)
                mm.then_inc(o_ready, 1)

            def turn(e):
                s = e % 2
                pe.wait_ge(d_in[s], DMA * (e // 2 + 1))
                if e >= 2:
                    pe.wait_ge(dt_out, e - 1)
                for c in range(CT):
                    mm = pe.transpose(tp[s][:, c * P:c * P + P], dx[s][:, c, :], K.ident[:])
                mm.then_inc(dt_ready, 1)

            hidden(0)
            for j in range(JOBS):
                if NR <= j + 1 < JOBS:
                    turn(j + 1 - NR)
                if j + 1 < JOBS:
                    hidden(j + 1)
                out(j)

        @block.scalar
        def _(act):
            act.wait_ge(bias_in, 4 * DMA)
            for j in range(JOBS):
                e, s = j - NR, j % 2
                for i in range(FT):
                    act.wait_ge(h_ready, FT * j + i + 1)
                    if j >= 2 and i == 0:
                        act.wait_ge(o_ready, j - 1)
                    bias = b1r[:, i:i + 1] if e < 0 else b1[:, e, i:i + 1]
                    act.activation(hT[s][:, i, :], hp[i][:], ACT.Gelu_apprx_tanh, bias=bias).then_inc(h_out, 1)
            act.wait_ge(mix_ready, 1)
            act.activation(K.G0[:], K.G0[:], ACT.Silu).then_inc(g0_ready, 1)

        @block.vector
        def _(v):
            ch = Chain(v, own)
            v.wait_ge(bias_in, 4 * DMA)
            for j in range(JOBS):
                e, s = j - NR, j % 2
                if NR <= j + 1 < JOBS:
                    v.wait_ge(dt_ready, j + 2 - NR)
                    if j + 1 - NR >= 2:
                        v.wait_ge(h_ready, FT * (j - 1) + FT)
                    v.tensor_copy(dT[(j + 1) % 2][:], tp[(j + 1) % 2][:]).then_inc(dt_out, 1)
                v.wait_ge(o_ready, j + 1)
                if e < 0:
                    v.tensor_tensor(RES[:, j * CT:j * CT + CT, :], op[s][:], mid_axis(b2r[:], CT),
                                    ALU.add).then_inc(o_out, 1)
                else:
                    if e >= 2:
                        v.wait_ge(e_wr[s], DMA * (e // 2))
                    v.tensor_tensor(eo[s][:], op[s][:], mid_axis(b2[:, e * D:e * D + D], CT),
                                    ALU.add).then_inc(o_out, 1)
            v.wait_ge(o_out, JOBS)
            v.wait_ge(gath, DMA * NT)
            ch.link(v.tensor_tensor(RES[:], RES[:], last_axis(K.coef_res[:], D), ALU.mult))
            ch.link(v.tensor_tensor(K.G0[:], RES[:], K.XN[:], ALU.add))
            ch.link(v.tensor_tensor(MOE[:], MOE[:], last_axis(K.coef_moe[:], D), ALU.mult))
            v.tensor_tensor(K.G0[:], K.G0[:], MOE[:], ALU.add).then_inc(mix_ready, 1)
            v.wait_ge(g0_ready, 1)


def project(nc, K, io, sb, ps, sem):
    fr_in, bp_in, wv_in = sem("fr_in"), sem("bp_in"), sem("wv_in")
    pos_i, sin_arg, sin_out, tab_neg = sem("pos_i"), sem("sin_arg"), sem("sin_out"), sem("tab_neg")
    ln_arg, ln_out, f_ready, f_wr = sem("ln_arg"), sem("ln_out"), sem("f_ready"), sem("f_wr")
    v_ready, vhi, vlo, v_wr = sem("v_ready"), sem("vhi"), sem("vlo"), [sem("v_wr0"), sem("v_wr1")]
    wqk_in = [sem("wqk_in0"), sem("wqk_in1")]
    qk_ready, qk_read, pair, summed = sem("qk_ready"), sem("qk_read"), sem("pair"), sem("summed")
    hi_ready, lo_ready, qk_wr = sem("hi_ready"), sem("lo_ready"), [sem("qk_wr0"), sem("qk_wr1")]
    own = sem("proj_dve")

    freq = sb("freq", [P, 1])
    pos = sb("pos", [P, S])
    posi = sb("pos_int", [P, S], I32)
    ang, tn = sb("ang", [P, S]), sb("turns", [P, S])
    COS, SIN = sb("cos_table", [P, S]), sb("sin_table", [P, S])
    half_pi, one_col = sb("half_pi", [P, 1]), sb("one_col", [P, 1])
    disti, dist = sb("dist_int", [H, FLEN], I32), sb("dist", [H, FLEN])
    bp, ba = sb("bias_p", [H, 1]), sb("bias_a", [H, 1])
    wv = sb("wv", [P, H * DH])
    vt = [sb(f"v_parts{i}", [P, H, 2, DH], BF16) for i in range(2)]
    wqk = [sb(f"wqk{i}", [P, 4, P]) for i in range(2)]
    t1 = [sb(f"rope1_{i}", [P, 2, CH]) for i in range(2)]
    t2 = [sb(f"rope2_{i}", [P, 2, CH]) for i in range(2)]
    parts = [sb(f"qk_parts{i}", [P, 4, CH], BF16) for i in range(2)]
    pp = [ps(f"proj_ps{i}", [P, 4, CH]) for i in range(2)]
    NC = S // CH
    XNT = K.XNT

    def jobs():
        for b in range(B):
            for c in range(NC):
                yield b * NC + c, b, c

    NJ = B * NC

    def tiles(ap):
        return ap.rearrange("p (t j) -> p t j", j=P)

    def rotated(s, i):
        ap = tiles(t1[s][:, i, :])
        return ap[:, :, ::-1] if i == 0 else ap

    def lo_part(v, gi, j):
        s = j % 2
        v.wait_ge(hi_ready, gi * (2 * NJ) + 2 * (j + 1))
        for i, scale in enumerate((SCALE, 1.0)):
            ins = v.scalar_tensor_tensor(out=tiles(parts[s][:, 2 * i + 1, :]), in0=rotated(s, i), scalar=scale,
                                         in1=tiles(parts[s][:, 2 * i, :]), op0=ALU.mult, op1=ALU.subtract)
        ins.then_inc(lo_ready, 1)

    def write(act, gi, j):
        b, c, s = j // NC, j % NC, j % 2
        act.wait_ge(lo_ready, gi * NJ + (j + 2))
        act.dma_start(K.qkscr[bass.ds(gi + b * G, 1), :, :, c * CH:c * CH + CH].rearrange("o p k c -> (o p) k c"),
                      parts[s][:]).then_inc(qk_wr[s], DMA)

    with nc.Block() as block:

        @block.sync
        def _(sp):
            for i in range(P // (DH // 2)):
                sp.dma_start(freq[32 * i:32 * i + 32, :], io["freqs"].rearrange("(p o) -> p o", o=1)).then_inc(fr_in, DMA)
            sp.dma_start(bp[:], io["bias_p"]).then_inc(bp_in, DMA)
            sp.dma_start(ba[:], io["bias_a"]).then_inc(bp_in, DMA)
            sp.dma_start(wv[:], io["wv"]).then_inc(wv_in, DMA)
            for r in range(2):
                sp.dma_start(wqk[r][:], io["wqk"][r]).then_inc(wqk_in[r], DMA)
            sp.wait_ge(f_ready, 1)
            sp.dma_start(K.fscr, dist[:]).then_inc(f_wr, DMA)
            for t in range(NT):
                sp.wait_ge(vhi, 2 * t + 2)
                sp.wait_ge(vlo, 2 * t + 2)
                b = t // BT
                sp.dma_start(K.vscr[b * H:b * H + H, :, t % BT, :].rearrange("h p c -> p h c"),
                             vt[t % 2][:].rearrange("p h a d -> p h (a d)")).then_inc(v_wr[t % 2], DMA)
            for s in range(2):
                sp.wait_ge(v_wr[s], DMA * NT // 2)
            sp.wait_ge(f_wr, DMA)
            with sp.Fori(0, G // 2 - 1) as gh:
                for r in range(2):
                    sp.wait_ge(qk_ready, gh * (2 * NJ) + (r + 1) * NJ)
                    sp.dma_start(wqk[r][:], io["wqk"][bass.ds(gh * 2 + (r + 2), 1)].rearrange("o p k m -> (o p) k m")).then_inc(wqk_in[r], DMA)

        @block.gpsimd
        def _(g):
            g.iota(posi[:], pattern=[[1, S]], base=0, channel_multiplier=0).then_inc(pos_i, 1)
            g.iota(disti[:], pattern=[[1, FLEN]], base=-(S - 1), channel_multiplier=0).then_inc(pos_i, 1)
            g.memset(half_pi[:], math.pi / 2).then_inc(pos_i, 1)
            g.memset(one_col[:], 1.0).then_inc(pos_i, 1)
            with g.Fori(0, G) as gi:
                for j, b, c in jobs():
                    s = j % 2
                    g.wait_ge(pair, gi * NJ + (j + 3))
                    g.tensor_tensor(t1[s][:], t1[s][:], t2[s][:], ALU.add).then_inc(summed, 1)

        @block.vector
        def _(v):
            ch = Chain(v, own)
            v.wait_ge(pos_i, 4)
            v.wait_ge(fr_in, 4 * DMA)
            ch.link(v.tensor_copy(pos[:], posi[:]))
            ch.link(v.tensor_scalar(ang[:], pos[:], freq[:, 0:1], None, ALU.mult))
            ch.link(v.tensor_scalar(tn[:], ang[:], 1.0 / (2.0 * math.pi), MAGIC, ALU.mult, ALU.add))
            ch.link(v.tensor_scalar(tn[:], tn[:], MAGIC, None, ALU.subtract))
            for part in (TWO_PI_1, TWO_PI_2, TWO_PI_3):
                ch.link(v.scalar_tensor_tensor(out=ang[:], in0=tn[:], scalar=-part, in1=ang[:],
                                               op0=ALU.mult, op1=ALU.add))
            ch.link(v.tensor_scalar(ang[:], ang[:], 3.1415925, -3.1415925, ALU.min, ALU.max))
            v.scalar_tensor_tensor(out=tn[:], in0=ang[:], scalar=-1.0, in1=ang[:], op0=ALU.mult, op1=ALU.max).then_inc(sin_arg, 1)
            v.wait_ge(bp_in, 2 * DMA)
            ch.link(v.tensor_copy(dist[:], disti[:]))
            ch.link(v.scalar_tensor_tensor(out=dist[:], in0=dist[:], scalar=-1.0, in1=dist[:], op0=ALU.mult, op1=ALU.max))
            ch.link(v.tensor_scalar(ba[:], ba[:], 0.01, None, ALU.max))
            v.tensor_scalar(bp[:], bp[:], 0.01, -1.0, ALU.max, ALU.mult).then_inc(ln_arg, 1)
            v.wait_ge(ln_out, 1)
            v.wait_ge(ln_arg, 1)
            v.tensor_scalar(dist[:], dist[:], bp[:, 0:1], None, ALU.mult).then_inc(f_ready, 1)
            v.wait_ge(sin_out, 2)
            for h in range(2):
                v.tensor_scalar(SIN[h * DH:h * DH + DH // 2, :], SIN[h * DH:h * DH + DH // 2, :], -1.0, None,
                                ALU.mult).then_inc(tab_neg, 1)
            for t in range(NT):
                for c in range(2):
                    n = 2 * t + c
                    v.wait_ge(vhi, n + 1)
                    hs = slice(c * H // 2, c * H // 2 + H // 2)
                    v.tensor_tensor(vt[t % 2][:, hs, 1, :],
                                    pp[n // 4 % 2][:, n % 4, :].rearrange("p (h d) -> p h d", d=DH),
                                    vt[t % 2][:, hs, 0, :], ALU.subtract).then_inc(vlo, 1)
            v.wait_ge(vlo, 2 * NT)
            v.wait_ge(tab_neg, 2)
            for _ in range(2):
                v.nop().then_inc(pair, 1)
            v.nop().then_inc(lo_ready, 1)
            with v.Fori(0, G) as gi:
                for j, b, c in jobs():
                    s = j % 2
                    v.wait_ge(qk_ready, gi * NJ + (j + 1))
                    v.wait_ge(lo_ready, gi * NJ + max(j, 1))
                    cs = slice(c * CH, c * CH + CH)
                    q4 = pp[s][:].rearrange("p (k w) c -> p k w c", w=2)
                    v.tensor_tensor(t1[s][:], q4[:, :, 0, :], mid_axis(COS[:, cs], 2), ALU.mult)
                    v.tensor_tensor(t2[s][:], q4[:, :, 1, :], mid_axis(SIN[:, cs], 2), ALU.mult).then_inc(pair, 1)
                    if j >= 1:
                        lo_part(v, gi, j - 1)
                lo_part(v, gi, NJ - 1)

        @block.scalar
        def _(act):
            act.wait_ge(sin_arg, 1)
            act.activation(SIN[:], ang[:], ACT.Sin).then_inc(sin_out, 1)
            act.activation(COS[:], tn[:], ACT.Sin, bias=half_pi[:, 0:1], scale=-1.0).then_inc(sin_out, 1)
            act.wait_ge(ln_arg, 1)
            act.activation(dist[:], dist[:], ACT.Ln, bias=one_col[0:H, 0:1], scale=ba[:, 0:1]).then_inc(ln_out, 1)
            for t in range(NT):
                if t >= 2:
                    act.wait_ge(v_wr[t % 2], DMA * (t // 2))
                for c in range(2):
                    n = 2 * t + c
                    act.wait_ge(v_ready, n + 1)
                    act.copy(vt[t % 2][:, c * H // 2:c * H // 2 + H // 2, 0, :],
                             pp[n // 4 % 2][:, n % 4, :].rearrange("p (h d) -> p h d", d=DH)).then_inc(vhi, 1)
            with act.Fori(0, G) as gi:
                for j, b, c in jobs():
                    s = j % 2
                    act.wait_ge(summed, gi * NJ + (j + 1))
                    if j >= 2:
                        act.wait_ge(qk_wr[s], gi * (DMA * NJ // 2) + DMA * (j // 2))
                    act.activation(tiles(parts[s][:, 0, :]), rotated(s, 0), ACT.Copy, scale=SCALE).then_inc(hi_ready, 1)
                    act.activation(parts[s][:, 2, :], t1[s][:, 1, :], ACT.Copy).then_inc(hi_ready, 1)
                    if j >= 1:
                        write(act, gi, j - 1)
                write(act, gi, NJ - 1)
                for s in range(2):
                    act.wait_ge(qk_wr[s], gi * (DMA * NJ // 2) + DMA * NJ // 2)

        @block.tensor
        def _(pe):
            pe.wait_ge(wv_in, DMA)
            for t in range(NT):
                for c in range(2):
                    n = 2 * t + c
                    if n >= 8:
                        pe.wait_ge(vlo, n - 7)
                    pe.matmul(pp[n // 4 % 2][:, n % 4, :], XNT[:, t * P:t * P + P], wv[:, c * CH:c * CH + CH],
                              start=True, stop=True).then_inc(v_ready, 1)
            with pe.Fori(0, G // 2) as gh:
                for r in range(2):
                    pe.wait_ge(wqk_in[r], gh * DMA + DMA)
                    for j, b, c in jobs():
                        s = j % 2
                        pe.wait_ge(pair, gh * (2 * NJ) + (r * NJ + j + 1))
                        for i in range(4):
                            mm = pe.matmul(pp[s][:, i, :], wqk[r][:, i, :],
                                           XNT[:, b * S + c * CH:b * S + c * CH + CH], start=True, stop=True)
                        mm.then_inc(qk_ready, 1)


def attend(nc, K, io, sb, ps, sem):
    qk_in, kl_in, tab_in, v_in, wo_in = [[sem(f"{n}_in{s}") for s in range(2)] for n in ("aq", "ak", "at", "av", "aw")]
    s_ready, biased, exped = sem("s_ready"), sem("biased"), sem("exped")
    turned, turn_out, lo_ready = sem("turned"), sem("turn_out"), sem("p_lo_ready")
    pv_ready, ot_ready, op_ready, added, zeroed = sem("pv_ready"), sem("ot_ready"), sem("op_ready"), sem("added"), sem("acc_zeroed")
    recip = sem("recip")

    QS = [sb(f"q_hi_lo{s}", [P, S], BF16) for s in range(2)]
    KS = [sb(f"k_hi_hi{s}", [P, S], BF16) for s in range(2)]
    KL = [sb(f"k_lo{s}", [DH, S], BF16) for s in range(2)]
    VV = [sb(f"v_hi_lo{s}", [P, BT, 2 * DH], BF16) for s in range(2)]
    TB = [sb(f"bias_tab{s}", [P, TAB]) for s in range(2)]
    WO = [sb(f"wo{s}", [P, P]) for s in range(2)]
    SB = [sb(f"scores{i}", [P, S]) for i in range(2)]
    PR = [sb(f"probs{i}", [P, S]) for i in range(2)]
    PT = sb("probs_t", [P, 8, BT, P])
    LO = sb("probs_t_lo", [P, 8, BT, P], BF16)
    OT = [sb(f"out_t{i}", [P, CH]) for i in range(2)]
    neg_max, row_sum = sb("neg_max", [P, 16]), sb("row_sum", [P, 16])
    inv = sb("inv_sum", [P, 16])
    gate = sb("wait_holder", [P, 2])
    sp_ = [ps(f"score_ps{i}", [P, S]) for i in range(2)]
    tp = [ps(f"turn_ps{i}", [P, 4, P]) for i in range(2)]
    ov, oo = ps("pv_ps", [P, CH]), ps("proj_out_ps", [P, 4, P])
    PTB = PT[:].bitcast(BF16)

    NI = B * G
    U = 2 * BT
    LS, LE, LT, LP = 9, 8, 7, 2

    def run(eng, step):
        for u in range(-LS, 0):
            step(0, u, lambda x: 0 <= x < U)
        with eng.Fori(0, NI - 1) as it:
            for u in range(U):
                step(it, u, lambda x: True)
        for u in range(U):
            step(NI - 1, u, lambda x: x < U)

    def at(it, n, add):
        return it * n + add

    with nc.Block() as block:

        @block.sync
        def _(sp):
            def load(ix, s):
                q = K.qkscr[bass.ds(ix, 1)].rearrange("o p k c -> (o p) k c")
                rows = slice(s * DH, s * DH + DH)
                sp.dma_start(QS[s][0:DH, :], q[rows, 0, :]).then_inc(qk_in[s], DMA)
                sp.dma_start(QS[s][DH:P, :], q[rows, 1, :]).then_inc(qk_in[s], DMA)
                sp.dma_start(KS[s][0:DH, :], q[rows, 2, :]).then_inc(qk_in[s], DMA)
                sp.dma_start(KS[s][DH:P, :], q[rows, 2, :]).then_inc(qk_in[s], DMA)
                sp.dma_start(KL[s][:], q[rows, 3, :]).then_inc(kl_in[s], DMA)
                tab = bass.AP(tensor=K.fscr.tensor, offset=((ix % G) * 2 + s) * FLEN, ap=[[1, P], [1, TAB]])
                sp.dma_start(TB[s][:], tab).then_inc(tab_in[s], DMA)

            def load_v(ix, s):
                sp.dma_start(VV[s][:], K.vscr[bass.ds(ix * 2 + s, 1)].rearrange("o p t c -> (o p) t c")).then_inc(v_in[s], DMA)
                sp.dma_start(WO[s][:], io["wo2"][bass.ds((ix % G) * 2 + s, 1)].rearrange("o p m -> (o p) m")).then_inc(wo_in[s], DMA)

            for s in range(2):
                load(0, s)
                load_v(0, s)
            with sp.Fori(0, NI - 1) as it:
                for s in range(2):
                    sp.wait_ge(s_ready, at(it, U, BT * (s + 1)))
                    sp.wait_ge(biased, at(it, U, BT * (s + 1)))
                    load(it + 1, s)
                    sp.wait_ge(op_ready, at(it, 4, 2 * (s + 1)))
                    load_v(it + 1, s)

        @block.tensor
        def _(pe):
            def scores(it, n):
                s, t, k = n // BT % 2, n % BT, n // U
                if t == 0:
                    pe.wait_ge(qk_in[s], at(it, 4 * DMA, 4 * DMA * (k + 1)))
                    pe.wait_ge(kl_in[s], at(it, DMA, DMA * (k + 1)))
                if not (isinstance(it, int) and it == 0 and n < 2):
                    pe.wait_ge(biased, at(it, U, n - 1))
                o, q = sp_[n % 2], slice(t * P, t * P + P)
                for c in range(2):
                    cs = slice(c * CH, c * CH + CH)
                    pe.matmul(o[:, cs], QS[s][:, q], KS[s][:, cs], start=True, stop=False)
                    mm = pe.matmul(o[:, cs], QS[s][0:DH, q], KL[s][:, cs], start=False, stop=True)
                mm.then_inc(s_ready, 1)

            def turn(it, n):
                pe.wait_ge(exped, at(it, U, n + 1))
                for half in range(2):
                    w = 2 * n + half
                    if not (isinstance(it, int) and it == 0 and w < 2):
                        pe.wait_ge(turn_out, at(it, 2 * U, w - 1))
                    for k in range(4):
                        mm = pe.transpose(tp[half][:, k, :], PR[n % 2][:, (4 * half + k) * P:(4 * half + k + 1) * P],
                                          K.ident[:])
                    mm.then_inc(turned, 1)

            def by_v(it, n):
                c, s = n // 4, n // BT % 2
                r0 = 4 * (c % 2)
                if n % BT == 0:
                    pe.wait_ge(v_in[s], at(it, DMA, DMA * (n // U + 1)))
                if n % 4 == 0:
                    pe.wait_ge(lo_ready, at(it, U, n + 4))
                    if not (isinstance(it, int) and it == 0 and c == 0):
                        pe.wait_ge(ot_ready, at(it, 4, c))
                for k in (2 * (n % 4), 2 * (n % 4) + 1):
                    pe.matmul(ov[:], VV[s][:, k, :], PTB[:, r0:r0 + 4, k, 1::2], start=(k == 0), stop=False)
                    mm = pe.matmul(ov[:], VV[s][:, k, :], LO[:, r0:r0 + 4, k, :], start=False, stop=(k == BT - 1))
                if n % 4 == 3:
                    mm.then_inc(pv_ready, 1)

            def out(it, c):
                s = c // 2 % 2
                if c % 2 == 0:
                    pe.wait_ge(wo_in[s], at(it, DMA, DMA))
                pe.wait_ge(ot_ready, at(it, 4, c + 1))
                pe.wait_ge(added, at(it, 16, 4 * c + 1))
                for k in range(4):
                    mm = pe.matmul(oo[:, k, :], OT[c % 2][:, k * P:k * P + P], WO[s][:], start=True, stop=True)
                mm.then_inc(op_ready, 1)

            def step(it, u, there):
                if there(u + LS):
                    scores(it, u + LS)
                if there(u + LT):
                    turn(it, u + LT)
                if there(u + LP):
                    by_v(it, u + LP)
                if there(u) and u % 4 == 3:
                    out(it, u // 4)

            run(pe, step)

        @block.vector
        def _(v):
            def bias_max(it, n):
                s, t = n // BT % 2, n % BT
                v.wait_ge(s_ready, at(it, U, n + 1))
                if t == 0:
                    v.wait_ge(tab_in[s], at(it, DMA, DMA * (n // U + 1)))
                if not (isinstance(it, int) and it == 0 and n < 2):
                    v.wait_ge(exped, at(it, U, n - 1))
                j = TAB - S - t * P
                v.memset(gate[:, n % 2:n % 2 + 1], 0.0)
                v.tensor_tensor_reduce(SB[n % 2][:], sp_[n % 2][:], TB[s][:, j:j + S], -1.0, 3.0e38,
                                       ALU.add, ALU.min, neg_max[:, n % 16:n % 16 + 1]).then_inc(biased, 1)

            def take_out(it, c):
                v.wait_ge(pv_ready, at(it, 4, c + 1))
                v.tensor_copy(OT[c % 2][:], ov[:]).then_inc(ot_ready, 1)

            def add_share(it, c):
                v.wait_ge(added, at(it, 16, 4 * c + 1))
                v.reciprocal(inv[:, 4 * c:4 * c + 4], row_sum[:, 4 * c:4 * c + 4]).then_inc(recip, 1)
                v.wait_ge(recip, at(it, 4, c + 1))
                v.wait_ge(op_ready, at(it, 4, c + 1))
                for k in range(4):
                    t = (4 * c + k) % BT
                    row = (it // G) * BT + t
                    if not isinstance(row, int):
                        acc = K.SACC[:, bass.ds(row, 1), :].rearrange("p o d -> p (o d)")
                    else:
                        acc = K.SACC[:, row, :]
                    v.scalar_tensor_tensor(out=acc, in0=oo[:, k, :], scalar=inv[:, 4 * c + k:4 * c + k + 1],
                                           in1=acc, op0=ALU.mult, op1=ALU.add).then_inc(added, 1)

            def step(it, u, there):
                if there(u) and u % 4 == 2:
                    take_out(it, u // 4)
                if there(u + LS):
                    bias_max(it, u + LS)
                if there(u) and u % 4 == 3:
                    add_share(it, u // 4)

            v.memset(K.SACC[:], 0.0).then_inc(zeroed, 1)
            v.wait_ge(zeroed, 1)
            v.nop().then_inc(added, 1)
            run(v, step)

        @block.scalar
        def _(act):
            def exp(it, n):
                act.wait_ge(biased, at(it, U, n + 1))
                if not (isinstance(it, int) and it == 0 and n < 2):
                    act.wait_ge(turned, at(it, 2 * U, 2 * (n - 1)))
                m = n % 16
                act.activation(PR[n % 2][:], SB[n % 2][:], ACT.Exp, bias=neg_max[:, m:m + 1], scale=-1.0,
                               accum_out=row_sum[:, m:m + 1]).then_inc(exped, 1)

            def untile(it, n):
                if n % 4 == 0 and not (isinstance(it, int) and it == 0 and n < 8):
                    act.wait_ge(pv_ready, at(it, 4, n // 4 - 1))
                for half in range(2):
                    act.wait_ge(turned, at(it, 2 * U, 2 * n + half + 1))
                    act.copy(PT[:, n % 8, 4 * half:4 * half + 4, :], tp[half][:]).then_inc(turn_out, 1)

            def step(it, u, there):
                if there(u + LE):
                    exp(it, u + LE)
                if there(u + LT):
                    untile(it, u + LT)

            run(act, step)

        @block.gpsimd
        def _(g):
            def low(it, n):
                r = n % 8
                g.wait_ge(turn_out, at(it, 2 * U, 2 * n + 2))
                g.tensor_tensor(LO[:, r, :, :], PT[:, r, :, :], PTB[:, r, :, 1::2], ALU.subtract).then_inc(lo_ready, 1)

            def step(it, u, there):
                if there(u + LT):
                    low(it, u + LT)

            run(g, step)


def recur(nc, K, io, sb, ps, sem):
    w_in, dec_in, base_ready = sem("rw_in"), sem("dec_in"), sem("base_ready")
    var_ready, rstd_ready, half_ready = sem("var1_ready"), sem("rstd1_ready"), sem("half1_ready")
    xn_ready, made, act_out, kv_read = sem("xn1_ready"), sem("made"), sem("act_out"), sem("kv_read")
    scanned, weighed, weighed_used, s1_ready, s1_out = (sem("scanned"), sem("weighed"), sem("weighed_used"),
                                                        sem("s1_ready"), sem("s1_out"))
    own, flip_ready, flipped, flip_read = sem("recur_dve"), sem("flip_ready"), sem("flipped"), sem("flip_read")

    st = sb("ln1_stats", [P, 5, NT])
    neg_half = sb("neg_half1", [P, NT])
    big = sb("ln1_tmp", [P, NT, D])
    wq, wk = sb("q_w", [P, P]), sb("k_w", [P, P])
    wv, wo = sb("v_w_rep", [P, 8, P]), sb("o_w_rep", [P, 8, P])
    c1w, c2w = sb("cs_w1", [P, D // 4]), sb("cs_w2_rep", [D // 4, P])
    c1b, c2b = sb("cs_b1", [D // 4, 1]), sb("cs_b2_rep", [P, 1])
    base = sb("decay_base", [P, 1])
    QT, KT = sb("q_t", [P, 2, S]), sb("k_t", [P, 2, S])
    C1, LAM = sb("cs_hidden", [D // 4, S]), sb("lam", [P, 2, S])
    KV, SC, WT = sb("kv", [P, 2, S]), sb("state", [P, 2, S]), sb("q_state", [P, 2, S])
    pj = [ps(f"made_ps{i}", [P, S]) for i in range(2)]
    so = ps("s1_ps", [P, BT, P])
    fs = ps("s0_ps", [P, BT, P])
    flip = sb("flip", [P, P])
    FE = 8
    X, XN, X1, XNT = K.X, K.XN, K.X, K.XNT

    with nc.Block() as block:

        @block.sync
        def _(sp):
            for dst, src in ((wq[:], io["q_w"]), (wk[:], io["k_w"]), (wv[:], io["v_w"]), (wo[:], io["o_w"]), (c1w[:], io["cs_w1"]),
                             (c2w[:], io["cs_w2"]), (c1b[:], io["cs_b1"]), (c2b[:], io["cs_b2"])):
                sp.dma_start(dst, src).then_inc(w_in, DMA)
            sp.dma_start(base[:], io["decay"]).then_inc(dec_in, DMA)

        @block.vector
        def _(v):
            ch = Chain(v, own)

            def join(b):
                n = slice(b * BT, b * BT + BT)
                v.wait_ge(flipped, b + 1)
                ch.link(v.tensor_tensor(big[:, n, :], fs[:], K.G0[:, n, :], ALU.mult))
                v.nop().then_inc(flip_read, 1)
                ch.link(v.tensor_tensor(X1[:, n, :], X[:, n, :], big[:, n, :], ALU.add))
                norm_batch(v, ch, X1, XN, big, st, b, 1e-5, var_ready, rstd_ready, b + 1)
                v.nop().then_inc(xn_ready, 1)

            def scans(b):
                lam = LAM[:, b % 2, :]
                v.wait_ge(act_out, 5 * b + 5)
                v.wait_ge(base_ready, 1)
                ch.link(v.tensor_scalar(lam, lam, 0.2, 1.0, ALU.mult, ALU.add))
                ch.link(v.tensor_scalar(lam, lam, base[:, 0:1], 0.0, ALU.mult, ALU.max))
                ch.link(v.tensor_scalar(lam, lam, 0.9995, None, ALU.min))
                for f in range(FE):
                    n = b * FE + f
                    v.wait_ge(made, 13 * b + 5 + f + 1)
                    if n >= 2:
                        v.wait_ge(scanned, n - 1)
                    v.tensor_tensor(KV[:, n % 2, :], pj[(13 * b + 5 + f) % 2][:], KT[:, b % 2, :],
                                    ALU.mult).then_inc(kv_read, 1)
                    v.wait_ge(kv_read, n + 1)
                    if n >= 2:
                        v.wait_ge(weighed, n - 1)
                    v.tensor_tensor_scan(SC[:, n % 2, :], lam, KV[:, n % 2, :], 0.0, ALU.mult,
                                         ALU.add).then_inc(scanned, 1)

            join(0)
            for b in range(B):
                if b + 1 < B:
                    join(b + 1)
                scans(b)

        @block.gpsimd
        def _(g):
            g.memset(neg_half[:], -0.5).then_inc(half_ready, 1)
            g.wait_ge(half_ready, 1)

            g.memset(flip[:], 0.0).then_inc(half_ready, 1)
            g.wait_ge(half_ready, 2)
            g.affine_select(out=flip[:], in_=flip[:], compare_op=ALU.not_equal, fill=1.0, base=1 - P,
                            pattern=[[1, P]], channel_multiplier=1).then_inc(flip_ready, 1)

            def rstd(b):
                n = slice(b * BT, b * BT + BT)
                g.wait_ge(var_ready, b + 1)
                g.tensor_tensor(st[:, 4, n], st[:, 3, n], neg_half[:, n], ALU.pow).then_inc(rstd_ready, 1)

            rstd(0)
            for b in range(B):
                if b + 1 < B:
                    rstd(b + 1)
                for f in range(FE):
                    n = b * FE + f
                    g.wait_ge(scanned, n + 1)
                    if n >= 2:
                        g.wait_ge(weighed_used, n - 1)
                    g.tensor_tensor(WT[:, n % 2, :], SC[:, n % 2, :], QT[:, b % 2, :], ALU.mult).then_inc(weighed, 1)

        @block.scalar
        def _(act):
            act.wait_ge(dec_in, DMA)
            act.wait_ge(w_in, 8 * DMA)
            act.activation(base[:], base[:], ACT.Sigmoid).then_inc(base_ready, 1)
            for b in range(B):
                for i in range(5):
                    act.wait_ge(made, 13 * b + i + 1)
                    src = pj[(13 * b + i) % 2]
                    if b >= 2 and i == 1:
                        act.wait_ge(weighed, FE * (b - 1))
                        act.wait_ge(scanned, FE * (b - 1))
                    if i == 0:
                        ins = act.copy(XNT[:, b * S:b * S + S], src[:])
                    elif i == 1:
                        ins = act.copy(QT[:, b % 2, :], src[:])
                    elif i == 2:
                        ins = act.copy(KT[:, b % 2, :], src[:])
                    elif i == 3:
                        ins = act.activation(C1[:], src[0:D // 4, :], ACT.Tanh, bias=c1b[:, 0:1])
                    else:
                        ins = act.activation(LAM[:, b % 2, :], src[:], ACT.Sigmoid, bias=c2b[:, 0:1])
                    ins.then_inc(act_out, 1)
                act.wait_ge(s1_ready, b + 1)
                act.copy(K.S1[:, b * BT:b * BT + BT, :], so[:]).then_inc(s1_out, 1)

        @block.tensor
        def _(pe):
            pe.wait_ge(w_in, 8 * DMA)

            def halves(dst, lhs, src, m=P):
                for c in range(S // CH):
                    mm = pe.matmul(dst[0:m, c * CH:c * CH + CH], lhs, src[:, c * CH:c * CH + CH], start=True, stop=True)
                mm.then_inc(made, 1)

            def share(b, f):
                n = b * FE + f
                pe.wait_ge(weighed, n + 1)
                if f == 0 and b >= 1:
                    pe.wait_ge(s1_out, b)
                for t in range(BT):
                    mm = pe.matmul(so[:, t, :], WT[:, n % 2, t * P:t * P + P], wo[:, f, :],
                                   start=(f == 0 and t % 4 == 0), stop=(f == FE - 1), skip_group_check=True)
                mm.then_inc(weighed_used, 1)
                if f == FE - 1:
                    pe.wait_ge(weighed_used, n + 1)
                    pe.nop().then_inc(s1_ready, 1)

            def unflip(b):
                if b >= 1:
                    pe.wait_ge(flip_read, b)
                for t in range(BT):
                    mm = pe.matmul(fs[:, t, :], flip[:], K.SACC[:, b * BT + t, :], start=True, stop=True)
                mm.then_inc(flipped, 1)

            pe.wait_ge(flip_ready, 1)
            unflip(0)
            for b in range(B):
                if b + 1 < B:
                    unflip(b + 1)
                pe.wait_ge(xn_ready, b + 1)
                if b >= 1:
                    pe.wait_ge(kv_read, FE * b)
                dst = pj[13 * b % 2]
                for t in range(BT):
                    mm = pe.transpose(dst[:, t * P:t * P + P], XN[:, b * BT + t, :], K.ident[:])
                mm.then_inc(made, 1)
                pe.wait_ge(act_out, 5 * b + 1)
                x = XNT[:, b * S:b * S + S]
                halves(pj[(13 * b + 1) % 2], wq[:], x)
                halves(pj[(13 * b + 2) % 2], wk[:], x)
                pe.wait_ge(act_out, 5 * b + 2)
                halves(pj[(13 * b + 3) % 2], c1w[:], x, D // 4)
                pe.wait_ge(act_out, 5 * b + 4)
                halves(pj[(13 * b + 4) % 2], c2w[:], C1[:])
                for f in range(FE):
                    if f == 1:
                        pe.wait_ge(act_out, 5 * b + 5)
                    if f >= 2:
                        pe.wait_ge(kv_read, FE * b + f - 1)
                    halves(pj[(13 * b + 5 + f) % 2], wv[:, f, :], x)
                    if f >= 2:
                        share(b, f - 2)
                share(b, FE - 2)
                share(b, FE - 1)


def finish(nc, K, io, sb, ps, sem):
    w_in, b_in, iota_ready = sem("fw_in"), sem("fb_in"), sem("iota1_ready")
    z_ready, z_out, max_sub, exp_ready, zm_ready = sem("z_ready"), sem("z_out"), sem("max1_sub"), sem("exp1_ready"), sem("zm_ready")
    zt_ready, zt_out, h_ready, h_out, o_ready, y_ready = (sem("zt_ready"), sem("zt_out"), sem("fh_ready"),
                                                          sem("fh_out"), sem("fo_ready"), sem("y_ready"))
    g1_ready, mixed, x2_ready, out_wr, own = sem("g1_ready"), sem("mixed"), sem("x2_ready"), sem("out_wr"), sem("fin_dve")
    ER = E * R
    NZ = E + ER
    wz = sb("gate_lora_a", [P, NZ])
    lb = sb("lora_b", [ER, F])
    wi, wo = sb("wi", [P, F]), sb("wo_t", [P, FT, D])
    wib, gb, wob = sb("wi_b", [P, FT]), sb("gate_b", [P, E]), sb("wo_b", [P, D])
    ZL, ZM = sb("z_rows", [P, NT, NZ]), sb("z_masked", [P, NT, ER])
    ZT = sb("z_t", [ER, B * S])
    io8, r1, hot, col = sb("iota8_1", [P, NT, E]), sb("route1_1", [P, NT, E]), sb("onehot1", [P, NT, E]), sb("cols1", [P, 2, NT])
    hT = [sb(f"fhid{i}", [P, FT, CH]) for i in range(2)]
    Y = [sb(f"y{i}", [P, 4, D]) for i in range(2)]
    ZB = 12
    pb = [ps(f"fin_ps{i}", [P, CH]) for i in range(8)]
    NJ = NT // 4

    with nc.Block() as block:

        @block.sync
        def _(sp):
            for dst, src in ((wz[:], io["wz"]), (lb[:], io["lora_b"]), (wi[:], io["wi"]),
                             (wo[:], io["wo_t"].rearrange("(i p) d -> p i d", p=P))):
                sp.dma_start(dst, src).then_inc(w_in, DMA)
            for dst, src in ((wib[:], io["wi_b"]), (gb[:], io["gate_b"].partition_broadcast(P)),
                             (wob[:], io["wo_b"].partition_broadcast(P))):
                sp.dma_start(dst, src).then_inc(b_in, DMA)
            for j in range(NJ):
                sp.wait_ge(x2_ready, j + 1)
                b, t = j // 2, 4 * (j % 2)
                sp.dma_start(io["out"][b].rearrange("(t p) d -> p t d", p=P)[:, t:t + 4, :],
                             K.X[:, 4 * j:4 * j + 4, :]).then_inc(out_wr, DMA)
            sp.wait_ge(out_wr, DMA * NJ)

        @block.gpsimd
        def _(g):
            g.iota(io8[:], pattern=[[0, NT], [1, E]], base=0, channel_multiplier=0,
                   allow_small_or_imprecise_dtypes=True).then_inc(iota_ready, 1)
            for j in range(NJ):
                g.wait_ge(mixed, j + 1)
                n = slice(4 * j, 4 * j + 4)
                g.tensor_tensor(K.X[:, n, :], K.X[:, n, :], K.S1[:, n, :], ALU.add).then_inc(x2_ready, 1)

        @block.tensor
        def _(pe):
            pe.wait_ge(w_in, 4 * DMA)
            for t in range(NT):
                k = t % ZB * NZ
                mm = pe.matmul(pb[t // ZB][:, k:k + NZ], K.XNT[:, t * P:t * P + P], wz[:], start=True, stop=True)
            mm.then_inc(z_ready, 1)
            pe.wait_ge(zm_ready, 1)
            for j in range(NJ):
                for t in range(4):
                    mm = pe.transpose(pb[j][0:ER, t * P:t * P + P], ZM[:, 4 * j + t, :], K.ident[:])
                mm.then_inc(zt_ready, 1)
            pe.wait_ge(zt_out, NJ)

            def hidden(j):
                for i in range(FT):
                    if j >= 1:
                        pe.wait_ge(h_out, FT * (j - 1) + i + 1)
                    pe.matmul(pb[i][:], wi[:, i * P:i * P + P], K.XNT[:, j * CH:j * CH + CH], start=True, stop=False)
                    pe.matmul(pb[i][:], lb[:, i * P:i * P + P], ZT[:, j * CH:j * CH + CH],
                              start=False, stop=True).then_inc(h_ready, 1)

            def out(j):
                s = j % 2
                o = pb[4 + s]
                if j >= 2:
                    pe.wait_ge(y_ready, j - 1)
                for i in range(FT):
                    pe.wait_ge(h_out, FT * j + i + 1)
                    for c in range(4):
                        mm = pe.matmul(o[:, c * P:c * P + P], hT[s][:, i, c * P:c * P + P], wo[:, i, :],
                                       start=(i == 0 and c == 0), stop=(i == FT - 1), skip_group_check=True)
                mm.then_inc(o_ready, 1)

            hidden(0)
            for j in range(NJ):
                if j + 1 < NJ:
                    hidden(j + 1)
                out(j)

        @block.scalar
        def _(act):
            act.wait_ge(max_sub, 1)
            act.activation(ZL[:, :, 0:E], ZL[:, :, 0:E], ACT.Exp).then_inc(exp_ready, 1)
            for j in range(NJ):
                act.wait_ge(zt_ready, j + 1)
                act.copy(ZT[:, j * CH:j * CH + CH], pb[j][0:ER, :]).then_inc(zt_out, 1)
            act.wait_ge(b_in, 3 * DMA)

            def relu(j):
                for i in range(FT):
                    act.wait_ge(h_ready, FT * j + i + 1)
                    if j >= 2 and i == 0:
                        act.wait_ge(o_ready, j - 1)
                    act.activation(hT[j % 2][:, i, :], pb[i][:], ACT.Relu, bias=wib[:, i:i + 1]).then_inc(h_out, 1)

            def gate(j):
                act.wait_ge(y_ready, j + 1)
                act.activation(Y[j % 2][:], Y[j % 2][:], ACT.Silu).then_inc(g1_ready, 1)

            for j in range(NJ):
                relu(j)
                if j >= 1:
                    gate(j - 1)
            gate(NJ - 1)

        @block.vector
        def _(v):
            ch = Chain(v, own)
            v.wait_ge(z_ready, 1)
            for k in range(3):
                n = min(ZB, NT - k * ZB)
                ins = v.tensor_copy(ZL[:, k * ZB:k * ZB + n, :], pb[k][:, 0:n * NZ].rearrange("p (t z) -> p t z", z=NZ))
            ch.link(ins)
            v.wait_ge(b_in, 3 * DMA)
            lg = ZL[:, :, 0:E]
            ch.link(v.tensor_tensor(lg, lg, mid_axis(gb[:], NT), ALU.add))
            ch.link(v.tensor_reduce(col[:, 0, :], lg, AX_X, ALU.max))
            v.tensor_tensor(lg, lg, last_axis(col[:, 0, :], E), ALU.subtract).then_inc(max_sub, 1)
            v.wait_ge(exp_ready, 1)
            v.wait_ge(iota_ready, 1)
            ch.link(v.tensor_scalar(r1[:], lg, 1.0, float(E), ALU.is_lt, ALU.mult))
            ch.link(v.tensor_tensor(r1[:], r1[:], io8[:], ALU.add))
            ch.link(v.tensor_reduce(col[:, 1, :], r1[:], AX_X, ALU.min))
            ch.link(v.tensor_tensor(hot[:], io8[:], last_axis(col[:, 1, :], E), ALU.is_equal))
            for r in range(R):
                ins = v.tensor_tensor(ZM[:].rearrange("p t (e r) -> p t e r", r=R)[:, :, :, r],
                                      ZL[:, :, E:NZ].rearrange("p t (e r) -> p t e r", r=R)[:, :, :, r], hot[:], ALU.mult)
            ins.then_inc(zm_ready, 1)
            for j in range(NJ):
                s, n = j % 2, slice(4 * j, 4 * j + 4)
                v.wait_ge(o_ready, j + 1)
                if j >= 2:
                    v.wait_ge(mixed, j - 1)
                v.tensor_tensor(Y[s][:], pb[4 + s][:].rearrange("p (t d) -> p t d", d=D), mid_axis(wob[:], 4),
                                ALU.add).then_inc(y_ready, 1)
                v.wait_ge(g1_ready, j + 1)
                v.tensor_tensor(K.S1[:, n, :], K.S1[:, n, :], Y[s][:], ALU.mult).then_inc(mixed, 1)


def program(nc, io):
    with ExitStack() as outer:
        def maker(stack):
            def sb(name, shape, dt=F32):
                return stack.enter_context(nc.sbuf_tensor(name, shape, dt))

            def ps(name, shape, dt=F32):
                return stack.enter_context(nc.psum_tensor(name, shape, dt))
            return sb, ps

        def sem(name):
            return outer.enter_context(nc.semaphore(name))

        sb, _ = maker(outer)
        K = Shared()
        K.ident = sb("ident", [P, P])
        K.X = sb("x", [P, NT, D])
        K.G0 = sb("g0", [P, NT, D])
        K.disp = nc.dram_tensor("dispatch", [E * CAP, D], F32, kind="Internal").ap()
        K.eout = nc.dram_tensor("expert_rows", [E * CAP, D], F32, kind="Internal").ap()
        K.fscr = nc.dram_tensor("bias_by_distance", [H, FLEN], F32, kind="Internal").ap()
        K.vscr = nc.dram_tensor("v_parts", [B * H, P, BT, 2 * DH], BF16, kind="Internal").ap()
        K.qkscr = nc.dram_tensor("qk_parts", [B * G, P, 4, S], BF16, kind="Internal").ap()

        def run(block):
            with ExitStack() as own:
                block_sb, block_ps = maker(own)
                block(nc, K, io, block_sb, block_ps, sem)

        with ExitStack() as layer0:
            sb0, _ = maker(layer0)
            K.XN, K.XNT = sb0("xn", [P, NT, D]), sb0("xn_t", [P, B * S])
            with ExitStack() as moe:
                sb_moe, _ = maker(moe)
                K.A, K.AT = sb_moe("a", [P, NT, D]), sb_moe("a_t", [P, B * S])
                K.coef_res, K.coef_moe = sb_moe("coef_res", [P, NT]), sb_moe("coef_moe", [P, NT])
                K.gather_idx, K.scatter_idx = sb_moe("gather_idx", [P, NT], U32), sb_moe("scatter_idx", [P, NT], U32)
                with ExitStack() as zeros:
                    K.Z = maker(zeros)[0]("zeros", [P, E * CAP * D // P])
                    run(prepare)
                with ExitStack() as rows:
                    sb_rows, _ = maker(rows)
                    K.RES, K.MOE = sb_rows("res_out", [P, NT, D]), sb_rows("moe_out", [P, NT, D])
                    run(experts)
            run(project)
        K.SACC = sb("s0", [P, NT, D])
        run(attend)
        K.XN, K.XNT, K.S1 = sb("xn1", [P, NT, D]), sb("xn1_t", [P, B * S]), sb("s1", [P, NT, D])
        run(recur)
        run(finish)


def layouts(inp):
    import numpy as np
    a = {k: np.ascontiguousarray(v) for k, v in inp.items()}
    c = np.ascontiguousarray
    qkv = a["L0_attn_qkv_w"].reshape(3, H, DH, D)

    def pair(w):
        return w.reshape(G, P, D).transpose(0, 2, 1)

    def swapped(w):
        return np.concatenate([w[:, DH // 2:], w[:, :DH // 2]], axis=1)
    wqk = np.stack([pair(qkv[0]), pair(swapped(qkv[0])), pair(qkv[1]), pair(swapped(qkv[1]))], axis=2)
    wo = a["L0_attn_out_w"].reshape(D, H, DH).transpose(1, 2, 0)
    wo2 = np.concatenate([wo, wo], axis=1)
    he = a["L1_attn_v_w"].reshape(H, 8, D)
    vrep = np.repeat(he.transpose(2, 1, 0)[:, :, :, None], 8, axis=3).reshape(D, 8, P)
    ow = a["L1_attn_o_w"].reshape(D, H, 8)
    orep = np.repeat(ow.transpose(1, 2, 0)[:, None], 8, axis=1).reshape(P, 8, D)
    cs2 = np.repeat(a["L1_attn_cs_w2"].T[:, :, None], 8, axis=2).reshape(D // 4, P)
    return dict(
        x=a["L0_attn_x"], wqk=c(wqk), wv=c(a["L0_attn_qkv_w"][2 * H * DH:].T), wo2=c(wo2),
        bias_p=a["L0_attn_bias_p"].reshape(H, 1), bias_a=a["L0_attn_bias_a"].reshape(H, 1), freqs=a["L0_attn_rope_freqs"],
        attn_nw=a["L0_ffn_attn_nw"], attn_nb=a["L0_ffn_attn_nb"], wg=a["L0_ffn_wg"], inter_w=a["L0_ffn_inter_w"],
        inter_b=c(a["L0_ffn_inter_b"].reshape(E, FT, P).transpose(2, 0, 1)), output_w=a["L0_ffn_output_w"], output_b=a["L0_ffn_output_b"],
        res_inter_w=a["L0_ffn_res_inter_w"], res_inter_b=c(a["L0_ffn_res_inter_b"].reshape(FT, P).T),
        res_output_w=a["L0_ffn_res_output_w"], res_output_b=a["L0_ffn_res_output_b"], res_coef=a["L0_ffn_res_coef"],
        q_w=c(a["L1_attn_q_w"].T), k_w=c(a["L1_attn_k_w"].T), v_w=c(vrep), o_w=c(orep), cs_w1=c(a["L1_attn_cs_w1"].T),
        cs_b1=a["L1_attn_cs_b1"].reshape(D // 4, 1), cs_w2=c(cs2),
        cs_b2=c(np.repeat(a["L1_attn_cs_b2"], 8).reshape(P, 1)), decay=a["L1_attn_decay_params"].reshape(P, 1),
        wz=c(np.concatenate([a["L1_ffn_gate_W"].T, a["L1_ffn_lora_A"].reshape(E * R, D).T], axis=1)),
        gate_b=a["L1_ffn_gate_b"], wi=c(a["L1_ffn_wi_W"].T), wi_b=c(a["L1_ffn_wi_b"].reshape(FT, P).T), wo_t=c(a["L1_ffn_wo_W"].T),
        wo_b=a["L1_ffn_wo_b"], lora_b=c(a["L1_ffn_lora_B"].transpose(0, 2, 1).reshape(E * R, F)),
    )


def kernel(**inputs):
    import numpy as np
    import concourse.bacc as bacc
    from concourse.bass_utils import run_bass_kernel_spmd

    nc = bacc.Bacc("TRN2", target_bir_lowering=False, num_devices=1)
    arrays, aps = {}, {}
    for name, a in layouts(inputs).items():
        arrays[f"in_{name}"] = a
        aps[name] = nc.dram_tensor(f"in_{name}", a.shape, mybir.dt.from_np(a.dtype), kind="ExternalInput").ap()
    aps["out"] = nc.dram_tensor("out_0", [B, S, D], F32, kind="ExternalOutput").ap()
    program(nc, aps)
    r = run_bass_kernel_spmd(nc, [arrays], core_ids=[0])
    return r.results[0]["out_0"]
```

```python
from contextlib import ExitStack
import math

import concourse.bass as bass
from concourse import mybir

ALU = mybir.AluOpType
ACT = mybir.ActivationFunctionType
AX_X = mybir.AxisListType.X
F32 = mybir.dt.float32
BF16 = mybir.dt.bfloat16
I32 = mybir.dt.int32
U32 = mybir.dt.uint32

P = 128
B, S, D = 4, 1024, 128
NT = B * S // P
BT = S // P
H, DH = 16, 64
G = H // 2
E, F, R = 8, 512, 4
FT = F // P
CAP = B * S // E
SCALE = 1.0 / math.sqrt(DH)
RING = 4
DMA = 16
CH = 512
MAGIC = 12582912.0
TWO_PI_1 = 6.28125
TWO_PI_2 = 0.00193500518798828125
TWO_PI_3 = 2.0 * math.pi - TWO_PI_1 - TWO_PI_2
TAB = 2 * S - P
FLEN = 2 * S


class Shared:
    pass


class Chain:

    def __init__(self, eng, sem):
        self.eng, self.sem, self.count = eng, sem, 0

    def link(self, ins):
        self.count += 1
        ins.then_inc(self.sem, 1)
        self.eng.wait_ge(self.sem, self.count)


def last_axis(ap, n):
    return ap.unsqueeze(2).to_broadcast([ap.shape[0], ap.shape[1], n])


def mid_axis(ap, n):
    return ap.unsqueeze(1).to_broadcast([ap.shape[0], n, ap.shape[1]])


def row_stats(v, ch, src, st, b, eps, sem_var):
    for t in range(b * BT, b * BT + BT):
        ins = v.bn_stats(st.six[:, t, :], src[:, t, :])
    ch.link(ins)
    for t in range(b * BT, b * BT + BT):
        ins = v.bn_aggr(st.mean_var[:, t, :], st.six[:, t, :])
    ch.link(ins)
    n = slice(b * BT, b * BT + BT)
    v.tensor_scalar(st.var[:, n], st.mean_var[:, n, 1], eps, None, ALU.add).then_inc(sem_var, 1)


def apply_norm(v, ch, src, dst, st, b, sem_rstd, nth):
    v.wait_ge(sem_rstd, nth)
    for t in range(b * BT, b * BT + BT):
        ins = v.tensor_scalar(dst[:, t, :], src[:, t, :], st.mean_var[:, t, 0:1], st.rstd[:, t:t + 1],
                              ALU.subtract, ALU.mult)
    ch.link(ins)


class NormStats:

    def __init__(self, sb, name):
        self.six = sb(name + "_six", [P, NT, 6])
        self.mean_var = sb(name + "_mean_var", [P, NT, 2])
        self.var, self.rstd = sb(name + "_var", [P, NT]), sb(name + "_rstd", [P, NT])


def prepare(nc, K, io, sb, ps, sem):
    x_in = [sem(f"x_in{b}") for b in range(B)]
    par_in, wg_in, zero_ready, zero_out = sem("par_in"), sem("wg_in"), sem("zero_ready"), sem("zero_out")
    var_ready, rstd_ready, half_ready = sem("var_ready"), sem("rstd_ready"), sem("half_ready")
    xn_ready, a_ready, tr_ready, tr_out = sem("xn_ready"), sem("a_ready"), sem("tr_ready"), sem("tr_out")
    ident_ready, logit_ready, max_sub, exp_ready = sem("ident_ready"), sem("logit_ready"), sem("max_sub"), sem("exp_ready")
    hot_ready, pos_ready, tri_ready, iota_ready = sem("hot_ready"), sem("pos_ready"), sem("tri_ready"), sem("iota_ready")
    dve_own, pool_own = sem("prep_dve"), sem("prep_pool")

    st = [NormStats(sb, "ln0"), NormStats(sb, "ln_moe")]
    neg_half = sb("neg_half", [P, NT])
    gbc, bbc = sb("attn_nw_rows", [P, D]), sb("attn_nb_rows", [P, D])
    wgc = sb("wgc", [P, E + 2])
    tri, ones = sb("tri", [P, P]), sb("ones_sq", [P, P])
    lg = sb("logits0", [P, NT, E + 2])
    r1, r2 = sb("route1", [P, NT, E]), sb("route2", [P, NT, E])
    hot = sb("onehot", [P, NT, E])
    io8 = sb("iota8", [P, NT, E])
    col = sb("route_cols", [P, 12, NT])
    one_row = sb("one_row", [P, NT])
    w1r, w2r = sb("w1_res", [P, F]), sb("w2_res", [P, FT, D])
    b1r = sb("b1_res_cols", [P, FT])
    hT = [sb(f"res_hidden_t{i}", [P, FT, CH]) for i in range(2)]
    res_in, res_bias_in = sem("res_in"), sem("res_bias_in")
    h_ready, h_out, o_ready, o_out = sem("rh_ready"), sem("rh_out"), sem("ro_ready"), sem("ro_out")
    idx_ready, scat = sem("idx_ready"), sem("scattered")
    tp = [ps(f"prep_t{i}", [P, 2 * CH]) for i in range(2)]
    lps, counts = ps("logit_ps", [P, NT, E + 2]), ps("count_ps", [P, 2, NT, E])
    pre, tot = counts[:, 0], counts[:, 1]
    op = [ps(f"res_out_ps{i}", [P, CH // P, D]) for i in range(2)]
    CT = CH // P
    NR = NT // CT
    X, XN, A = sb("x_rows", [P, NT, D]), K.XN, K.A
    COUNT_JOB = 1

    def hidden_ps(i):
        return tp[i // 2][:, i % 2 * CH:i % 2 * CH + CH]

    def take_out(act, j):
        act.wait_ge(o_ready, j + 1)
        act.copy(K.RES[:, j * CT:j * CT + CT, :], op[j % 2][:]).then_inc(o_out, 1)

    norm_order = [(0, 0), (0, 1), (1, 0), (0, 2), (1, 1), (0, 3), (1, 2), (1, 3)]
    norm_done = [[], [(0, 0)], [(0, 1)], [(1, 0)], [(0, 2)], [(1, 1)], [(0, 3)], [(1, 2), (1, 3)]]

    with nc.Block() as block:

        @block.sync
        def _(sp):
            for b in range(B):
                sp.dma_start(X[:, b * BT:b * BT + BT, :],
                             io["x"][b].rearrange("(t p) d -> p t d", p=P)).then_inc(x_in[b], DMA)
            sp.dma_start(gbc[:], io["attn_nw"].partition_broadcast(P)).then_inc(par_in, DMA)
            sp.dma_start(bbc[:], io["attn_nb"].partition_broadcast(P)).then_inc(par_in, DMA)
            sp.dma_start(wgc[:, 0:E], io["wg"]).then_inc(wg_in, DMA)
            sp.dma_start(wgc[:, E:E + 2], io["res_coef"]).then_inc(wg_in, DMA)
            sp.dma_start(w1r[:], io["res_inter_w"]).then_inc(res_in, DMA)
            sp.dma_start(w2r[:], io["res_output_w"].rearrange("(i p) d -> p i d", p=P)).then_inc(res_in, DMA)
            sp.dma_start(b1r[:], io["res_inter_b"]).then_inc(res_bias_in, DMA)
            sp.wait_ge(zero_ready, 1)
            sp.dma_start(K.disp.rearrange("(p t) d -> p (t d)", p=P), K.Z[:]).then_inc(zero_out, DMA)
            for e in range(RING):
                load_expert(sp, K, io, e)
            sp.wait_ge(scat, DMA * NT)
            for e in range(RING):
                load_rows(sp, K, e)

        @block.gpsimd
        def _(g):
            g.memset(K.ident[:], 0.0).then_inc(pool_own, 1)
            g.memset(neg_half[:], -0.5).then_inc(half_ready, 1)
            g.wait_ge(pool_own, 1)
            g.affine_select(out=K.ident[:], in_=K.ident[:], compare_op=ALU.not_equal, fill=1.0, base=0,
                            pattern=[[-1, P]], channel_multiplier=1).then_inc(ident_ready, 1)
            g.memset(K.Z[:], 0.0).then_inc(zero_ready, 1)
            g.memset(ones[:], 1.0).then_inc(pool_own, 1)
            g.wait_ge(pool_own, 2)
            g.affine_select(out=tri[:], in_=ones[:], compare_op=ALU.is_gt, fill=0.0, base=0,
                            pattern=[[1, P]], channel_multiplier=-1).then_inc(tri_ready, 1)
            g.memset(one_row[:], 1.0).then_inc(tri_ready, 1)
            g.iota(io8[:], pattern=[[0, NT], [1, E]], base=0, channel_multiplier=0,
                   allow_small_or_imprecise_dtypes=True).then_inc(iota_ready, 1)
            g.wait_ge(half_ready, 1)
            for n, (m, b) in enumerate(norm_order):
                g.wait_ge(var_ready, n + 1)
                k = slice(b * BT, b * BT + BT)
                g.tensor_tensor(st[m].rstd[:, k], st[m].var[:, k], neg_half[:, k], ALU.pow).then_inc(rstd_ready, 1)
            g.wait_ge(a_ready, B)
            g.wait_ge(idx_ready, 1)
            g.wait_ge(zero_out, DMA)
            for t in range(NT):
                g.indirect_dma_start(out=K.disp, out_offset=bass.IndirectOffsetOnAxis(K.scatter_idx[:, t:t + 1], 0),
                                     in_=K.A[:, t, :], in_offset=None, bounds_check=E * CAP - 1,
                                     oob_is_err=False).then_inc(scat, DMA)

        @block.vector
        def _(v):
            ch = Chain(v, dve_own)
            def affine(b, nth):
                v.wait_ge(rstd_ready, nth)
                for t in range(b * BT, b * BT + BT):
                    ins = v.scalar_tensor_tensor(out=A[:, t, :], in0=XN[:, t, :], scalar=st[1].mean_var[:, t, 0:1],
                                                 in1=gbc[:], op0=ALU.subtract, op1=ALU.mult)
                ch.link(ins)
                for t in range(b * BT, b * BT + BT):
                    ins = v.scalar_tensor_tensor(out=A[:, t, :], in0=A[:, t, :], scalar=st[1].rstd[:, t:t + 1],
                                                 in1=bbc[:], op0=ALU.mult, op1=ALU.add)
                ins.then_inc(a_ready, 1)

            for i, (m, b) in enumerate(norm_order):
                if m == 0:
                    v.wait_ge(x_in[b], DMA)
                    row_stats(v, ch, X, st[0], b, 1e-5, var_ready)
                else:
                    row_stats(v, ch, XN, st[1], b, 1e-12, var_ready)
                for m, b in norm_done[i]:
                    nth = norm_order.index((m, b)) + 1
                    if m == 0:
                        apply_norm(v, ch, X, XN, st[0], b, rstd_ready, nth)
                        v.nop().then_inc(xn_ready, 1)
                    else:
                        if b == 0:
                            v.wait_ge(par_in, 2 * DMA)
                        affine(b, nth)
            v.wait_ge(logit_ready, 1)
            ch.link(v.tensor_copy(lg[:], lps[:]))
            ch.link(v.tensor_reduce(col[:, 0, :], lg[:, :, 0:E], AX_X, ALU.max))
            ch.link(v.tensor_reduce(col[:, 1, :], lg[:, :, E:E + 2], AX_X, ALU.max))
            ch.link(v.tensor_tensor(lg[:, :, 0:E], lg[:, :, 0:E], last_axis(col[:, 0, :], E), ALU.subtract))
            v.tensor_tensor(lg[:, :, E:E + 2], lg[:, :, E:E + 2], last_axis(col[:, 1, :], 2),
                            ALU.subtract).then_inc(max_sub, 1)
            v.wait_ge(exp_ready, 1)
            ch.link(v.tensor_reduce(col[:, 2, :], lg[:, :, 0:E], AX_X, ALU.add))
            ch.link(v.reciprocal(col[:, 3, :], col[:, 2, :]))
            ch.link(v.tensor_reduce(col[:, 4, :], lg[:, :, E:E + 2], AX_X, ALU.add))
            ch.link(v.reciprocal(col[:, 5, :], col[:, 4, :]))
            ch.link(v.tensor_tensor(K.coef_res[:], lg[:, :, E], col[:, 5, :], ALU.mult))
            ch.link(v.tensor_tensor(col[:, 6, :], lg[:, :, E + 1], col[:, 5, :], ALU.mult))
            v.wait_ge(iota_ready, 1)
            ch.link(v.tensor_scalar(r1[:], lg[:, :, 0:E], 1.0, float(E), ALU.is_lt, ALU.mult))
            ch.link(v.tensor_tensor(r1[:], r1[:], io8[:], ALU.add))
            ch.link(v.tensor_reduce(col[:, 7, :], r1[:], AX_X, ALU.min))
            v.tensor_tensor(hot[:], io8[:], last_axis(col[:, 7, :], E), ALU.is_equal).then_inc(hot_ready, 1)
            v.wait_ge(pos_ready, 1)
            ch.link(v.tensor_copy(r2[:], tot))
            v.wait_ge(tri_ready, 2)
            for e in range(E):
                ins = v.tensor_tensor_scan(r1[:, :, e], one_row[:], r2[:, :, e], 0.0, ALU.mult, ALU.add)
            ch.link(ins)
            ch.link(v.tensor_tensor(r1[:], r1[:], r2[:], ALU.subtract))
            ch.link(v.tensor_tensor(r1[:], pre, r1[:], ALU.add))
            ch.link(v.tensor_tensor(r1[:], r1[:], hot[:], ALU.mult))
            ch.link(v.tensor_reduce(col[:, 8, :], r1[:], AX_X, ALU.add))
            ch.link(v.tensor_scalar(col[:, 9, :], col[:, 8, :], float(CAP), None, ALU.is_lt))
            ch.link(v.tensor_tensor(K.coef_moe[:], col[:, 6, :], col[:, 3, :], ALU.mult))
            ch.link(v.tensor_tensor(K.coef_moe[:], K.coef_moe[:], col[:, 9, :], ALU.mult))
            ch.link(v.scalar_tensor_tensor(out=col[:, 10, :], in0=col[:, 7, :], scalar=float(CAP),
                                           in1=col[:, 8, :], op0=ALU.mult, op1=ALU.add))
            ch.link(v.tensor_tensor(col[:, 10, :], col[:, 10, :], col[:, 9, :], ALU.mult))
            ch.link(v.tensor_copy(K.gather_idx[:], col[:, 10, :]))
            ch.link(v.tensor_scalar(col[:, 11, :], col[:, 9, :], -float(2 * E * CAP), float(2 * E * CAP),
                                    ALU.mult, ALU.add))
            ch.link(v.tensor_tensor(col[:, 11, :], col[:, 11, :], col[:, 10, :], ALU.add))
            v.tensor_copy(K.scatter_idx[:], col[:, 11, :]).then_inc(idx_ready, 1)

        @block.tensor
        def _(pe):
            pe.wait_ge(ident_ready, 1)
            for n in range(2 * B):
                b, src = n // 2, (XN, A)[n % 2]
                pe.wait_ge((xn_ready, a_ready)[n % 2], b + 1)
                if n >= 2:
                    pe.wait_ge(tr_out, n - 1)
                for t in range(BT):
                    mm = pe.transpose(tp[n % 2][:, t * P:t * P + P], src[:, b * BT + t, :], K.ident[:])
                mm.then_inc(tr_ready, 1)
            pe.wait_ge(wg_in, 2 * DMA)
            pe.wait_ge(tr_out, 2 * B)
            for t in range(NT):
                mm = pe.matmul(lps[:, t, :], K.AT[:, t * P:t * P + P], wgc[:], start=True, stop=True)
            mm.then_inc(logit_ready, 1)
            pe.wait_ge(res_in, 2 * DMA)

            def hidden(j):
                for i in range(FT):
                    if j >= 1:
                        pe.wait_ge(h_out, FT * (j - 1) + i + 1)
                    pe.matmul(hidden_ps(i), w1r[:, i * P:i * P + P], K.AT[:, j * CH:j * CH + CH],
                              start=True, stop=True).then_inc(h_ready, 1)

            def out(j):
                s = j % 2
                if j >= 2:
                    pe.wait_ge(o_out, j - 1)
                for i in range(FT):
                    pe.wait_ge(h_out, FT * j + i + 1)
                    for c in range(CT):
                        mm = pe.matmul(op[s][:, c, :], hT[s][:, i, c * P:c * P + P], w2r[:, i, :],
                                       start=(i == 0 and c == 0), stop=(i == FT - 1), skip_group_check=True)
                mm.then_inc(o_ready, 1)

            hidden(0)
            for j in range(NR):
                if j + 1 < NR:
                    hidden(j + 1)
                if j == COUNT_JOB:
                    pe.wait_ge(hot_ready, 1)
                    pe.wait_ge(tri_ready, 1)
                    pe.matmul(pre, tri[:], hot[:], start=True, stop=True)
                    pe.matmul(tot, ones[:], hot[:], start=True, stop=True).then_inc(pos_ready, 1)
                out(j)

        @block.scalar
        def _(act):
            for n in range(2 * B):
                b, dst = n // 2, (K.XNT, K.AT)[n % 2]
                act.wait_ge(tr_ready, n + 1)
                act.copy(dst[:, b * S:b * S + S], tp[n % 2][:]).then_inc(tr_out, 1)
            act.wait_ge(max_sub, 1)
            act.activation(lg[:], lg[:], ACT.Exp).then_inc(exp_ready, 1)
            act.wait_ge(res_bias_in, DMA)
            for j in range(NR):
                for i in range(FT):
                    act.wait_ge(h_ready, FT * j + i + 1)
                    if j >= 2 and i == 0:
                        act.wait_ge(o_ready, j - 1)
                    act.activation(hT[j % 2][:, i, :], hidden_ps(i), ACT.Gelu_apprx_tanh,
                                   bias=b1r[:, i:i + 1]).then_inc(h_out, 1)
                if j >= 1:
                    take_out(act, j - 1)
            take_out(act, NR - 1)


def load_expert(sp, K, io, e):
    s = e % RING
    sp.dma_start(K.w1[s][:], io["inter_w"][e]).then_inc(K.w_in[s], DMA)
    sp.dma_start(K.w2[s][:], io["output_w"][e].rearrange("(i p) d -> p i d", p=P)).then_inc(K.w_in[s], DMA)


def load_rows(sp, K, e):
    s = e % RING
    sp.dma_start(K.dx[s][:], K.disp[bass.ts(e, CAP), :].rearrange("(c p) d -> p c d", p=P)).then_inc(K.d_in[s], DMA)


def experts(nc, K, io, sb, ps, sem):
    bias_in = sem("bias_in")
    dt_ready, dt_out = sem("dt_ready"), sem("dt_out")
    h_ready, h_out, o_ready, o_out = sem("h_ready"), sem("h_out"), sem("o_ready"), sem("o_out")
    e_wr = [sem("e_wr0"), sem("e_wr1")]
    own = sem("exp_dve")

    b1 = sb("b1_cols", [P, E, FT])
    b2, b2r = sb("b2_rows", [P, E * D]), sb("b2_res_rows", [P, D])
    dT = [sb(f"dispatched_t{i}", [P, CAP]) for i in range(2)]
    hT = [sb(f"hidden_t{i}", [P, FT, CAP]) for i in range(2)]
    eo = [sb(f"expert_out{i}", [P, CAP // P, D]) for i in range(2)]
    hp = [ps(f"hid_ps{i}", [P, CH]) for i in range(4)]
    op = [ps(f"out_ps{i}", [P, CAP // P, D]) for i in range(2)]
    tp = [ps(f"dt_ps{i}", [P, CH]) for i in range(2)]
    CT = CAP // P
    w1, w2, dx = K.w1, K.w2, K.dx

    with nc.Block() as block:

        @block.sync
        def _(sp):
            sp.dma_start(b1[:], io["inter_b"]).then_inc(bias_in, DMA)
            sp.dma_start(b2[:], io["output_b"].rearrange("e d -> (e d)").partition_broadcast(P)).then_inc(bias_in, DMA)
            sp.dma_start(b2r[:], io["res_output_b"].partition_broadcast(P)).then_inc(bias_in, DMA)
            for e in range(E):
                sp.wait_ge(o_out, e + 1)
                sp.dma_start(K.eout[bass.ts(e, CAP), :].rearrange("(c p) d -> p c d", p=P), eo[e % 2][:]).then_inc(e_wr[e % 2], DMA)
                if e + RING < E:
                    load_expert(sp, K, io, e + RING)
                    load_rows(sp, K, e + RING)
            for s in range(2):
                sp.wait_ge(e_wr[s], DMA * E // 2)

        @block.tensor
        def _(pe):
            def turn(e):
                pe.wait_ge(K.d_in[e % RING], DMA * (e // RING + 1))
                if e >= 2:
                    pe.wait_ge(dt_out, e - 1)
                for c in range(CT):
                    mm = pe.transpose(tp[e % 2][:, c * P:c * P + P], dx[e % RING][:, c, :], K.ident[:])
                mm.then_inc(dt_ready, 1)

            def hidden(e):
                pe.wait_ge(K.w_in[e % RING], 2 * DMA * (e // RING + 1))
                pe.wait_ge(dt_out, e + 1)
                for i in range(FT):
                    if e >= 1:
                        pe.wait_ge(h_out, FT * (e - 1) + i + 1)
                    pe.matmul(hp[i][:], w1[e % RING][:, i * P:i * P + P], dT[e % 2][:], start=True,
                              stop=True).then_inc(h_ready, 1)

            def out(e):
                s = e % 2
                if e >= 2:
                    pe.wait_ge(o_out, e - 1)
                for i in range(FT):
                    pe.wait_ge(h_out, FT * e + i + 1)
                    for c in range(CT):
                        mm = pe.matmul(op[s][:, c, :], hT[s][:, i, c * P:c * P + P], w2[e % RING][:, i, :],
                                       start=(i == 0 and c == 0), stop=(i == FT - 1), skip_group_check=True)
                mm.then_inc(o_ready, 1)

            turn(0)
            turn(1)
            hidden(0)
            for e in range(E):
                if e + 2 < E:
                    turn(e + 2)
                if e + 1 < E:
                    hidden(e + 1)
                out(e)

        @block.scalar
        def _(act):
            act.wait_ge(bias_in, 3 * DMA)
            for e in range(E):
                for i in range(FT):
                    act.wait_ge(h_ready, FT * e + i + 1)
                    if e >= 2 and i == 0:
                        act.wait_ge(o_ready, e - 1)
                    act.activation(hT[e % 2][:, i, :], hp[i][:], ACT.Gelu_apprx_tanh, bias=b1[:, e, i:i + 1]).then_inc(h_out, 1)

        @block.vector
        def _(v):
            ch = Chain(v, own)

            def take_rows(e):
                v.wait_ge(dt_ready, e + 1)
                if e >= 2:
                    v.wait_ge(h_ready, FT * (e - 1))
                v.tensor_copy(dT[e % 2][:], tp[e % 2][:]).then_inc(dt_out, 1)

            def residual(b):
                n = slice(b * BT, b * BT + BT)
                ch.link(v.tensor_tensor(K.RES[:, n, :], K.RES[:, n, :], mid_axis(b2r[:], BT), ALU.add))
                ch.link(v.tensor_tensor(K.RES[:, n, :], K.RES[:, n, :], last_axis(K.coef_res[:, n], D), ALU.mult))
                ch.link(v.tensor_tensor(K.G0[:, n, :], K.RES[:, n, :], K.XN[:, n, :], ALU.add))

            take_rows(0)
            take_rows(1)
            v.wait_ge(bias_in, 3 * DMA)
            for e in range(E):
                s = e % 2
                if e + 2 < E:
                    take_rows(e + 2)
                if e < B:
                    residual(e)
                v.wait_ge(o_ready, e + 1)
                if e >= 2:
                    v.wait_ge(e_wr[s], DMA * (e // 2))
                v.tensor_tensor(eo[s][:], op[s][:], mid_axis(b2[:, e * D:e * D + D], CT), ALU.add).then_inc(o_out, 1)


def project(nc, K, io, sb, ps, sem):
    fr_in, bp_in, wv_in = sem("fr_in"), sem("bp_in"), sem("wv_in")
    pos_i, sin_arg, sin_out, tab_neg = sem("pos_i"), sem("sin_arg"), sem("sin_out"), sem("tab_neg")
    ln_arg, ln_out, f_ready, f_wr = sem("ln_arg"), sem("ln_out"), sem("f_ready"), sem("f_wr")
    v_ready, vhi, vlo, v_wr = sem("v_ready"), sem("vhi"), sem("vlo"), [sem(f"v_wr{s}") for s in range(4)]
    wqk_in = [sem("wqk_in0"), sem("wqk_in1")]
    qk_ready, qk_read, pair, summed = sem("qk_ready"), sem("qk_read"), sem("pair"), sem("summed")
    hi_ready, lo_ready, qk_wr = sem("hi_ready"), sem("lo_ready"), [sem(f"qk_wr{s}") for s in range(4)]
    gath, mixed, mix_ready, g0_ready = sem("gathered"), sem("moe_scaled"), sem("mix_ready"), sem("g0_ready")
    own = sem("proj_dve")

    freq = sb("freq", [P, 1])
    pos = sb("pos", [P, S])
    posi = sb("pos_int", [P, S], I32)
    ang, tn = sb("ang", [P, S]), sb("turns", [P, S])
    COS, SIN = sb("cos_table", [P, S]), sb("sin_table", [P, S])
    half_pi, one_col = sb("half_pi", [P, 1]), sb("one_col", [P, 1])
    disti, dist = sb("dist_int", [H, FLEN], I32), sb("dist", [H, FLEN])
    bp, ba = sb("bias_p", [H, 1]), sb("bias_a", [H, 1])
    wv = sb("wv", [P, H * DH])
    vt = [sb(f"v_parts{i}", [P, H, 2, DH], BF16) for i in range(4)]
    wqk = [sb(f"wqk{i}", [P, 4, P]) for i in range(2)]
    t1 = [sb(f"rope1_{i}", [P, 2, CH]) for i in range(4)]
    t2 = [sb(f"rope2_{i}", [P, 2, CH]) for i in range(4)]
    parts = [sb(f"qk_parts{i}", [P, 4, CH], BF16) for i in range(4)]
    pp = [ps(f"proj_ps{i}", [P, 4, CH]) for i in range(2)]
    NC = S // CH
    XNT = K.XNT

    def jobs():
        for b in range(B):
            for c in range(NC):
                yield b * NC + c, b, c

    NJ = B * NC

    def tiles(ap):
        return ap.rearrange("p (t j) -> p t j", j=P)

    def rotated(r, i):
        ap = tiles(t1[r][:, i, :])
        return ap[:, :, ::-1] if i == 0 else ap

    LEAD = 2

    def run_jobs(eng, step):
        for u in range(-LEAD, 0):
            step(0, u, lambda x: x >= 0)
        with eng.Fori(0, G - 1) as gi:
            for u in range(NJ):
                step(gi, u, lambda x: True)
        for u in range(NJ):
            step(G - 1, u, lambda x: x < NJ)

    def rope(v, gi, j):
        c, s, r = j % NC, j % 2, j % 4
        cs = slice(c * CH, c * CH + CH)
        q4 = pp[s][:].rearrange("p (k w) c -> p k w c", w=2)
        v.wait_ge(qk_ready, gi * NJ + (j + 1))
        v.wait_ge(lo_ready, gi * NJ + max(j, 1))
        v.tensor_tensor(t1[r][:], q4[:, :, 0, :], mid_axis(COS[:, cs], 2), ALU.mult)
        v.tensor_tensor(t2[r][:], q4[:, :, 1, :], mid_axis(SIN[:, cs], 2), ALU.mult).then_inc(pair, 1)

    def hi_part(act, gi, j):
        s = j % 4
        act.wait_ge(summed, gi * NJ + (j + 1))
        act.wait_ge(qk_wr[s], gi * (DMA * NJ // 4) + (DMA * (j // 4) + 1))
        act.activation(tiles(parts[s][:, 0, :]), rotated(s, 0), ACT.Copy, scale=SCALE).then_inc(hi_ready, 1)
        act.activation(parts[s][:, 2, :], t1[s][:, 1, :], ACT.Copy).then_inc(hi_ready, 1)

    def lo_part(v, gi, j):
        s = j % 4
        v.wait_ge(hi_ready, gi * (2 * NJ) + 2 * (j + 1))
        for i, scale in enumerate((SCALE, 1.0)):
            ins = v.scalar_tensor_tensor(out=tiles(parts[s][:, 2 * i + 1, :]), in0=rotated(s, i), scalar=scale,
                                         in1=tiles(parts[s][:, 2 * i, :]), op0=ALU.mult, op1=ALU.subtract)
        ins.then_inc(lo_ready, 1)

    def write(act, gi, j):
        b, c, s = j // NC, j % NC, j % 4
        act.wait_ge(lo_ready, gi * NJ + (j + 2 + LEAD))
        act.dma_start(K.qkscr[bass.ds(gi + b * G, 1), :, :, c * CH:c * CH + CH].rearrange("o p k c -> (o p) k c"),
                      parts[s][:]).then_inc(qk_wr[s], DMA)

    with nc.Block() as block:

        @block.sync
        def _(sp):
            for i in range(P // (DH // 2)):
                sp.dma_start(freq[32 * i:32 * i + 32, :], io["freqs"].rearrange("(p o) -> p o", o=1)).then_inc(fr_in, DMA)
            sp.dma_start(bp[:], io["bias_p"]).then_inc(bp_in, DMA)
            sp.dma_start(ba[:], io["bias_a"]).then_inc(bp_in, DMA)
            sp.dma_start(wv[:], io["wv"]).then_inc(wv_in, DMA)
            for r in range(2):
                sp.dma_start(wqk[r][:], io["wqk"][r]).then_inc(wqk_in[r], DMA)
            sp.wait_ge(f_ready, 1)
            sp.dma_start(K.fscr, dist[:]).then_inc(f_wr, DMA)
            for t in range(NT):
                sp.wait_ge(vhi, 2 * t + 2)
                sp.wait_ge(vlo, 2 * t + 2)
                sp.dma_start(K.vscr[t], vt[t % 4][:].rearrange("p h a d -> p h (a d)")).then_inc(v_wr[t % 4], DMA)
            for s in range(4):
                sp.wait_ge(v_wr[s], DMA * NT // 4)
            sp.wait_ge(f_wr, DMA)
            with sp.Fori(0, G // 2 - 1) as gh:
                for r in range(2):
                    sp.wait_ge(qk_ready, gh * (2 * NJ) + (r + 1) * NJ)
                    sp.dma_start(wqk[r][:], io["wqk"][bass.ds(gh * 2 + (r + 2), 1)].rearrange("o p k m -> (o p) k m")).then_inc(wqk_in[r], DMA)

        @block.gpsimd
        def _(g):
            g.iota(posi[:], pattern=[[1, S]], base=0, channel_multiplier=0).then_inc(pos_i, 1)
            g.iota(disti[:], pattern=[[1, FLEN]], base=-(S - 1), channel_multiplier=0).then_inc(pos_i, 1)
            g.memset(half_pi[:], math.pi / 2).then_inc(pos_i, 1)
            g.memset(one_col[:], 1.0).then_inc(pos_i, 1)
            for t in range(NT):
                g.indirect_dma_start(out=K.MOE[:, t, :], out_offset=None, in_=K.eout,
                                     in_offset=bass.IndirectOffsetOnAxis(K.gather_idx[:, t:t + 1], 0),
                                     bounds_check=E * CAP - 1, oob_is_err=False).then_inc(gath, DMA)
            g.wait_ge(gath, DMA * NT)
            g.tensor_tensor(K.MOE[:], K.MOE[:], last_axis(K.coef_moe[:], D), ALU.mult).then_inc(mixed, 1)
            g.wait_ge(mixed, 1)
            g.tensor_tensor(K.G0[:], K.G0[:], K.MOE[:], ALU.add).then_inc(mix_ready, 1)
            with g.Fori(0, G) as gi:
                for j, b, c in jobs():
                    r = j % 4
                    g.wait_ge(pair, gi * NJ + (j + 3))
                    g.tensor_tensor(t1[r][:], t1[r][:], t2[r][:], ALU.add).then_inc(summed, 1)

        @block.vector
        def _(v):
            ch = Chain(v, own)
            v.wait_ge(pos_i, 4)
            v.wait_ge(fr_in, 4 * DMA)
            ch.link(v.tensor_copy(pos[:], posi[:]))
            ch.link(v.tensor_scalar(ang[:], pos[:], freq[:, 0:1], None, ALU.mult))
            ch.link(v.tensor_scalar(tn[:], ang[:], 1.0 / (2.0 * math.pi), MAGIC, ALU.mult, ALU.add))
            ch.link(v.tensor_scalar(tn[:], tn[:], MAGIC, None, ALU.subtract))
            for part in (TWO_PI_1, TWO_PI_2, TWO_PI_3):
                ch.link(v.scalar_tensor_tensor(out=ang[:], in0=tn[:], scalar=-part, in1=ang[:],
                                               op0=ALU.mult, op1=ALU.add))
            ch.link(v.tensor_scalar(ang[:], ang[:], 3.1415925, -3.1415925, ALU.min, ALU.max))
            v.scalar_tensor_tensor(out=tn[:], in0=ang[:], scalar=-1.0, in1=ang[:], op0=ALU.mult, op1=ALU.max).then_inc(sin_arg, 1)
            v.wait_ge(bp_in, 2 * DMA)
            ch.link(v.tensor_copy(dist[:], disti[:]))
            ch.link(v.scalar_tensor_tensor(out=dist[:], in0=dist[:], scalar=-1.0, in1=dist[:], op0=ALU.mult, op1=ALU.max))
            ch.link(v.tensor_scalar(ba[:], ba[:], 0.01, None, ALU.max))
            v.tensor_scalar(bp[:], bp[:], 0.01, -1.0, ALU.max, ALU.mult).then_inc(ln_arg, 1)
            v.wait_ge(ln_out, 1)
            v.wait_ge(ln_arg, 1)
            v.tensor_scalar(dist[:], dist[:], bp[:, 0:1], None, ALU.mult).then_inc(f_ready, 1)
            v.wait_ge(sin_out, 2)
            for h in range(2):
                v.tensor_scalar(SIN[h * DH:h * DH + DH // 2, :], SIN[h * DH:h * DH + DH // 2, :], -1.0, None,
                                ALU.mult).then_inc(tab_neg, 1)
            for t in range(NT):
                for c in range(2):
                    n = 2 * t + c
                    v.wait_ge(vhi, n + 1)
                    hs = slice(c * H // 2, c * H // 2 + H // 2)
                    v.tensor_tensor(vt[t % 4][:, hs, 1, :],
                                    pp[n // 4 % 2][:, n % 4, :].rearrange("p (h d) -> p h d", d=DH),
                                    vt[t % 4][:, hs, 0, :], ALU.subtract).then_inc(vlo, 1)
            v.wait_ge(vlo, 2 * NT)
            v.wait_ge(tab_neg, 2)
            for _ in range(2):
                v.nop().then_inc(pair, 1)
            v.nop().then_inc(lo_ready, LEAD + 1)

            def step(gi, u, there):
                if there(u + LEAD):
                    rope(v, gi, u + LEAD)
                if there(u):
                    lo_part(v, gi, u)

            run_jobs(v, step)

        @block.scalar
        def _(act):
            act.wait_ge(sin_arg, 1)
            act.activation(SIN[:], ang[:], ACT.Sin).then_inc(sin_out, 1)
            act.activation(COS[:], tn[:], ACT.Sin, bias=half_pi[:, 0:1], scale=-1.0).then_inc(sin_out, 1)
            act.wait_ge(ln_arg, 1)
            act.activation(dist[:], dist[:], ACT.Ln, bias=one_col[0:H, 0:1], scale=ba[:, 0:1]).then_inc(ln_out, 1)
            for t in range(NT):
                if t >= 4:
                    act.wait_ge(v_wr[t % 4], DMA * (t // 4))
                for c in range(2):
                    n = 2 * t + c
                    act.wait_ge(v_ready, n + 1)
                    act.copy(vt[t % 4][:, c * H // 2:c * H // 2 + H // 2, 0, :],
                             pp[n // 4 % 2][:, n % 4, :].rearrange("p (h d) -> p h d", d=DH)).then_inc(vhi, 1)
            act.wait_ge(mix_ready, 1)
            act.activation(K.G0[:], K.G0[:], ACT.Silu).then_inc(g0_ready, 1)
            for s in range(4):
                act.nop().then_inc(qk_wr[s], 1)

            def step(gi, u, there):
                if there(u + LEAD):
                    hi_part(act, gi, u + LEAD)
                if there(u):
                    write(act, gi, u)

            run_jobs(act, step)
            for s in range(4):
                act.wait_ge(qk_wr[s], G * (DMA * NJ // 4) + 1)

        @block.tensor
        def _(pe):
            pe.wait_ge(wv_in, DMA)
            for t in range(NT):
                for c in range(2):
                    n = 2 * t + c
                    if n >= 8:
                        pe.wait_ge(vlo, n - 7)
                    pe.matmul(pp[n // 4 % 2][:, n % 4, :], XNT[:, t * P:t * P + P], wv[:, c * CH:c * CH + CH],
                              start=True, stop=True).then_inc(v_ready, 1)
            with pe.Fori(0, G // 2) as gh:
                for r in range(2):
                    pe.wait_ge(wqk_in[r], gh * DMA + DMA)
                    for j, b, c in jobs():
                        s = j % 2
                        pe.wait_ge(pair, gh * (2 * NJ) + (r * NJ + j + 1))
                        for i in range(4):
                            mm = pe.matmul(pp[s][:, i, :], wqk[r][:, i, :],
                                           XNT[:, b * S + c * CH:b * S + c * CH + CH], start=True, stop=True)
                        mm.then_inc(qk_ready, 1)


def attend(nc, K, io, sb, ps, sem):
    qk_in, kl_in, tab_in, v_in, wo_in = [[sem(f"{n}_in{s}") for s in range(2)] for n in ("aq", "ak", "at", "av", "aw")]
    s_ready, biased, exped = sem("s_ready"), sem("biased"), sem("exped")
    turned, turn_out, lo_ready = sem("turned"), sem("turn_out"), sem("p_lo_ready")
    pv_ready, ot_ready, op_ready, added, zeroed = sem("pv_ready"), sem("ot_ready"), sem("op_ready"), sem("added"), sem("acc_zeroed")
    recip = sem("recip")

    QS = [sb(f"q_hi_lo{s}", [P, S], BF16) for s in range(2)]
    KS = [sb(f"k_hi_hi{s}", [P, S], BF16) for s in range(2)]
    QX = [sb(f"q_lo_hi{s}", [P, S], BF16) for s in range(2)]
    KL = [sb(f"k_lo_lo{s}", [P, S], BF16) for s in range(2)]
    VV = [sb(f"v_hi_lo{s}", [P, BT, 2 * DH], BF16) for s in range(2)]
    TB = [sb(f"bias_tab{s}", [P, TAB]) for s in range(2)]
    WO = [sb(f"wo{s}", [P, P]) for s in range(2)]
    SB = [sb(f"scores{i}", [P, S]) for i in range(2)]
    PR = [sb(f"probs{i}", [P, S]) for i in range(2)]
    PT = sb("probs_t", [P, 2 * BT, BT, P])
    LO = sb("probs_t_lo", [P, 2 * BT, BT, P], BF16)
    OT = [sb(f"out_t{i}", [P, CH]) for i in range(2)]
    neg_max, row_sum = sb("neg_max", [P, 16]), sb("row_sum", [P, 16])
    inv = sb("inv_sum", [P, 16])
    gate = sb("wait_holder", [P, 2])
    sp_ = [ps(f"score_ps{i}", [P, S]) for i in range(2)]
    tp = [ps(f"turn_ps{i}", [P, 4, P]) for i in range(2)]
    ov = [ps(f"pv_ps{i}", [P, 4, P]) for i in range(2)]
    PTB = PT[:].bitcast(BF16)

    NI = B * G
    U = 2 * BT
    LS, LE, LT = 11, 10, 9
    V_STEPS, OUT_STEP, PROJ_STEP = 6, 6, 7

    def run(eng, step):
        for u in range(-LS, 0):
            step(0, u, lambda x: 0 <= x < U)
        with eng.Fori(0, NI - 1) as it:
            for u in range(U):
                step(it, u, lambda x: True)
        for u in range(U):
            step(NI - 1, u, lambda x: x < U)

    def at(it, n, add):
        return it * n + add

    with nc.Block() as block:

        @block.sync
        def _(sp):
            def load(ix, s):
                q = K.qkscr[bass.ds(ix, 1)].rearrange("o p k c -> (o p) k c")
                rows = slice(s * DH, s * DH + DH)
                sp.dma_start(QS[s][0:DH, :], q[rows, 0, :]).then_inc(qk_in[s], DMA)
                sp.dma_start(QS[s][DH:P, :], q[rows, 1, :]).then_inc(qk_in[s], DMA)
                sp.dma_start(QX[s][0:DH, :], q[rows, 1, :]).then_inc(qk_in[s], DMA)
                sp.dma_start(QX[s][DH:P, :], q[rows, 0, :]).then_inc(qk_in[s], DMA)
                sp.dma_start(KS[s][0:DH, :], q[rows, 2, :]).then_inc(qk_in[s], DMA)
                sp.dma_start(KS[s][DH:P, :], q[rows, 2, :]).then_inc(qk_in[s], DMA)
                sp.dma_start(KL[s][0:DH, :], q[rows, 3, :]).then_inc(kl_in[s], DMA)
                sp.dma_start(KL[s][DH:P, :], q[rows, 3, :]).then_inc(kl_in[s], DMA)
                tab = bass.AP(tensor=K.fscr.tensor, offset=((ix % G) * 2 + s) * FLEN, ap=[[1, P], [1, TAB]])
                sp.dma_start(TB[s][:], tab).then_inc(tab_in[s], DMA)

            def load_v(ix, s):
                row = H * 2 * DH
                v = bass.AP(tensor=K.vscr.tensor, offset=(ix // G) * (BT * P * row) + ((ix % G) * 2 + s) * (2 * DH),
                            ap=[[row, P], [P * row, BT], [1, 2 * DH]])
                sp.dma_start(VV[s][:], v).then_inc(v_in[s], DMA)
                sp.dma_start(WO[s][:], io["wo2"][bass.ds((ix % G) * 2 + s, 1)].rearrange("o p m -> (o p) m")).then_inc(wo_in[s], DMA)

            for s in range(2):
                load(0, s)
                load_v(0, s)
            with sp.Fori(0, NI - 1) as it:
                for s in range(2):
                    sp.wait_ge(s_ready, at(it, U, BT * (s + 1)))
                    sp.wait_ge(biased, at(it, U, BT * (s + 1)))
                    load(it + 1, s)
                    sp.wait_ge(op_ready, at(it, 4, 2 * (s + 1)))
                    load_v(it + 1, s)

        @block.tensor
        def _(pe):
            def scores(it, n):
                s, t, k = n // BT % 2, n % BT, n // U
                if t == 0:
                    pe.wait_ge(qk_in[s], at(it, 6 * DMA, 6 * DMA * (k + 1)))
                    pe.wait_ge(kl_in[s], at(it, 2 * DMA, 2 * DMA * (k + 1)))
                if not (isinstance(it, int) and it == 0 and n < 2):
                    pe.wait_ge(biased, at(it, U, n - 1))
                o, q = sp_[n % 2], slice(t * P, t * P + P)
                cs = [slice(c * CH, c * CH + CH) for c in range(2)]
                for c in range(2):
                    pe.matmul(o[:, cs[c]], (QS, QX)[c][s][:, q], KS[s][:, cs[c]], start=True, stop=False)
                for c in range(2):
                    rows = slice(c * DH, c * DH + DH)
                    mm = pe.matmul(o[:, cs[c]], (QS, QX)[c][s][rows, q], KL[s][rows, cs[c]], start=False, stop=True)
                mm.then_inc(s_ready, 1)

            def turn(it, n):
                pe.wait_ge(exped, at(it, U, n + 1))
                for half in range(2):
                    w = 2 * n + half
                    if not (isinstance(it, int) and it == 0 and w < 2):
                        pe.wait_ge(turn_out, at(it, 2 * U, w - 1))
                    for k in range(4):
                        mm = pe.transpose(tp[half][:, k, :], PR[n % 2][:, (4 * half + k) * P:(4 * half + k + 1) * P],
                                          K.ident[:])
                    mm.then_inc(turned, 1)

            def by_v(it, h, j):
                if j == 0:
                    pe.wait_ge(v_in[h], at(it, DMA, DMA))
                    pe.wait_ge(lo_ready, at(it, U, BT * (h + 1)))
                    pe.wait_ge(added, at(it, 16, BT * h + 1))
                units = [(k, part) for k in range(BT) for part in range(3)]
                n = len(units) // V_STEPS
                for k, part in units[j * n:j * n + n]:
                    for c in ((0,), (1,), (0, 1))[part]:
                        r = BT * h + 4 * c
                        if part < 2:
                            mm = pe.matmul(ov[c][:], VV[h][:, k, :], PTB[:, r:r + 4, k, 1::2], start=(k == 0),
                                           stop=False, skip_group_check=True)
                        else:
                            mm = pe.matmul(ov[c][c * DH:c * DH + DH], VV[h][:, k, 0:DH], LO[:, r:r + 4, k, :],
                                           start=False, stop=(k == BT - 1), skip_group_check=True)
                if j == V_STEPS - 1:
                    mm.then_inc(pv_ready, 1)

            def out(it, h):
                pe.wait_ge(wo_in[h], at(it, DMA, DMA))
                for c in range(2):
                    pe.wait_ge(ot_ready, at(it, 4, 2 * h + c + 1))
                    for k in range(4):
                        mm = pe.matmul(ov[c][:, k, :], OT[c][:, k * P:k * P + P], WO[h][:], start=True, stop=True)
                    mm.then_inc(op_ready, 1)

            def step(it, u, there):
                h, j = u // BT, u % BT
                if there(u + LS):
                    scores(it, u + LS)
                if there(u) and j == PROJ_STEP:
                    out(it, h)
                if there(u + LT):
                    turn(it, u + LT)
                if there(u) and j < V_STEPS:
                    by_v(it, h, j)

            run(pe, step)

        @block.vector
        def _(v):
            def bias_max(it, n):
                s, t = n // BT % 2, n % BT
                v.wait_ge(s_ready, at(it, U, n + 1))
                if t == 0:
                    v.wait_ge(tab_in[s], at(it, DMA, DMA * (n // U + 1)))
                if not (isinstance(it, int) and it == 0 and n < 2):
                    v.wait_ge(exped, at(it, U, n - 1))
                j = TAB - S - t * P
                v.memset(gate[:, n % 2:n % 2 + 1], 0.0)
                v.tensor_tensor_reduce(SB[n % 2][:], sp_[n % 2][:], TB[s][:, j:j + S], -1.0, 3.0e38,
                                       ALU.add, ALU.min, neg_max[:, n % 16:n % 16 + 1]).then_inc(biased, 1)

            def invert(it, h):
                v.wait_ge(exped, at(it, U, BT * (h + 1)))
                v.wait_ge(added, at(it, 16, BT * h + 1))
                v.reciprocal(inv[:, BT * h:BT * h + BT], row_sum[:, BT * h:BT * h + BT]).then_inc(recip, 1)

            def take_out(it, h):
                v.wait_ge(pv_ready, at(it, 2, h + 1))
                for c in range(2):
                    v.tensor_copy(OT[c][:], ov[c][:].rearrange("p t q -> p (t q)")).then_inc(ot_ready, 1)

            def add_share(it, h):
                v.wait_ge(recip, at(it, 2, h + 1))
                for t in range(BT):
                    if t % 4 == 0:
                        v.wait_ge(op_ready, at(it, 4, 2 * h + t // 4 + 1))
                    row = (it // G) * BT + t
                    if not isinstance(row, int):
                        acc = K.SACC[:, bass.ds(row, 1), :].rearrange("p o d -> p (o d)")
                    else:
                        acc = K.SACC[:, row, :]
                    v.scalar_tensor_tensor(out=acc, in0=ov[t // 4][:, t % 4, :], scalar=inv[:, BT * h + t:BT * h + t + 1],
                                           in1=acc, op0=ALU.mult, op1=ALU.add).then_inc(added, 1)

            def step(it, u, there):
                h, j = u // BT, u % BT
                if there(u) and j == OUT_STEP:
                    take_out(it, h)
                if there(u + LS):
                    bias_max(it, u + LS)
                if there(u) and j == V_STEPS - 1:
                    invert(it, h)
                if there(u) and j == PROJ_STEP:
                    add_share(it, h)

            v.memset(K.SACC[:], 0.0).then_inc(zeroed, 1)
            v.wait_ge(zeroed, 1)
            v.nop().then_inc(added, 1)
            run(v, step)

        @block.scalar
        def _(act):
            def exp(it, n):
                act.wait_ge(biased, at(it, U, n + 1))
                if not (isinstance(it, int) and it == 0 and n < 2):
                    act.wait_ge(turned, at(it, 2 * U, 2 * (n - 1)))
                m = n % 16
                if n % BT == 0 and not (isinstance(it, int) and it == 0 and n < U):
                    act.wait_ge(recip, at(it, 2, n // BT - 1))
                act.activation(PR[n % 2][:], SB[n % 2][:], ACT.Exp, bias=neg_max[:, m:m + 1], scale=-1.0,
                               accum_out=row_sum[:, m:m + 1]).then_inc(exped, 1)

            def untile(it, n):
                if n % BT == 0 and not (isinstance(it, int) and it == 0 and n < U):
                    act.wait_ge(pv_ready, at(it, 2, n // BT - 1))
                for half in range(2):
                    act.wait_ge(turned, at(it, 2 * U, 2 * n + half + 1))
                    act.copy(PT[:, n % U, 4 * half:4 * half + 4, :], tp[half][:]).then_inc(turn_out, 1)

            def step(it, u, there):
                if there(u + LE):
                    exp(it, u + LE)
                if there(u + LT):
                    untile(it, u + LT)

            run(act, step)

        @block.gpsimd
        def _(g):
            def low(it, n):
                r = n % U
                g.wait_ge(turn_out, at(it, 2 * U, 2 * n + 2))
                g.tensor_tensor(LO[:, r, :, :], PT[:, r, :, :], PTB[:, r, :, 1::2], ALU.subtract).then_inc(lo_ready, 1)

            def step(it, u, there):
                if there(u + LT):
                    low(it, u + LT)

            run(g, step)


def recur(nc, K, io, sb, ps, sem):
    x_in = [sem(f"x_again_in{b}") for b in range(B)]
    w_in, dec_in, base_ready = sem("rw_in"), sem("dec_in"), sem("base_ready")
    var_ready, rstd_ready, half_ready = sem("var1_ready"), sem("rstd1_ready"), sem("half1_ready")
    xn_ready, made, act_out, kv_read = sem("xn1_ready"), sem("made"), sem("act_out"), sem("kv_read")
    scanned, weighed, weighed_used, s1_ready, s1_out = (sem("scanned"), sem("weighed"), sem("weighed_used"),
                                                        sem("s1_ready"), sem("s1_out"))
    own, flip_ready, flipped, flip_read = sem("recur_dve"), sem("flip_ready"), sem("flipped"), sem("flip_read")

    st = NormStats(sb, "ln1")
    neg_half = sb("neg_half1", [P, NT])
    big = sb("ln1_tmp", [P, NT, D])
    wq, wk = sb("q_w", [P, P]), sb("k_w", [P, P])
    wv, wo = sb("v_w_rep", [P, 8, P]), sb("o_w_rep", [P, 8, P])
    c1w, c2w = sb("cs_w1", [P, D // 4]), sb("cs_w2_rep", [D // 4, P])
    c1b, c2b = sb("cs_b1", [D // 4, 1]), sb("cs_b2_rep", [P, 1])
    base = sb("decay_base", [P, 1])
    QT, KT = sb("q_t", [P, 2, S]), sb("k_t", [P, 2, S])
    C1, LAM = sb("cs_hidden", [D // 4, S]), sb("lam", [P, 2, S])
    KV, SC, WT = sb("kv", [P, 2, S]), sb("state", [P, 2, S]), sb("q_state", [P, 2, S])
    pj = [ps(f"made_ps{i}", [P, S]) for i in range(2)]
    so = ps("s1_ps", [P, BT, P])
    fs = ps("s0_ps", [P, BT, P])
    flip = sb("flip", [P, P])
    FE = 8
    X, XN, X1, XNT = K.X, K.XN, K.X, K.XNT

    with nc.Block() as block:

        @block.sync
        def _(sp):
            for b in range(B):
                sp.dma_start(X[:, b * BT:b * BT + BT, :],
                             io["x"][b].rearrange("(t p) d -> p t d", p=P)).then_inc(x_in[b], DMA)
            for dst, src in ((wq[:], io["q_w"]), (wk[:], io["k_w"]), (wv[:], io["v_w"]), (wo[:], io["o_w"]), (c1w[:], io["cs_w1"]),
                             (c2w[:], io["cs_w2"]), (c1b[:], io["cs_b1"]), (c2b[:], io["cs_b2"])):
                sp.dma_start(dst, src).then_inc(w_in, DMA)
            sp.dma_start(base[:], io["decay"]).then_inc(dec_in, DMA)


        @block.vector
        def _(v):
            ch = Chain(v, own)

            def join(b):
                n = slice(b * BT, b * BT + BT)
                v.wait_ge(flipped, b + 1)
                v.wait_ge(x_in[b], DMA)
                ch.link(v.tensor_tensor(big[:, n, :], fs[:], K.G0[:, n, :], ALU.mult))
                v.nop().then_inc(flip_read, 1)
                ch.link(v.tensor_tensor(X1[:, n, :], X[:, n, :], big[:, n, :], ALU.add))
                row_stats(v, ch, X1, st, b, 1e-5, var_ready)
                apply_norm(v, ch, X1, XN, st, b, rstd_ready, b + 1)
                v.nop().then_inc(xn_ready, 1)

            def scans(b):
                lam = LAM[:, b % 2, :]
                v.wait_ge(act_out, 5 * b + 5)
                v.wait_ge(base_ready, 1)
                ch.link(v.tensor_scalar(lam, lam, 0.2, 1.0, ALU.mult, ALU.add))
                ch.link(v.tensor_scalar(lam, lam, base[:, 0:1], 0.0, ALU.mult, ALU.max))
                ch.link(v.tensor_scalar(lam, lam, 0.9995, None, ALU.min))
                for f in range(FE):
                    n = b * FE + f
                    v.wait_ge(made, 13 * b + 5 + f + 1)
                    if n >= 2:
                        v.wait_ge(scanned, n - 1)
                    v.tensor_tensor(KV[:, n % 2, :], pj[(13 * b + 5 + f) % 2][:], KT[:, b % 2, :],
                                    ALU.mult).then_inc(kv_read, 1)
                    v.wait_ge(kv_read, n + 1)
                    if n >= 2:
                        v.wait_ge(weighed, n - 1)
                    v.tensor_tensor_scan(SC[:, n % 2, :], lam, KV[:, n % 2, :], 0.0, ALU.mult,
                                         ALU.add).then_inc(scanned, 1)

            join(0)
            for b in range(B):
                if b + 1 < B:
                    join(b + 1)
                scans(b)

        @block.gpsimd
        def _(g):
            g.memset(neg_half[:], -0.5).then_inc(half_ready, 1)
            g.wait_ge(half_ready, 1)

            g.memset(flip[:], 0.0).then_inc(half_ready, 1)
            g.wait_ge(half_ready, 2)
            g.affine_select(out=flip[:], in_=flip[:], compare_op=ALU.not_equal, fill=1.0, base=1 - P,
                            pattern=[[1, P]], channel_multiplier=1).then_inc(flip_ready, 1)

            def rstd(b):
                n = slice(b * BT, b * BT + BT)
                g.wait_ge(var_ready, b + 1)
                g.tensor_tensor(st.rstd[:, n], st.var[:, n], neg_half[:, n], ALU.pow).then_inc(rstd_ready, 1)

            rstd(0)
            for b in range(B):
                if b + 1 < B:
                    rstd(b + 1)
                for f in range(FE):
                    n = b * FE + f
                    g.wait_ge(scanned, n + 1)
                    if n >= 2:
                        g.wait_ge(weighed_used, n - 1)
                    g.tensor_tensor(WT[:, n % 2, :], SC[:, n % 2, :], QT[:, b % 2, :], ALU.mult).then_inc(weighed, 1)

        @block.scalar
        def _(act):
            act.wait_ge(dec_in, DMA)
            act.wait_ge(w_in, 8 * DMA)
            act.activation(base[:], base[:], ACT.Sigmoid).then_inc(base_ready, 1)
            for b in range(B):
                for i in range(5):
                    act.wait_ge(made, 13 * b + i + 1)
                    src = pj[(13 * b + i) % 2]
                    if b >= 2 and i == 1:
                        act.wait_ge(weighed, FE * (b - 1))
                        act.wait_ge(scanned, FE * (b - 1))
                    if i == 0:
                        ins = act.copy(XNT[:, b * S:b * S + S], src[:])
                    elif i == 1:
                        ins = act.copy(QT[:, b % 2, :], src[:])
                    elif i == 2:
                        ins = act.copy(KT[:, b % 2, :], src[:])
                    elif i == 3:
                        ins = act.activation(C1[:], src[0:D // 4, :], ACT.Tanh, bias=c1b[:, 0:1])
                    else:
                        ins = act.activation(LAM[:, b % 2, :], src[:], ACT.Sigmoid, bias=c2b[:, 0:1])
                    ins.then_inc(act_out, 1)
                act.wait_ge(s1_ready, b + 1)
                act.copy(K.S1[:, b * BT:b * BT + BT, :], so[:]).then_inc(s1_out, 1)

        @block.tensor
        def _(pe):
            pe.wait_ge(w_in, 8 * DMA)

            def halves(dst, lhs, src, m=P):
                for c in range(S // CH):
                    mm = pe.matmul(dst[0:m, c * CH:c * CH + CH], lhs, src[:, c * CH:c * CH + CH], start=True, stop=True)
                mm.then_inc(made, 1)

            def share(b, f):
                n = b * FE + f
                pe.wait_ge(weighed, n + 1)
                if f == 0 and b >= 1:
                    pe.wait_ge(s1_out, b)
                for t in range(BT):
                    mm = pe.matmul(so[:, t, :], WT[:, n % 2, t * P:t * P + P], wo[:, f, :],
                                   start=(f == 0 and t % 4 == 0), stop=(f == FE - 1), skip_group_check=True)
                mm.then_inc(weighed_used, 1)
                if f == FE - 1:
                    pe.wait_ge(weighed_used, n + 1)
                    pe.nop().then_inc(s1_ready, 1)

            def unflip(b):
                if b >= 1:
                    pe.wait_ge(flip_read, b)
                for t in range(BT):
                    mm = pe.matmul(fs[:, t, :], flip[:], K.SACC[:, b * BT + t, :], start=True, stop=True)
                mm.then_inc(flipped, 1)

            pe.wait_ge(flip_ready, 1)
            unflip(0)
            for b in range(B):
                if b + 1 < B:
                    unflip(b + 1)
                pe.wait_ge(xn_ready, b + 1)
                if b >= 1:
                    pe.wait_ge(kv_read, FE * b)
                dst = pj[13 * b % 2]
                for t in range(BT):
                    mm = pe.transpose(dst[:, t * P:t * P + P], XN[:, b * BT + t, :], K.ident[:])
                mm.then_inc(made, 1)
                pe.wait_ge(act_out, 5 * b + 1)
                x = XNT[:, b * S:b * S + S]
                halves(pj[(13 * b + 1) % 2], wq[:], x)
                halves(pj[(13 * b + 2) % 2], wk[:], x)
                pe.wait_ge(act_out, 5 * b + 2)
                halves(pj[(13 * b + 3) % 2], c1w[:], x, D // 4)
                pe.wait_ge(act_out, 5 * b + 4)
                halves(pj[(13 * b + 4) % 2], c2w[:], C1[:])
                for f in range(FE):
                    if f == 1:
                        pe.wait_ge(act_out, 5 * b + 5)
                    if f >= 2:
                        pe.wait_ge(kv_read, FE * b + f - 1)
                    halves(pj[(13 * b + 5 + f) % 2], wv[:, f, :], x)
                    if f >= 2:
                        share(b, f - 2)
                share(b, FE - 2)
                share(b, FE - 1)


def finish(nc, K, io, sb, ps, sem):
    w_in, b_in, iota_ready = sem("fw_in"), sem("fb_in"), sem("iota1_ready")
    z_ready, z_out, max_sub, exp_ready, zm_ready = sem("z_ready"), sem("z_out"), sem("max1_sub"), sem("exp1_ready"), sem("zm_ready")
    zt_ready, zt_out, h_ready, h_out, o_ready, y_ready = (sem("zt_ready"), sem("zt_out"), sem("fh_ready"),
                                                          sem("fh_out"), sem("fo_ready"), sem("y_ready"))
    g1_ready, mixed, x2_ready, out_wr, own = sem("g1_ready"), sem("mixed"), sem("x2_ready"), sem("out_wr"), sem("fin_dve")
    ER = E * R
    NZ = E + ER
    wz = sb("gate_lora_a", [P, NZ])
    lb = sb("lora_b", [ER, F])
    wi, wo = sb("wi", [P, F]), sb("wo_t", [P, FT, D])
    wib, gb, wob = sb("wi_b", [P, FT]), sb("gate_b", [P, E]), sb("wo_b", [P, D])
    ZL, ZM = sb("z_rows", [P, NT, NZ]), sb("z_masked", [P, NT, ER])
    ZT = sb("z_t", [ER, B * S])
    io8, r1, hot, col = sb("iota8_1", [P, NT, E]), sb("route1_1", [P, NT, E]), sb("onehot1", [P, NT, E]), sb("cols1", [P, 2, NT])
    hT = [sb(f"fhid{i}", [P, FT, CH]) for i in range(2)]
    Y = [sb(f"y{i}", [P, 4, D]) for i in range(2)]
    ZB = 12
    pb = [ps(f"fin_ps{i}", [P, CH]) for i in range(8)]
    NJ = NT // 4

    with nc.Block() as block:

        @block.sync
        def _(sp):
            for dst, src in ((wz[:], io["wz"]), (lb[:], io["lora_b"]), (wi[:], io["wi"]),
                             (wo[:], io["wo_t"].rearrange("(i p) d -> p i d", p=P))):
                sp.dma_start(dst, src).then_inc(w_in, DMA)
            for dst, src in ((wib[:], io["wi_b"]), (gb[:], io["gate_b"].partition_broadcast(P)),
                             (wob[:], io["wo_b"].partition_broadcast(P))):
                sp.dma_start(dst, src).then_inc(b_in, DMA)
            for j in range(NJ):
                sp.wait_ge(x2_ready, j + 1)
                b, t = j // 2, 4 * (j % 2)
                sp.dma_start(io["out"][b].rearrange("(t p) d -> p t d", p=P)[:, t:t + 4, :],
                             K.X[:, 4 * j:4 * j + 4, :]).then_inc(out_wr, DMA)
            sp.wait_ge(out_wr, DMA * NJ)

        @block.gpsimd
        def _(g):
            g.iota(io8[:], pattern=[[0, NT], [1, E]], base=0, channel_multiplier=0,
                   allow_small_or_imprecise_dtypes=True).then_inc(iota_ready, 1)
            for j in range(NJ):
                g.wait_ge(mixed, j + 1)
                n = slice(4 * j, 4 * j + 4)
                g.tensor_tensor(K.X[:, n, :], K.X[:, n, :], K.S1[:, n, :], ALU.add).then_inc(x2_ready, 1)

        @block.tensor
        def _(pe):
            pe.wait_ge(w_in, 4 * DMA)
            for t in range(NT):
                k = t % ZB * NZ
                mm = pe.matmul(pb[t // ZB][:, k:k + NZ], K.XNT[:, t * P:t * P + P], wz[:], start=True, stop=True)
            mm.then_inc(z_ready, 1)
            pe.wait_ge(zm_ready, 1)
            for j in range(NJ):
                for t in range(4):
                    mm = pe.transpose(pb[j][0:ER, t * P:t * P + P], ZM[:, 4 * j + t, :], K.ident[:])
                mm.then_inc(zt_ready, 1)
            pe.wait_ge(zt_out, NJ)

            def hidden(j):
                for i in range(FT):
                    if j >= 1:
                        pe.wait_ge(h_out, FT * (j - 1) + i + 1)
                    pe.matmul(pb[i][:], wi[:, i * P:i * P + P], K.XNT[:, j * CH:j * CH + CH], start=True, stop=False)
                    pe.matmul(pb[i][:], lb[:, i * P:i * P + P], ZT[:, j * CH:j * CH + CH],
                              start=False, stop=True).then_inc(h_ready, 1)

            def out(j):
                s = j % 2
                o = pb[4 + s]
                if j >= 2:
                    pe.wait_ge(y_ready, j - 1)
                for i in range(FT):
                    pe.wait_ge(h_out, FT * j + i + 1)
                    for c in range(4):
                        mm = pe.matmul(o[:, c * P:c * P + P], hT[s][:, i, c * P:c * P + P], wo[:, i, :],
                                       start=(i == 0 and c == 0), stop=(i == FT - 1), skip_group_check=True)
                mm.then_inc(o_ready, 1)

            hidden(0)
            for j in range(NJ):
                if j + 1 < NJ:
                    hidden(j + 1)
                out(j)

        @block.scalar
        def _(act):
            act.wait_ge(max_sub, 1)
            act.activation(ZL[:, :, 0:E], ZL[:, :, 0:E], ACT.Exp).then_inc(exp_ready, 1)
            for j in range(NJ):
                act.wait_ge(zt_ready, j + 1)
                act.copy(ZT[:, j * CH:j * CH + CH], pb[j][0:ER, :]).then_inc(zt_out, 1)
            act.wait_ge(b_in, 3 * DMA)

            def relu(j):
                for i in range(FT):
                    act.wait_ge(h_ready, FT * j + i + 1)
                    if j >= 2 and i == 0:
                        act.wait_ge(o_ready, j - 1)
                    act.activation(hT[j % 2][:, i, :], pb[i][:], ACT.Relu, bias=wib[:, i:i + 1]).then_inc(h_out, 1)

            def gate(j):
                act.wait_ge(y_ready, j + 1)
                act.activation(Y[j % 2][:], Y[j % 2][:], ACT.Silu).then_inc(g1_ready, 1)

            for j in range(NJ):
                relu(j)
                if j >= 1:
                    gate(j - 1)
            gate(NJ - 1)

        @block.vector
        def _(v):
            ch = Chain(v, own)
            v.wait_ge(z_ready, 1)
            for k in range(3):
                n = min(ZB, NT - k * ZB)
                ins = v.tensor_copy(ZL[:, k * ZB:k * ZB + n, :], pb[k][:, 0:n * NZ].rearrange("p (t z) -> p t z", z=NZ))
            ch.link(ins)
            v.wait_ge(b_in, 3 * DMA)
            lg = ZL[:, :, 0:E]
            ch.link(v.tensor_tensor(lg, lg, mid_axis(gb[:], NT), ALU.add))
            ch.link(v.tensor_reduce(col[:, 0, :], lg, AX_X, ALU.max))
            v.tensor_tensor(lg, lg, last_axis(col[:, 0, :], E), ALU.subtract).then_inc(max_sub, 1)
            v.wait_ge(exp_ready, 1)
            v.wait_ge(iota_ready, 1)
            ch.link(v.tensor_scalar(r1[:], lg, 1.0, float(E), ALU.is_lt, ALU.mult))
            ch.link(v.tensor_tensor(r1[:], r1[:], io8[:], ALU.add))
            ch.link(v.tensor_reduce(col[:, 1, :], r1[:], AX_X, ALU.min))
            ch.link(v.tensor_tensor(hot[:], io8[:], last_axis(col[:, 1, :], E), ALU.is_equal))
            for r in range(R):
                ins = v.tensor_tensor(ZM[:].rearrange("p t (e r) -> p t e r", r=R)[:, :, :, r],
                                      ZL[:, :, E:NZ].rearrange("p t (e r) -> p t e r", r=R)[:, :, :, r], hot[:], ALU.mult)
            ins.then_inc(zm_ready, 1)
            for j in range(NJ):
                s, n = j % 2, slice(4 * j, 4 * j + 4)
                v.wait_ge(o_ready, j + 1)
                if j >= 2:
                    v.wait_ge(mixed, j - 1)
                v.tensor_tensor(Y[s][:], pb[4 + s][:].rearrange("p (t d) -> p t d", d=D), mid_axis(wob[:], 4),
                                ALU.add).then_inc(y_ready, 1)
                v.wait_ge(g1_ready, j + 1)
                v.tensor_tensor(K.S1[:, n, :], K.S1[:, n, :], Y[s][:], ALU.mult).then_inc(mixed, 1)


def program(nc, io):
    with ExitStack() as outer:
        def maker(stack):
            def sb(name, shape, dt=F32):
                return stack.enter_context(nc.sbuf_tensor(name, shape, dt))

            def ps(name, shape, dt=F32):
                return stack.enter_context(nc.psum_tensor(name, shape, dt))
            return sb, ps

        def sem(name):
            return outer.enter_context(nc.semaphore(name))

        sb, _ = maker(outer)
        K = Shared()
        K.ident = sb("ident", [P, P])
        K.G0 = sb("g0", [P, NT, D])
        K.disp = nc.dram_tensor("dispatch", [E * CAP, D], F32, kind="Internal").ap()
        K.eout = nc.dram_tensor("expert_rows", [E * CAP, D], F32, kind="Internal").ap()
        K.fscr = nc.dram_tensor("bias_by_distance", [H, FLEN], F32, kind="Internal").ap()
        K.vscr = nc.dram_tensor("v_parts", [NT, P, H, 2 * DH], BF16, kind="Internal").ap()
        K.qkscr = nc.dram_tensor("qk_parts", [B * G, P, 4, S], BF16, kind="Internal").ap()

        def run(block):
            with ExitStack() as own:
                block_sb, block_ps = maker(own)
                block(nc, K, io, block_sb, block_ps, sem)

        with ExitStack() as layer0:
            sb0, _ = maker(layer0)
            K.XNT = sb0("xn_t", [P, B * S])
            K.coef_moe, K.gather_idx = sb0("coef_moe", [P, NT]), sb0("gather_idx", [P, NT], U32)
            with ExitStack() as moe:
                sb_moe, _ = maker(moe)
                K.XN = sb_moe("xn", [P, NT, D])
                K.A, K.AT = sb_moe("a", [P, NT, D]), sb_moe("a_t", [P, B * S])
                K.RES = sb_moe("res_out", [P, NT, D])
                K.w1, K.w2 = [sb_moe(f"w1_{i}", [P, F]) for i in range(RING)], [sb_moe(f"w2_{i}", [P, FT, D]) for i in range(RING)]
                K.dx = [sb_moe(f"dispatched{i}", [P, CAP // P, D]) for i in range(RING)]
                K.w_in, K.d_in = [sem(f"w_in{s}") for s in range(RING)], [sem(f"d_in{s}") for s in range(RING)]
                K.coef_res, K.scatter_idx = sb_moe("coef_res", [P, NT]), sb_moe("scatter_idx", [P, NT], U32)
                with ExitStack() as zeros:
                    K.Z = maker(zeros)[0]("zeros", [P, E * CAP * D // P])
                    run(prepare)
                run(experts)
            K.MOE = sb0("moe_rows", [P, NT, D])
            run(project)
        K.SACC = sb("s0", [P, NT, D])
        run(attend)
        K.X = sb("x1", [P, NT, D])
        K.XN, K.XNT, K.S1 = sb("xn1", [P, NT, D]), sb("xn1_t", [P, B * S]), sb("s1", [P, NT, D])
        run(recur)
        run(finish)


def layouts(inp):
    import numpy as np
    a = {k: np.ascontiguousarray(v) for k, v in inp.items()}
    c = np.ascontiguousarray
    qkv = a["L0_attn_qkv_w"].reshape(3, H, DH, D)

    def pair(w):
        return w.reshape(G, P, D).transpose(0, 2, 1)

    def swapped(w):
        return np.concatenate([w[:, DH // 2:], w[:, :DH // 2]], axis=1)
    wqk = np.stack([pair(qkv[0]), pair(swapped(qkv[0])), pair(qkv[1]), pair(swapped(qkv[1]))], axis=2)
    wo = a["L0_attn_out_w"].reshape(D, H, DH).transpose(1, 2, 0)
    wo2 = np.concatenate([wo, wo], axis=1)
    he = a["L1_attn_v_w"].reshape(H, 8, D)
    vrep = np.repeat(he.transpose(2, 1, 0)[:, :, :, None], 8, axis=3).reshape(D, 8, P)
    ow = a["L1_attn_o_w"].reshape(D, H, 8)
    orep = np.repeat(ow.transpose(1, 2, 0)[:, None], 8, axis=1).reshape(P, 8, D)
    cs2 = np.repeat(a["L1_attn_cs_w2"].T[:, :, None], 8, axis=2).reshape(D // 4, P)
    return dict(
        x=a["L0_attn_x"], wqk=c(wqk), wv=c(a["L0_attn_qkv_w"][2 * H * DH:].T), wo2=c(wo2),
        bias_p=a["L0_attn_bias_p"].reshape(H, 1), bias_a=a["L0_attn_bias_a"].reshape(H, 1), freqs=a["L0_attn_rope_freqs"],
        attn_nw=a["L0_ffn_attn_nw"], attn_nb=a["L0_ffn_attn_nb"], wg=a["L0_ffn_wg"], inter_w=a["L0_ffn_inter_w"],
        inter_b=c(a["L0_ffn_inter_b"].reshape(E, FT, P).transpose(2, 0, 1)), output_w=a["L0_ffn_output_w"], output_b=a["L0_ffn_output_b"],
        res_inter_w=a["L0_ffn_res_inter_w"], res_inter_b=c(a["L0_ffn_res_inter_b"].reshape(FT, P).T),
        res_output_w=a["L0_ffn_res_output_w"], res_output_b=a["L0_ffn_res_output_b"], res_coef=a["L0_ffn_res_coef"],
        q_w=c(a["L1_attn_q_w"].T), k_w=c(a["L1_attn_k_w"].T), v_w=c(vrep), o_w=c(orep), cs_w1=c(a["L1_attn_cs_w1"].T),
        cs_b1=a["L1_attn_cs_b1"].reshape(D // 4, 1), cs_w2=c(cs2),
        cs_b2=c(np.repeat(a["L1_attn_cs_b2"], 8).reshape(P, 1)), decay=a["L1_attn_decay_params"].reshape(P, 1),
        wz=c(np.concatenate([a["L1_ffn_gate_W"].T, a["L1_ffn_lora_A"].reshape(E * R, D).T], axis=1)),
        gate_b=a["L1_ffn_gate_b"], wi=c(a["L1_ffn_wi_W"].T), wi_b=c(a["L1_ffn_wi_b"].reshape(FT, P).T), wo_t=c(a["L1_ffn_wo_W"].T),
        wo_b=a["L1_ffn_wo_b"], lora_b=c(a["L1_ffn_lora_B"].transpose(0, 2, 1).reshape(E * R, F)),
    )


def kernel(**inputs):
    import numpy as np
    import concourse.bacc as bacc
    from concourse.bass_utils import run_bass_kernel_spmd

    nc = bacc.Bacc("TRN2", target_bir_lowering=False, num_devices=1)
    arrays, aps = {}, {}
    for name, a in layouts(inputs).items():
        arrays[f"in_{name}"] = a
        aps[name] = nc.dram_tensor(f"in_{name}", a.shape, mybir.dt.from_np(a.dtype), kind="ExternalInput").ap()
    aps["out"] = nc.dram_tensor("out_0", [B, S, D], F32, kind="ExternalOutput").ap()
    program(nc, aps)
    r = run_bass_kernel_spmd(nc, [arrays], core_ids=[0])
    return r.results[0]["out_0"]
```

```python
from contextlib import ExitStack
import math

import concourse.bass as bass
from concourse import mybir

ALU = mybir.AluOpType
ACT = mybir.ActivationFunctionType
AX_X = mybir.AxisListType.X
F32 = mybir.dt.float32
BF16 = mybir.dt.bfloat16
I32 = mybir.dt.int32
U32 = mybir.dt.uint32

P = 128
B, S, D = 4, 1024, 128
NT = B * S // P
BT = S // P
H, DH = 16, 64
G = H // 2
E, F, R = 8, 512, 4
FT = F // P
CAP = B * S // E
SCALE = 1.0 / math.sqrt(DH)
ER = E * R
NZ = E + ER
NV = BT
RING = 4
DMA = 16
CH = 512
MAGIC = 12582912.0
TWO_PI_1 = 6.28125
TWO_PI_2 = 0.00193500518798828125
TWO_PI_3 = 2.0 * math.pi - TWO_PI_1 - TWO_PI_2
TAB = 2 * S - P
FLEN = 2 * S


class Shared:
    pass


class Chain:

    def __init__(self, eng, sem):
        self.eng, self.sem, self.count = eng, sem, 0

    def link(self, ins):
        self.count += 1
        ins.then_inc(self.sem, 1)
        self.eng.wait_ge(self.sem, self.count)


def last_axis(ap, n):
    return ap.unsqueeze(2).to_broadcast([ap.shape[0], ap.shape[1], n])


def mid_axis(ap, n):
    return ap.unsqueeze(1).to_broadcast([ap.shape[0], n, ap.shape[1]])


def row_stats(v, ch, src, st, b, eps, sem_var):
    for t in range(b * BT, b * BT + BT):
        ins = v.bn_stats(st.six[:, t, :], src[:, t, :])
    ch.link(ins)
    for t in range(b * BT, b * BT + BT):
        ins = v.bn_aggr(st.mean_var[:, t, :], st.six[:, t, :])
    ch.link(ins)
    n = slice(b * BT, b * BT + BT)
    v.tensor_scalar(st.var[:, n], st.mean_var[:, n, 1], eps, None, ALU.add).then_inc(sem_var, 1)


def apply_norm(v, ch, src, dst, st, b, sem_rstd, nth):
    v.wait_ge(sem_rstd, nth)
    for t in range(b * BT, b * BT + BT):
        ins = v.tensor_scalar(dst[:, t, :], src[:, t, :], st.mean_var[:, t, 0:1], st.rstd[:, t:t + 1],
                              ALU.subtract, ALU.mult)
    ch.link(ins)


class NormStats:

    def __init__(self, sb, name):
        self.six = sb(name + "_six", [P, NT, 6])
        self.mean_var = sb(name + "_mean_var", [P, NT, 2])
        self.var, self.rstd = sb(name + "_var", [P, NT]), sb(name + "_rstd", [P, NT])


def prepare(nc, K, io, sb, ps, sem):
    x_in = [sem(f"x_in{b}") for b in range(B)]
    par_in, wg_in, zero_ready, zero_out = sem("par_in"), sem("wg_in"), sem("zero_ready"), sem("zero_out")
    var_ready, rstd_ready, half_ready = sem("var_ready"), sem("rstd_ready"), sem("half_ready")
    xn_ready, a_ready, tr_ready, tr_out = sem("xn_ready"), sem("a_ready"), sem("tr_ready"), sem("tr_out")
    ident_ready, logit_ready, max_sub, exp_ready = sem("ident_ready"), sem("logit_ready"), sem("max_sub"), sem("exp_ready")
    hot_ready, pos_ready, tri_ready, iota_ready = sem("hot_ready"), sem("pos_ready"), sem("tri_ready"), sem("iota_ready")
    dve_own, pool_own = sem("prep_dve"), sem("prep_pool")

    st = [NormStats(sb, "ln0"), NormStats(sb, "ln_moe")]
    neg_half = sb("neg_half", [P, NT])
    gbc, bbc = sb("attn_nw_rows", [P, D]), sb("attn_nb_rows", [P, D])
    wgc = sb("wgc", [P, E + 2])
    tri, ones = sb("tri", [P, P]), sb("ones_sq", [P, P])
    lg = sb("logits0", [P, NT, E + 2])
    r1, r2 = sb("route1", [P, NT, E]), sb("route2", [P, NT, E])
    hot = sb("onehot", [P, NT, E])
    io8 = sb("iota8", [P, NT, E])
    col = sb("route_cols", [P, 12, NT])
    one_row = sb("one_row", [P, NT])
    scatter_idx = sb("scatter_idx", [P, NT], U32)
    ZQ = E * CAP * D // P // 4
    Z = sb("zeros", [P, ZQ])
    w1r, w2r = sb("w1_res", [P, F]), sb("w2_res", [P, FT, D])
    b1r = sb("b1_res_cols", [P, FT])
    hT = [sb(f"res_hidden_t{i}", [P, FT, CH]) for i in range(2)]
    res_in, res_bias_in = sem("res_in"), sem("res_bias_in")
    h_ready, h_out, o_ready, o_out = sem("rh_ready"), sem("rh_out"), sem("ro_ready"), sem("ro_out")
    idx_ready, scat = sem("idx_ready"), sem("scattered")
    tp = [ps(f"prep_t{i}", [P, 2 * CH]) for i in range(2)]
    lps, counts = ps("logit_ps", [P, NT, E + 2]), ps("count_ps", [P, 2, NT, E])
    pre, tot = counts[:, 0], counts[:, 1]
    op = [ps(f"res_out_ps{i}", [P, CH // P, D]) for i in range(2)]
    CT = CH // P
    NR = NT // CT
    X, XN, A, AT = K.XN, K.XN, sb("a", [P, NT, D]), sb("a_t", [P, B * S])
    vt = [sb(f"v_parts_a{i}", [P, H, 2, DH], BF16) for i in range(2)]
    v32 = [hT[0][:, c, :].rearrange("p (h d) -> p h d", d=DH) for c in range(2)]
    va_ready, va_taken, va_hi, va_lo = sem("va_ready"), sem("va_taken"), sem("va_hi"), sem("va_lo")
    va_wr = [sem(f"va_wr{s}") for s in range(2)]

    def v_tiles(n):
        return range(n - 1, n) if n >= 1 else range(0)

    def v_ps(c):
        return op[c][:].rearrange("p t d -> p (t d)").rearrange("p (h d) -> p h d", d=DH)

    def v_heads(c):
        return slice(c * H // 2, c * H // 2 + H // 2)

    COUNT_JOB = 1

    def hidden_ps(i):
        return tp[i // 2][:, i % 2 * CH:i % 2 * CH + CH]

    def take_out(act, j):
        act.wait_ge(o_ready, j + 1)
        act.copy(K.G0[:, j * CT:j * CT + CT, :], op[j % 2][:]).then_inc(o_out, 1)

    norm_order = [(0, 0), (0, 1), (1, 0), (0, 2), (1, 1), (0, 3), (1, 2), (1, 3)]
    norm_done = [[], [(0, 0)], [(0, 1)], [(1, 0)], [(0, 2)], [(1, 1)], [(0, 3)], [(1, 2), (1, 3)]]

    with nc.Block() as block:

        @block.sync
        def _(sp):
            for b in range(B):
                sp.dma_start(X[:, b * BT:b * BT + BT, :],
                             io["x"][b].rearrange("(t p) d -> p t d", p=P)).then_inc(x_in[b], DMA)
            sp.dma_start(gbc[:], io["attn_nw"].partition_broadcast(P)).then_inc(par_in, DMA)
            sp.dma_start(bbc[:], io["attn_nb"].partition_broadcast(P)).then_inc(par_in, DMA)
            sp.dma_start(K.wv[:], io["wv"]).then_inc(K.wv_in, DMA)
            sp.dma_start(wgc[:, 0:E], io["wg"]).then_inc(wg_in, DMA)
            sp.dma_start(wgc[:, E:E + 2], io["res_coef"]).then_inc(wg_in, DMA)
            sp.dma_start(w1r[:], io["res_inter_w"]).then_inc(res_in, DMA)
            sp.dma_start(w2r[:], io["res_output_w"].rearrange("(i p) d -> p i d", p=P)).then_inc(res_in, DMA)
            sp.dma_start(b1r[:], io["res_inter_b"]).then_inc(res_bias_in, DMA)
            sp.wait_ge(zero_ready, 1)
            for q in range(4):
                sp.dma_start(K.disp.rearrange("(p t) d -> p (t d)", p=P)[:, q * ZQ:q * ZQ + ZQ], Z[:]).then_inc(zero_out, DMA)
            for t in range(NV):
                sp.wait_ge(va_hi, 2 * t + 2)
                sp.wait_ge(va_lo, 2 * t + 2)
                sp.dma_start(K.vscr[t], vt[t % 2][:].rearrange("p h a d -> p h (a d)")).then_inc(va_wr[t % 2], DMA)
            for e in range(RING):
                load_expert(sp, K, io, e)
            for s in range(2):
                sp.wait_ge(va_wr[s], DMA * NV // 2)
            sp.wait_ge(scat, DMA * NT)
            for e in range(RING):
                load_rows(sp, K, e)

        @block.gpsimd
        def _(g):
            g.memset(K.ident[:], 0.0).then_inc(pool_own, 1)
            g.memset(neg_half[:], -0.5).then_inc(half_ready, 1)
            g.wait_ge(pool_own, 1)
            g.affine_select(out=K.ident[:], in_=K.ident[:], compare_op=ALU.not_equal, fill=1.0, base=0,
                            pattern=[[-1, P]], channel_multiplier=1).then_inc(ident_ready, 1)
            g.memset(Z[:], 0.0).then_inc(zero_ready, 1)
            g.memset(ones[:], 1.0).then_inc(pool_own, 1)
            g.wait_ge(pool_own, 2)
            g.affine_select(out=tri[:], in_=ones[:], compare_op=ALU.is_gt, fill=0.0, base=0,
                            pattern=[[1, P]], channel_multiplier=-1).then_inc(tri_ready, 1)
            g.memset(one_row[:], 1.0).then_inc(tri_ready, 1)
            g.iota(io8[:], pattern=[[0, NT], [1, E]], base=0, channel_multiplier=0,
                   allow_small_or_imprecise_dtypes=True).then_inc(iota_ready, 1)
            def v_low(t):
                for c in range(2):
                    g.wait_ge(va_hi, 2 * t + c + 1)
                    g.tensor_tensor(vt[t % 2][:, v_heads(c), 1, :], v32[c], vt[t % 2][:, v_heads(c), 0, :],
                                    ALU.subtract).then_inc(va_lo, 1)

            g.wait_ge(half_ready, 1)
            for n, (m, b) in enumerate(norm_order):
                g.wait_ge(var_ready, n + 1)
                k = slice(b * BT, b * BT + BT)
                g.tensor_tensor(st[m].rstd[:, k], st[m].var[:, k], neg_half[:, k], ALU.pow).then_inc(rstd_ready, 1)
                if n >= 3:
                    for t in v_tiles(n - 2):
                        v_low(t)
            for n in range(2 * B - 2, 2 * B + 1):
                for t in v_tiles(n):
                    v_low(t)
            g.wait_ge(a_ready, B)
            g.wait_ge(idx_ready, 1)
            g.wait_ge(zero_out, 4 * DMA)
            for t in range(NT):
                g.indirect_dma_start(out=K.disp, out_offset=bass.IndirectOffsetOnAxis(scatter_idx[:, t:t + 1], 0),
                                     in_=A[:, t, :], in_offset=None, bounds_check=E * CAP - 1,
                                     oob_is_err=False).then_inc(scat, DMA)

        @block.vector
        def _(v):
            ch = Chain(v, dve_own)
            def affine(b, nth):
                v.wait_ge(rstd_ready, nth)
                for t in range(b * BT, b * BT + BT):
                    ins = v.scalar_tensor_tensor(out=A[:, t, :], in0=XN[:, t, :], scalar=st[1].mean_var[:, t, 0:1],
                                                 in1=gbc[:], op0=ALU.subtract, op1=ALU.mult)
                ch.link(ins)
                for t in range(b * BT, b * BT + BT):
                    ins = v.scalar_tensor_tensor(out=A[:, t, :], in0=A[:, t, :], scalar=st[1].rstd[:, t:t + 1],
                                                 in1=bbc[:], op0=ALU.mult, op1=ALU.add)
                ins.then_inc(a_ready, 1)

            for i, (m, b) in enumerate(norm_order):
                if m == 0:
                    v.wait_ge(x_in[b], DMA)
                    row_stats(v, ch, X, st[0], b, 1e-5, var_ready)
                else:
                    row_stats(v, ch, XN, st[1], b, 1e-12, var_ready)
                for m, b in norm_done[i]:
                    nth = norm_order.index((m, b)) + 1
                    if m == 0:
                        apply_norm(v, ch, X, XN, st[0], b, rstd_ready, nth)
                        v.nop().then_inc(xn_ready, 1)
                    else:
                        if b == 0:
                            v.wait_ge(par_in, 2 * DMA)
                        affine(b, nth)
            v.wait_ge(logit_ready, 1)
            ch.link(v.tensor_copy(lg[:], lps[:]))
            ch.link(v.tensor_reduce(col[:, 0, :], lg[:, :, 0:E], AX_X, ALU.max))
            ch.link(v.tensor_reduce(col[:, 1, :], lg[:, :, E:E + 2], AX_X, ALU.max))
            ch.link(v.tensor_tensor(lg[:, :, 0:E], lg[:, :, 0:E], last_axis(col[:, 0, :], E), ALU.subtract))
            v.tensor_tensor(lg[:, :, E:E + 2], lg[:, :, E:E + 2], last_axis(col[:, 1, :], 2),
                            ALU.subtract).then_inc(max_sub, 1)
            v.wait_ge(exp_ready, 1)
            ch.link(v.tensor_reduce(col[:, 2, :], lg[:, :, 0:E], AX_X, ALU.add))
            ch.link(v.reciprocal(col[:, 3, :], col[:, 2, :]))
            ch.link(v.tensor_reduce(col[:, 4, :], lg[:, :, E:E + 2], AX_X, ALU.add))
            ch.link(v.reciprocal(col[:, 5, :], col[:, 4, :]))
            ch.link(v.tensor_tensor(K.coef_res[:], lg[:, :, E], col[:, 5, :], ALU.mult))
            ch.link(v.tensor_tensor(col[:, 6, :], lg[:, :, E + 1], col[:, 5, :], ALU.mult))
            v.wait_ge(iota_ready, 1)
            ch.link(v.tensor_scalar(r1[:], lg[:, :, 0:E], 1.0, float(E), ALU.is_lt, ALU.mult))
            ch.link(v.tensor_tensor(r1[:], r1[:], io8[:], ALU.add))
            ch.link(v.tensor_reduce(col[:, 7, :], r1[:], AX_X, ALU.min))
            v.tensor_tensor(hot[:], io8[:], last_axis(col[:, 7, :], E), ALU.is_equal).then_inc(hot_ready, 1)
            v.wait_ge(pos_ready, 1)
            ch.link(v.tensor_copy(r2[:], tot))
            v.wait_ge(tri_ready, 2)
            for e in range(E):
                ins = v.tensor_tensor_scan(r1[:, :, e], one_row[:], r2[:, :, e], 0.0, ALU.mult, ALU.add)
            ch.link(ins)
            ch.link(v.tensor_tensor(r1[:], r1[:], r2[:], ALU.subtract))
            ch.link(v.tensor_tensor(r1[:], pre, r1[:], ALU.add))
            ch.link(v.tensor_tensor(r1[:], r1[:], hot[:], ALU.mult))
            ch.link(v.tensor_reduce(col[:, 8, :], r1[:], AX_X, ALU.add))
            ch.link(v.tensor_scalar(col[:, 9, :], col[:, 8, :], float(CAP), None, ALU.is_lt))
            ch.link(v.tensor_tensor(K.coef_moe[:], col[:, 6, :], col[:, 3, :], ALU.mult))
            ch.link(v.tensor_tensor(K.coef_moe[:], K.coef_moe[:], col[:, 9, :], ALU.mult))
            ch.link(v.scalar_tensor_tensor(out=col[:, 10, :], in0=col[:, 7, :], scalar=float(CAP),
                                           in1=col[:, 8, :], op0=ALU.mult, op1=ALU.add))
            ch.link(v.tensor_tensor(col[:, 10, :], col[:, 10, :], col[:, 9, :], ALU.mult))
            ch.link(v.tensor_copy(K.gather_idx[:], col[:, 10, :]))
            ch.link(v.tensor_scalar(col[:, 11, :], col[:, 9, :], -float(2 * E * CAP), float(2 * E * CAP),
                                    ALU.mult, ALU.add))
            ch.link(v.tensor_tensor(col[:, 11, :], col[:, 11, :], col[:, 10, :], ALU.add))
            v.tensor_copy(scatter_idx[:], col[:, 11, :]).then_inc(idx_ready, 1)

        @block.tensor
        def _(pe):
            def v_rows(t):
                pe.wait_ge(K.wv_in, DMA)
                pe.wait_ge(tr_out, 2 * (t // BT) + 1)
                for c in range(2):
                    if t >= 1:
                        pe.wait_ge(va_taken, 2 * t + c - 1)
                    pe.matmul(op[c][:].rearrange("p t d -> p (t d)"), K.XNT[:, t * P:t * P + P],
                              K.wv[:, c * CH:c * CH + CH], start=True, stop=True).then_inc(va_ready, 1)

            pe.wait_ge(ident_ready, 1)
            for n in range(2 * B):
                b, src = n // 2, (XN, A)[n % 2]
                pe.wait_ge((xn_ready, a_ready)[n % 2], b + 1)
                if n >= 2:
                    pe.wait_ge(tr_out, n - 1)
                for t in range(BT):
                    mm = pe.transpose(tp[n % 2][:, t * P:t * P + P], src[:, b * BT + t, :], K.ident[:])
                mm.then_inc(tr_ready, 1)
                for t in v_tiles(n):
                    v_rows(t)
            pe.wait_ge(wg_in, 2 * DMA)
            pe.wait_ge(tr_out, 2 * B)
            for t in range(NT):
                mm = pe.matmul(lps[:, t, :], AT[:, t * P:t * P + P], wgc[:], start=True, stop=True)
            mm.then_inc(logit_ready, 1)
            for t in v_tiles(2 * B):
                v_rows(t)
            pe.wait_ge(res_in, 2 * DMA)

            def hidden(j):
                for i in range(FT):
                    if j >= 1:
                        pe.wait_ge(h_out, FT * (j - 1) + i + 1)
                    pe.matmul(hidden_ps(i), w1r[:, i * P:i * P + P], AT[:, j * CH:j * CH + CH],
                              start=True, stop=True).then_inc(h_ready, 1)

            def out(j):
                s = j % 2
                if j >= 2:
                    pe.wait_ge(o_out, j - 1)
                else:
                    pe.wait_ge(va_taken, 2 * NV)
                for i in range(FT):
                    pe.wait_ge(h_out, FT * j + i + 1)
                    for c in range(CT):
                        mm = pe.matmul(op[s][:, c, :], hT[s][:, i, c * P:c * P + P], w2r[:, i, :],
                                       start=(i == 0 and c == 0), stop=(i == FT - 1), skip_group_check=True)
                mm.then_inc(o_ready, 1)

            hidden(0)
            for j in range(NR):
                if j + 1 < NR:
                    hidden(j + 1)
                if j == COUNT_JOB:
                    pe.wait_ge(hot_ready, 1)
                    pe.wait_ge(tri_ready, 1)
                    pe.matmul(pre, tri[:], hot[:], start=True, stop=True)
                    pe.matmul(tot, ones[:], hot[:], start=True, stop=True).then_inc(pos_ready, 1)
                out(j)

        @block.scalar
        def _(act):
            def v_high(t):
                if t >= 2:
                    act.wait_ge(va_wr[t % 2], DMA * (t // 2))
                for c in range(2):
                    act.wait_ge(va_ready, 2 * t + c + 1)
                    if t >= 1:
                        act.wait_ge(va_lo, 2 * t + c - 1)
                    act.copy(v32[c], v_ps(c)).then_inc(va_taken, 1)
                    act.wait_ge(va_taken, 2 * t + c + 1)
                    act.copy(vt[t % 2][:, v_heads(c), 0, :], v32[c]).then_inc(va_hi, 1)

            for n in range(2 * B):
                b, dst = n // 2, (K.XNT, AT)[n % 2]
                act.wait_ge(tr_ready, n + 1)
                act.copy(dst[:, b * S:b * S + S], tp[n % 2][:]).then_inc(tr_out, 1)
                for t in v_tiles(n):
                    v_high(t)
            for t in v_tiles(2 * B):
                v_high(t)
            act.wait_ge(max_sub, 1)
            act.activation(lg[:], lg[:], ACT.Exp).then_inc(exp_ready, 1)
            act.wait_ge(res_bias_in, DMA)
            act.wait_ge(va_lo, 2 * NV)
            for j in range(NR):
                for i in range(FT):
                    act.wait_ge(h_ready, FT * j + i + 1)
                    if j >= 2 and i == 0:
                        act.wait_ge(o_ready, j - 1)
                    act.activation(hT[j % 2][:, i, :], hidden_ps(i), ACT.Gelu_apprx_tanh,
                                   bias=b1r[:, i:i + 1]).then_inc(h_out, 1)
                if j >= 1:
                    take_out(act, j - 1)
            take_out(act, NR - 1)


def load_expert(sp, K, io, e):
    s = e % RING
    sp.dma_start(K.w1[s][:], io["inter_w"][e]).then_inc(K.w_in[s], DMA)
    sp.dma_start(K.w2[s][:], io["output_w"][e].rearrange("(i p) d -> p i d", p=P)).then_inc(K.w_in[s], DMA)


def load_rows(sp, K, e):
    s = e % RING
    sp.dma_start(K.dx[s][:], K.disp[bass.ts(e, CAP), :].rearrange("(c p) d -> p c d", p=P)).then_inc(K.d_in[s], DMA)


def experts(nc, K, io, sb, ps, sem):
    fr_in, bp_in = sem("fr_in"), sem("bp_in")
    pos_made, sin_arg, sin_out = sem("pos_made"), sem("sin_arg"), sem("sin_out")
    ln_arg, ln_out, f_ready, f_wr = sem("ln_arg"), sem("ln_out"), sem("f_ready"), sem("f_wr")
    freq = sb("freq", [P, 1])
    pos, ang, tn = sb("pos", [P, S]), sb("ang", [P, S]), sb("turns", [P, S])
    half_pi, one_col = sb("half_pi", [P, 1]), sb("one_col", [P, 1])
    dist = sb("dist", [H, FLEN])
    bp, ba = sb("bias_p", [H, 1]), sb("bias_a", [H, 1])
    COS, SIN = K.COS, K.SIN
    bias_in = sem("bias_in")
    dt_ready, dt_out = sem("dt_ready"), sem("dt_out")
    h_ready, h_out, o_ready, o_out = sem("h_ready"), sem("h_out"), sem("o_ready"), sem("o_out")
    e_wr = [sem("e_wr0"), sem("e_wr1")]
    own = sem("exp_dve")

    b1 = sb("b1_cols", [P, E, FT])
    b2, b2r = sb("b2_rows", [P, E * D]), sb("b2_res_rows", [P, D])
    dT = [sb(f"dispatched_t{i}", [P, CAP]) for i in range(2)]
    hT = [sb(f"hidden_t{i}", [P, FT, CAP]) for i in range(2)]
    eo = [sb(f"expert_out{i}", [P, CAP // P, D]) for i in range(2)]
    hp = [ps(f"hid_ps{i}", [P, CH]) for i in range(4)]
    op = [ps(f"out_ps{i}", [P, CAP // P, D]) for i in range(2)]
    tp = [ps(f"dt_ps{i}", [P, CH]) for i in range(2)]
    CT = CAP // P
    TABLE_JOB = E - 1
    w1, w2, dx = K.w1, K.w2, K.dx

    with nc.Block() as block:

        @block.sync
        def _(sp):
            sp.dma_start(b1[:], io["inter_b"]).then_inc(bias_in, DMA)
            sp.dma_start(b2[:], io["output_b"].rearrange("e d -> (e d)").partition_broadcast(P)).then_inc(bias_in, DMA)
            sp.dma_start(b2r[:], io["res_output_b"].partition_broadcast(P)).then_inc(bias_in, DMA)
            for i in range(P // (DH // 2)):
                sp.dma_start(freq[32 * i:32 * i + 32, :], io["freqs"].rearrange("(p o) -> p o", o=1)).then_inc(fr_in, DMA)
            sp.dma_start(bp[:], io["bias_p"]).then_inc(bp_in, DMA)
            sp.dma_start(ba[:], io["bias_a"]).then_inc(bp_in, DMA)
            for e in range(E):
                sp.wait_ge(o_out, e + 1)
                sp.dma_start(K.eout[bass.ts(e, CAP), :].rearrange("(c p) d -> p c d", p=P), eo[e % 2][:]).then_inc(e_wr[e % 2], DMA)
                if e + RING < E:
                    load_expert(sp, K, io, e + RING)
                    load_rows(sp, K, e + RING)
            sp.wait_ge(f_ready, 1)
            sp.dma_start(K.fscr, dist[:]).then_inc(f_wr, DMA)
            for s in range(2):
                sp.wait_ge(e_wr[s], DMA * E // 2)
            sp.wait_ge(f_wr, DMA)

        @block.gpsimd
        def _(g):
            g.iota(pos[:], pattern=[[1, S]], base=0, channel_multiplier=0,
                   allow_small_or_imprecise_dtypes=True).then_inc(pos_made, 1)
            g.iota(dist[:], pattern=[[1, FLEN]], base=-(S - 1), channel_multiplier=0,
                   allow_small_or_imprecise_dtypes=True).then_inc(pos_made, 1)
            g.memset(half_pi[:], math.pi / 2).then_inc(pos_made, 1)
            g.memset(one_col[:], 1.0).then_inc(pos_made, 1)

        @block.tensor
        def _(pe):
            def turn(e):
                pe.wait_ge(K.d_in[e % RING], DMA * (e // RING + 1))
                if e >= 2:
                    pe.wait_ge(dt_out, e - 1)
                for c in range(CT):
                    mm = pe.transpose(tp[e % 2][:, c * P:c * P + P], dx[e % RING][:, c, :], K.ident[:])
                mm.then_inc(dt_ready, 1)

            def hidden(e):
                pe.wait_ge(K.w_in[e % RING], 2 * DMA * (e // RING + 1))
                pe.wait_ge(dt_out, e + 1)
                for i in range(FT):
                    if e >= 1:
                        pe.wait_ge(h_out, FT * (e - 1) + i + 1)
                    pe.matmul(hp[i][:], w1[e % RING][:, i * P:i * P + P], dT[e % 2][:], start=True,
                              stop=True).then_inc(h_ready, 1)

            def out(e):
                s = e % 2
                if e >= 2:
                    pe.wait_ge(o_out, e - 1)
                for i in range(FT):
                    pe.wait_ge(h_out, FT * e + i + 1)
                    for c in range(CT):
                        mm = pe.matmul(op[s][:, c, :], hT[s][:, i, c * P:c * P + P], w2[e % RING][:, i, :],
                                       start=(i == 0 and c == 0), stop=(i == FT - 1), skip_group_check=True)
                mm.then_inc(o_ready, 1)

            turn(0)
            turn(1)
            hidden(0)
            for e in range(E):
                if e + 2 < E:
                    turn(e + 2)
                if e + 1 < E:
                    hidden(e + 1)
                out(e)

        @block.scalar
        def _(act):
            act.wait_ge(bias_in, 3 * DMA)
            for e in range(E):
                for i in range(FT):
                    act.wait_ge(h_ready, FT * e + i + 1)
                    if e >= 2 and i == 0:
                        act.wait_ge(o_ready, e - 1)
                    act.activation(hT[e % 2][:, i, :], hp[i][:], ACT.Gelu_apprx_tanh, bias=b1[:, e, i:i + 1]).then_inc(h_out, 1)
                if e == TABLE_JOB:
                    act.wait_ge(sin_arg, 1)
                    act.activation(SIN[:], ang[:], ACT.Sin).then_inc(sin_out, 1)
                    act.activation(COS[:], tn[:], ACT.Sin, bias=half_pi[:, 0:1], scale=-1.0).then_inc(sin_out, 1)
                    act.wait_ge(ln_arg, 1)
                    act.activation(dist[:], dist[:], ACT.Ln, bias=one_col[0:H, 0:1], scale=ba[:, 0:1]).then_inc(ln_out, 1)

        @block.vector
        def _(v):
            ch = Chain(v, own)

            def take_rows(e):
                v.wait_ge(dt_ready, e + 1)
                if e >= 2:
                    v.wait_ge(h_ready, FT * (e - 1))
                v.tensor_copy(dT[e % 2][:], tp[e % 2][:]).then_inc(dt_out, 1)

            def residual(b):
                n = slice(b * BT, b * BT + BT)
                ch.link(v.tensor_tensor(K.G0[:, n, :], K.G0[:, n, :], mid_axis(b2r[:], BT), ALU.add))
                ch.link(v.tensor_tensor(K.G0[:, n, :], K.G0[:, n, :], last_axis(K.coef_res[:, n], D), ALU.mult))
                ch.link(v.tensor_tensor(K.G0[:, n, :], K.G0[:, n, :], K.XN[:, n, :], ALU.add))

            def angles():
                v.wait_ge(pos_made, 4)
                v.wait_ge(fr_in, 4 * DMA)
                ch.link(v.tensor_scalar(ang[:], pos[:], freq[:, 0:1], None, ALU.mult))
                ch.link(v.tensor_scalar(tn[:], ang[:], 1.0 / (2.0 * math.pi), MAGIC, ALU.mult, ALU.add))
                ch.link(v.tensor_scalar(tn[:], tn[:], MAGIC, None, ALU.subtract))
                for part in (TWO_PI_1, TWO_PI_2, TWO_PI_3):
                    ch.link(v.scalar_tensor_tensor(out=ang[:], in0=tn[:], scalar=-part, in1=ang[:],
                                                   op0=ALU.mult, op1=ALU.add))
                ch.link(v.tensor_scalar(ang[:], ang[:], 3.1415925, -3.1415925, ALU.min, ALU.max))
                v.scalar_tensor_tensor(out=tn[:], in0=ang[:], scalar=-1.0, in1=ang[:], op0=ALU.mult,
                                       op1=ALU.max).then_inc(sin_arg, 1)

            def distances():
                v.wait_ge(bp_in, 2 * DMA)
                ch.link(v.scalar_tensor_tensor(out=dist[:], in0=dist[:], scalar=-1.0, in1=dist[:], op0=ALU.mult, op1=ALU.max))
                ch.link(v.tensor_scalar(ba[:], ba[:], 0.01, None, ALU.max))
                ch.link(v.tensor_scalar(bp[:], bp[:], 0.01, -1.0, ALU.max, ALU.mult))
                v.nop().then_inc(ln_arg, 1)

            def tables():
                v.wait_ge(ln_out, 1)
                v.tensor_scalar(dist[:], dist[:], bp[:, 0:1], None, ALU.mult).then_inc(f_ready, 1)
                v.wait_ge(sin_out, 2)
                for h in range(2):
                    ch.link(v.tensor_scalar(SIN[h * DH:h * DH + DH // 2, :], SIN[h * DH:h * DH + DH // 2, :], -1.0,
                                            None, ALU.mult))

            take_rows(0)
            take_rows(1)
            v.wait_ge(bias_in, 3 * DMA)
            for e in range(E):
                s = e % 2
                if e + 2 < E:
                    take_rows(e + 2)
                if e < B:
                    residual(e)
                elif e == B:
                    angles()
                    distances()
                v.wait_ge(o_ready, e + 1)
                if e >= 2:
                    v.wait_ge(e_wr[s], DMA * (e // 2))
                v.tensor_tensor(eo[s][:], op[s][:], mid_axis(b2[:, e * D:e * D + D], CT), ALU.add).then_inc(o_out, 1)
            tables()


def project(nc, K, io, sb, ps, sem):
    v_ready, vhi, vlo, v_wr = sem("v_ready"), sem("vhi"), sem("vlo"), [sem(f"v_wr{s}") for s in range(4)]
    wqk_in = [sem("wqk_in0"), sem("wqk_in1")]
    qk_ready, qk_read, pair, summed = sem("qk_ready"), sem("qk_read"), sem("pair"), sem("summed")
    hi_ready, lo_ready, qk_wr = sem("hi_ready"), sem("lo_ready"), [sem(f"qk_wr{s}") for s in range(4)]
    gath, mixed, mix_ready, g0_ready = sem("gathered"), sem("moe_scaled"), sem("mix_ready"), sem("g0_ready")

    COS, SIN = K.COS, K.SIN
    wv = K.wv
    NW = NT - NV
    vt = [sb(f"v_parts{i}", [P, H, 2, DH], BF16) for i in range(4)]
    wqk = [sb(f"wqk{i}", [P, 4, P]) for i in range(2)]
    t1 = [sb(f"rope1_{i}", [P, 2, CH]) for i in range(4)]
    t2 = [sb(f"rope2_{i}", [P, 2, CH]) for i in range(4)]
    parts = [sb(f"qk_parts{i}", [P, 4, CH], BF16) for i in range(4)]
    pp = [ps(f"proj_ps{i}", [P, 4, CH]) for i in range(2)]
    NC = S // CH
    XNT = K.XNT

    def jobs():
        for b in range(B):
            for c in range(NC):
                yield b * NC + c, b, c

    NJ = B * NC

    def tiles(ap):
        return ap.rearrange("p (t j) -> p t j", j=P)

    def rotated(r, i):
        ap = tiles(t1[r][:, i, :])
        return ap[:, :, ::-1] if i == 0 else ap

    LEAD = 2

    def run_jobs(eng, step):
        for u in range(-LEAD, 0):
            step(0, u, lambda x: x >= 0)
        with eng.Fori(0, G - 1) as gi:
            for u in range(NJ):
                step(gi, u, lambda x: True)
        for u in range(NJ):
            step(G - 1, u, lambda x: x < NJ)

    def rope(v, gi, j):
        c, s, r = j % NC, j % 2, j % 4
        cs = slice(c * CH, c * CH + CH)
        q4 = pp[s][:].rearrange("p (k w) c -> p k w c", w=2)
        v.wait_ge(qk_ready, gi * NJ + (j + 1))
        v.wait_ge(lo_ready, gi * NJ + max(j, 1))
        v.tensor_tensor(t1[r][:], q4[:, :, 0, :], mid_axis(COS[:, cs], 2), ALU.mult)
        v.tensor_tensor(t2[r][:], q4[:, :, 1, :], mid_axis(SIN[:, cs], 2), ALU.mult).then_inc(pair, 1)

    def hi_part(act, gi, j):
        s = j % 4
        act.wait_ge(summed, gi * NJ + (j + 1))
        act.wait_ge(qk_wr[s], gi * (DMA * NJ // 4) + (DMA * (j // 4) + 1))
        act.activation(tiles(parts[s][:, 0, :]), rotated(s, 0), ACT.Copy, scale=SCALE).then_inc(hi_ready, 1)
        act.activation(parts[s][:, 2, :], t1[s][:, 1, :], ACT.Copy).then_inc(hi_ready, 1)

    def lo_part(v, gi, j):
        s = j % 4
        v.wait_ge(hi_ready, gi * (2 * NJ) + 2 * (j + 1))
        for i, scale in enumerate((SCALE, 1.0)):
            ins = v.scalar_tensor_tensor(out=tiles(parts[s][:, 2 * i + 1, :]), in0=rotated(s, i), scalar=scale,
                                         in1=tiles(parts[s][:, 2 * i, :]), op0=ALU.mult, op1=ALU.subtract)
        ins.then_inc(lo_ready, 1)

    def write(act, gi, j):
        b, c, s = j // NC, j % NC, j % 4
        act.wait_ge(lo_ready, gi * NJ + (j + 2 + LEAD))
        act.dma_start(K.qkscr[bass.ds(gi + b * G, 1), :, :, c * CH:c * CH + CH].rearrange("o p k c -> (o p) k c"),
                      parts[s][:]).then_inc(qk_wr[s], DMA)

    with nc.Block() as block:

        @block.sync
        def _(sp):
            for r in range(2):
                sp.dma_start(wqk[r][:], io["wqk"][r]).then_inc(wqk_in[r], DMA)
            for t in range(NW):
                sp.wait_ge(vhi, 2 * t + 2)
                sp.wait_ge(vlo, 2 * t + 2)
                sp.dma_start(K.vscr[NV + t], vt[t % 4][:].rearrange("p h a d -> p h (a d)")).then_inc(v_wr[t % 4], DMA)
            for s in range(4):
                sp.wait_ge(v_wr[s], DMA * NW // 4)
            with sp.Fori(0, G // 2 - 1) as gh:
                for r in range(2):
                    sp.wait_ge(qk_ready, gh * (2 * NJ) + (r + 1) * NJ)
                    sp.dma_start(wqk[r][:], io["wqk"][bass.ds(gh * 2 + (r + 2), 1)].rearrange("o p k m -> (o p) k m")).then_inc(wqk_in[r], DMA)
            for s in range(4):
                sp.wait_ge(qk_wr[s], DMA * NJ // 4 + 1)
            for s in range(2):
                load_scores_in(sp, K, 0, s)

        @block.gpsimd
        def _(g):
            for t in range(NT):
                g.indirect_dma_start(out=K.MOE[:, t, :], out_offset=None, in_=K.eout,
                                     in_offset=bass.IndirectOffsetOnAxis(K.gather_idx[:, t:t + 1], 0),
                                     bounds_check=E * CAP - 1, oob_is_err=False).then_inc(gath, DMA)
            g.wait_ge(gath, DMA * NT)
            g.tensor_tensor(K.MOE[:], K.MOE[:], last_axis(K.coef_moe[:], D), ALU.mult).then_inc(mixed, 1)
            g.wait_ge(mixed, 1)
            g.tensor_tensor(K.G0[:], K.G0[:], K.MOE[:], ALU.add).then_inc(mix_ready, 1)
            with g.Fori(0, G) as gi:
                for j, b, c in jobs():
                    r = j % 4
                    g.wait_ge(pair, gi * NJ + (j + 3))
                    g.tensor_tensor(t1[r][:], t1[r][:], t2[r][:], ALU.add).then_inc(summed, 1)

        @block.vector
        def _(v):
            for t in range(NW):
                for c in range(2):
                    n = 2 * t + c
                    v.wait_ge(vhi, n + 1)
                    hs = slice(c * H // 2, c * H // 2 + H // 2)
                    v.tensor_tensor(vt[t % 4][:, hs, 1, :],
                                    pp[n // 4 % 2][:, n % 4, :].rearrange("p (h d) -> p h d", d=DH),
                                    vt[t % 4][:, hs, 0, :], ALU.subtract).then_inc(vlo, 1)
            v.wait_ge(vlo, 2 * NW)
            for _ in range(2):
                v.nop().then_inc(pair, 1)
            v.nop().then_inc(lo_ready, LEAD + 1)

            def step(gi, u, there):
                if there(u + LEAD):
                    rope(v, gi, u + LEAD)
                if there(u):
                    lo_part(v, gi, u)

            run_jobs(v, step)

        @block.scalar
        def _(act):
            for t in range(NW):
                if t >= 4:
                    act.wait_ge(v_wr[t % 4], DMA * (t // 4))
                for c in range(2):
                    n = 2 * t + c
                    act.wait_ge(v_ready, n + 1)
                    act.copy(vt[t % 4][:, c * H // 2:c * H // 2 + H // 2, 0, :],
                             pp[n // 4 % 2][:, n % 4, :].rearrange("p (h d) -> p h d", d=DH)).then_inc(vhi, 1)
            act.wait_ge(mix_ready, 1)
            act.activation(K.G0[:], K.G0[:], ACT.Silu).then_inc(g0_ready, 1)
            for s in range(4):
                act.nop().then_inc(qk_wr[s], 1)

            def step(gi, u, there):
                if there(u + LEAD):
                    hi_part(act, gi, u + LEAD)
                if there(u):
                    write(act, gi, u)

            run_jobs(act, step)
            for s in range(4):
                act.wait_ge(qk_wr[s], G * (DMA * NJ // 4) + 1)

        @block.tensor
        def _(pe):
            for t in range(NW):
                for c in range(2):
                    n = 2 * t + c
                    if n >= 8:
                        pe.wait_ge(vlo, n - 7)
                    pe.matmul(pp[n // 4 % 2][:, n % 4, :], XNT[:, (NV + t) * P:(NV + t + 1) * P], wv[:, c * CH:c * CH + CH],
                              start=True, stop=True).then_inc(v_ready, 1)
            with pe.Fori(0, G // 2) as gh:
                for r in range(2):
                    pe.wait_ge(wqk_in[r], gh * DMA + DMA)
                    for j, b, c in jobs():
                        s = j % 2
                        pe.wait_ge(pair, gh * (2 * NJ) + (r * NJ + j + 1))
                        for i in range(4):
                            mm = pe.matmul(pp[s][:, i, :], wqk[r][:, i, :],
                                           XNT[:, b * S + c * CH:b * S + c * CH + CH], start=True, stop=True)
                        mm.then_inc(qk_ready, 1)


def load_scores_in(sp, K, ix, s):
    q = K.qkscr[bass.ds(ix, 1)].rearrange("o p k c -> (o p) k c")
    rows = slice(s * DH, s * DH + DH)
    sp.dma_start(K.QS[s][0:DH, :], q[rows, 0, :]).then_inc(K.qk_in[s], DMA)
    sp.dma_start(K.QS[s][DH:P, :], q[rows, 1, :]).then_inc(K.qk_in[s], DMA)
    sp.dma_start(K.QX[s][0:DH, :], q[rows, 1, :]).then_inc(K.qk_in[s], DMA)
    sp.dma_start(K.QX[s][DH:P, :], q[rows, 0, :]).then_inc(K.qk_in[s], DMA)
    sp.dma_start(K.KS[s][0:DH, :], q[rows, 2, :]).then_inc(K.qk_in[s], DMA)
    sp.dma_start(K.KS[s][DH:P, :], q[rows, 2, :]).then_inc(K.qk_in[s], DMA)
    sp.dma_start(K.KL[s][0:DH, :], q[rows, 3, :]).then_inc(K.qk_in[s], DMA)
    sp.dma_start(K.KL[s][DH:P, :], q[rows, 3, :]).then_inc(K.qk_in[s], DMA)
    tab = bass.AP(tensor=K.fscr.tensor, offset=((ix % G) * 2 + s) * FLEN, ap=[[1, P], [1, TAB]])
    sp.dma_start(K.TB[s][:], tab).then_inc(K.tab_in[s], DMA)


def attend(nc, K, io, sb, ps, sem):
    qk_in, tab_in = K.qk_in, K.tab_in
    v_in, wo_in = [[sem(f"{n}_in{s}") for s in range(2)] for n in ("av", "aw")]
    s_ready, biased, exped = sem("s_ready"), sem("biased"), sem("exped")
    turned, turn_out, lo_ready = sem("turned"), sem("turn_out"), sem("p_lo_ready")
    pv_ready, ot_ready, op_ready, added, zeroed = sem("pv_ready"), sem("ot_ready"), sem("op_ready"), sem("added"), sem("acc_zeroed")
    recip = sem("recip")

    QS, QX, KS, KL, TB = K.QS, K.QX, K.KS, K.KL, K.TB
    VV = [sb(f"v_hi_lo{s}", [P, BT, 2 * DH], BF16) for s in range(2)]
    WO = [sb(f"wo{s}", [P, P]) for s in range(2)]
    SB = [sb(f"scores{i}", [P, S]) for i in range(2)]
    PR = [sb(f"probs{i}", [P, S]) for i in range(2)]
    PT = sb("probs_t", [P, 2 * BT, BT, P])
    LO = sb("probs_t_lo", [P, 2 * BT, BT, P], BF16)
    WB = [sb(f"wo_parts{s}", [P, 2, P], BF16) for s in range(2)]
    OH = [sb(f"out_t_hi{i}", [P, CH], BF16) for i in range(2)]
    OL = [sb(f"out_t_lo{i}", [P, CH], BF16) for i in range(2)]
    ot_hi, wo_hi, wo_ready = sem("ot_hi"), sem("wo_hi"), sem("wo_ready")
    neg_max, row_sum = sb("neg_max", [P, 16]), sb("row_sum", [P, 16])
    inv = sb("inv_sum", [P, 16])
    gate = sb("wait_holder", [P, 2])
    sp_ = [ps(f"score_ps{i}", [P, S]) for i in range(2)]
    tp = [ps(f"turn_ps{i}", [P, 4, P]) for i in range(2)]
    ov = [ps(f"pv_ps{i}", [P, 4, P]) for i in range(2)]
    PTB = PT[:].bitcast(BF16)

    NI = B * G
    U = 2 * BT
    LS, LE, LT = 11, 10, 9
    V_STEPS, OUT_STEP, PROJ_STEP = 6, 6, 7

    def run(eng, step):
        for u in range(-LS, 0):
            step(0, u, lambda x: 0 <= x < U)
        with eng.Fori(0, NI - 1) as it:
            for u in range(U):
                step(it, u, lambda x: True)
        for u in range(U):
            step(NI - 1, u, lambda x: x < U)

    def at(it, n, add):
        return it * n + add

    with nc.Block() as block:

        @block.sync
        def _(sp):
            def load_v(ix, s):
                row = H * 2 * DH
                v = bass.AP(tensor=K.vscr.tensor, offset=(ix // G) * (BT * P * row) + ((ix % G) * 2 + s) * (2 * DH),
                            ap=[[row, P], [P * row, BT], [1, 2 * DH]])
                sp.dma_start(VV[s][:], v).then_inc(v_in[s], DMA)
                sp.dma_start(WO[s][:], io["wo2"][bass.ds((ix % G) * 2 + s, 1)].rearrange("o p m -> (o p) m")).then_inc(wo_in[s], DMA)

            for s in range(2):
                load_v(0, s)
            with sp.Fori(0, NI - 1) as it:
                for s in range(2):
                    sp.wait_ge(s_ready, at(it, U, BT * (s + 1)))
                    sp.wait_ge(biased, at(it, U, BT * (s + 1)))
                    load_scores_in(sp, K, it + 1, s)
                    sp.wait_ge(op_ready, at(it, 4, 2 * (s + 1)))
                    load_v(it + 1, s)

        @block.tensor
        def _(pe):
            def scores(it, n):
                s, t, k = n // BT % 2, n % BT, n // U
                if t == 0:
                    pe.wait_ge(qk_in[s], at(it, 8 * DMA, 8 * DMA * (k + 1)))
                if not (isinstance(it, int) and it == 0 and n < 2):
                    pe.wait_ge(biased, at(it, U, n - 1))
                o, q = sp_[n % 2], slice(t * P, t * P + P)
                cs = [slice(c * CH, c * CH + CH) for c in range(2)]
                for c in range(2):
                    pe.matmul(o[:, cs[c]], (QS, QX)[c][s][:, q], KS[s][:, cs[c]], start=True, stop=False)
                for c in range(2):
                    rows = slice(c * DH, c * DH + DH)
                    mm = pe.matmul(o[:, cs[c]], (QS, QX)[c][s][rows, q], KL[s][rows, cs[c]], start=False, stop=True)
                mm.then_inc(s_ready, 1)

            def turn(it, n):
                pe.wait_ge(exped, at(it, U, n + 1))
                for half in range(2):
                    w = 2 * n + half
                    if not (isinstance(it, int) and it == 0 and w < 2):
                        pe.wait_ge(turn_out, at(it, 2 * U, w - 1))
                    for k in range(4):
                        mm = pe.transpose(tp[half][:, k, :], PR[n % 2][:, (4 * half + k) * P:(4 * half + k + 1) * P],
                                          K.ident[:])
                    mm.then_inc(turned, 1)

            def by_v(it, h, j):
                if j == 0:
                    pe.wait_ge(v_in[h], at(it, DMA, DMA))
                    pe.wait_ge(lo_ready, at(it, U, BT * (h + 1)))
                    pe.wait_ge(added, at(it, 16, BT * h + 1))
                units = [(k, part) for k in range(BT) for part in range(3)]
                n = len(units) // V_STEPS
                for k, part in units[j * n:j * n + n]:
                    for c in ((0,), (1,), (0, 1))[part]:
                        r = BT * h + 4 * c
                        if part < 2:
                            mm = pe.matmul(ov[c][:], VV[h][:, k, :], PTB[:, r:r + 4, k, 1::2], start=(k == 0),
                                           stop=False, skip_group_check=True)
                        else:
                            mm = pe.matmul(ov[c][c * DH:c * DH + DH], VV[h][:, k, 0:DH], LO[:, r:r + 4, k, :],
                                           start=False, stop=(k == BT - 1), skip_group_check=True)
                if j == V_STEPS - 1:
                    mm.then_inc(pv_ready, 1)

            def out(it, h):
                pe.wait_ge(wo_ready, at(it, 2, h + 1))
                for c in range(2):
                    pe.wait_ge(ot_ready, at(it, 4, 2 * h + c + 1))
                    for k in range(4):
                        q = slice(k * P, k * P + P)
                        pe.matmul(ov[c][:, k, :], OH[c][:, q], WB[h][:, 0, :], start=(k == 0), stop=False, skip_group_check=True)
                        pe.matmul(ov[c][:, k, :], OH[c][:, q], WB[h][:, 1, :], start=False, stop=False, skip_group_check=True)
                        mm = pe.matmul(ov[c][:, k, :], OL[c][:, q], WB[h][:, 0, :], start=False, stop=True, skip_group_check=True)
                    mm.then_inc(op_ready, 1)

            def step(it, u, there):
                h, j = u // BT, u % BT
                if there(u + LS):
                    scores(it, u + LS)
                if there(u) and j == PROJ_STEP:
                    out(it, h)
                if there(u + LT):
                    turn(it, u + LT)
                if there(u) and j < V_STEPS:
                    by_v(it, h, j)

            run(pe, step)

        @block.vector
        def _(v):
            def bias_max(it, n):
                s, t = n // BT % 2, n % BT
                v.wait_ge(s_ready, at(it, U, n + 1))
                if t == 0:
                    v.wait_ge(tab_in[s], at(it, DMA, DMA * (n // U + 1)))
                if not (isinstance(it, int) and it == 0 and n < 2):
                    v.wait_ge(exped, at(it, U, n - 1))
                j = TAB - S - t * P
                v.memset(gate[:, n % 2:n % 2 + 1], 0.0)
                v.tensor_tensor_reduce(SB[n % 2][:], sp_[n % 2][:], TB[s][:, j:j + S], -1.0, 3.0e38,
                                       ALU.add, ALU.min, neg_max[:, n % 16:n % 16 + 1]).then_inc(biased, 1)

            def invert(it, h):
                v.wait_ge(exped, at(it, U, BT * (h + 1)))
                v.wait_ge(added, at(it, 16, BT * h + 1))
                v.reciprocal(inv[:, BT * h:BT * h + BT], row_sum[:, BT * h:BT * h + BT]).then_inc(recip, 1)

            def split_wo(it, h):
                v.wait_ge(wo_in[h], at(it, DMA, DMA))
                v.tensor_copy(WB[h][:, 0, :], WO[h][:]).then_inc(wo_hi, 1)
                v.wait_ge(wo_hi, at(it, 2, h + 1))
                v.tensor_tensor(WB[h][:, 1, :], WO[h][:], WB[h][:, 0, :], ALU.subtract).then_inc(wo_ready, 1)

            def take_out(it, h):
                for c in range(2):
                    v.wait_ge(ot_hi, at(it, 4, 2 * h + c + 1))
                    v.tensor_tensor(OL[c][:], ov[c][:].rearrange("p t q -> p (t q)"), OH[c][:], ALU.subtract).then_inc(ot_ready, 1)

            def add_share(it, h):
                v.wait_ge(recip, at(it, 2, h + 1))
                for t in range(BT):
                    if t % 4 == 0:
                        v.wait_ge(op_ready, at(it, 4, 2 * h + t // 4 + 1))
                    row = (it // G) * BT + t
                    if not isinstance(row, int):
                        acc = K.SACC[:, bass.ds(row, 1), :].rearrange("p o d -> p (o d)")
                    else:
                        acc = K.SACC[:, row, :]
                    v.scalar_tensor_tensor(out=acc, in0=ov[t // 4][:, t % 4, :], scalar=inv[:, BT * h + t:BT * h + t + 1],
                                           in1=acc, op0=ALU.mult, op1=ALU.add).then_inc(added, 1)

            def step(it, u, there):
                h, j = u // BT, u % BT
                if there(u) and j == OUT_STEP:
                    take_out(it, h)
                if there(u + LS):
                    bias_max(it, u + LS)
                if there(u) and j == V_STEPS - 1:
                    invert(it, h)
                    split_wo(it, h)
                if there(u) and j == PROJ_STEP:
                    add_share(it, h)

            v.memset(K.SACC[:], 0.0).then_inc(zeroed, 1)
            v.wait_ge(zeroed, 1)
            v.nop().then_inc(added, 1)
            run(v, step)

        @block.scalar
        def _(act):
            def exp(it, n):
                act.wait_ge(biased, at(it, U, n + 1))
                if not (isinstance(it, int) and it == 0 and n < 2):
                    act.wait_ge(turned, at(it, 2 * U, 2 * (n - 1)))
                m = n % 16
                if n % BT == 0 and not (isinstance(it, int) and it == 0 and n < U):
                    act.wait_ge(recip, at(it, 2, n // BT - 1))
                act.activation(PR[n % 2][:], SB[n % 2][:], ACT.Exp, bias=neg_max[:, m:m + 1], scale=-1.0,
                               accum_out=row_sum[:, m:m + 1]).then_inc(exped, 1)

            def untile(it, n):
                if n % BT == 0 and not (isinstance(it, int) and it == 0 and n < U):
                    act.wait_ge(pv_ready, at(it, 2, n // BT - 1))
                for half in range(2):
                    act.wait_ge(turned, at(it, 2 * U, 2 * n + half + 1))
                    act.copy(PT[:, n % U, 4 * half:4 * half + 4, :], tp[half][:]).then_inc(turn_out, 1)

            def take_out(it, h):
                act.wait_ge(pv_ready, at(it, 2, h + 1))
                for c in range(2):
                    act.copy(OH[c][:], ov[c][:].rearrange("p t q -> p (t q)")).then_inc(ot_hi, 1)

            def step(it, u, there):
                if there(u) and u % BT == OUT_STEP:
                    take_out(it, u // BT)
                if there(u + LE):
                    exp(it, u + LE)
                if there(u + LT):
                    untile(it, u + LT)

            run(act, step)

        @block.gpsimd
        def _(g):
            def low(it, n):
                r = n % U
                g.wait_ge(turn_out, at(it, 2 * U, 2 * n + 2))
                g.tensor_tensor(LO[:, r, :, :], PT[:, r, :, :], PTB[:, r, :, 1::2], ALU.subtract).then_inc(lo_ready, 1)

            def step(it, u, there):
                if there(u + LT):
                    low(it, u + LT)

            run(g, step)


def recur(nc, K, io, sb, ps, sem):
    x_in = [sem("x_again_in"), sem("x_rest_in")]
    vo_in = sem("vo_in")
    w_in, base_ready = sem("rw_in"), sem("base_ready")
    var_ready, rstd_ready, half_ready = sem("var1_ready"), sem("rstd1_ready"), sem("half1_ready")
    xn_ready, made, act_out, kv_read = sem("xn1_ready"), sem("made"), sem("act_out"), sem("kv_read")
    scanned, weighed, weighed_used, s1_ready, s1_out = (sem("scanned"), sem("weighed"), sem("weighed_used"),
                                                        sem("s1_ready"), sem("s1_out"))
    own, flip_ready, flipped, flip_read = sem("recur_dve"), sem("flip_ready"), sem("flipped"), sem("flip_read")

    st = NormStats(sb, "ln1")
    neg_half = sb("neg_half1", [P, NT])
    prod = sb("s0_g0", [P, BT, D])
    lbf = sb("lora_b_f32", [3 * ER, F])
    wz, gb = sb("gate_lora_a", [P, NZ]), sb("gate_b", [P, E])
    ZL = sb("z_rows", [P, NT, NZ])
    io8, r1, hot, col = sb("iota8_1", [P, NT, E]), sb("route1_1", [P, NT, E]), sb("onehot1", [P, NT, E]), sb("cols1", [P, 2, NT])
    wz_in, iota_ready = sem("wz_in"), sem("iota1_ready")
    z_ready, z_out, max_sub, exp_ready = sem("z_ready"), sem("z_out"), sem("max1_sub"), sem("exp1_ready")
    wq, wk = sb("q_w", [P, P]), sb("k_w", [P, P])
    wv, wo = sb("v_w_rep", [P, 8, P]), sb("o_w_rep", [P, 8, P])
    c1w, c2w = sb("cs_w1", [P, D // 4]), sb("cs_w2_rep", [D // 4, P])
    c1b, c2b = sb("cs_b1", [D // 4, 1]), sb("cs_b2_rep", [P, 1])
    base = sb("decay_base", [P, 1])
    QT, KT = sb("q_t", [P, 2, S]), sb("k_t", [P, 2, S])
    C1, LAM = sb("cs_hidden", [D // 4, S]), sb("lam", [P, 2, S])
    KV, SC, WT = sb("kv", [P, 2, S]), sb("state", [P, 2, S]), sb("q_state", [P, 2, S])
    pj = [ps(f"made_ps{i}", [P, S]) for i in range(2)]
    so = ps("s1_ps", [P, BT, P])
    fs = ps("s0_ps", [P, BT, P])
    flip = sb("flip", [P, P])
    zp = fs[:].rearrange("p t d -> p (t d)")[:, 0:BT * NZ].rearrange("p (t z) -> p t z", z=NZ)
    Z_AT = 3
    FE = 8
    X, XN, X1, XNT = K.X, K.XN, K.X, K.XNT

    with nc.Block() as block:

        @block.sync
        def _(sp):
            def load_x(b):
                sp.dma_start(X[:, b * BT:b * BT + BT, :],
                             io["x"][b].rearrange("(t p) d -> p t d", p=P)).then_inc(x_in[min(b, 1)], DMA)

            load_x(0)
            for dst, src in ((wq[:], io["q_w"]), (wk[:], io["k_w"]), (c1w[:], io["cs_w1"]),
                             (c2w[:], io["cs_w2"]), (c1b[:], io["cs_b1"]), (c2b[:], io["cs_b2"])):
                sp.dma_start(dst, src).then_inc(w_in, DMA)
            sp.dma_start(base[:], io["decay"]).then_inc(w_in, DMA)
            sp.dma_start(wv[:], io["v_w"]).then_inc(vo_in, DMA)
            sp.dma_start(wo[:], io["o_w"]).then_inc(vo_in, DMA)
            load_x(1)
            sp.dma_start(wz[:], io["wz"]).then_inc(wz_in, DMA)
            load_x(2)
            load_x(3)
            sp.dma_start(gb[:], io["gate_b"].partition_broadcast(P)).then_inc(wz_in, DMA)
            for dst, src in ((lbf[0:ER, :], io["lora_b"]), (lbf[ER:2 * ER, :], io["lora_b"]), (lbf[2 * ER:3 * ER, :], io["lora_b"]),
                             (K.wi[:], io["wi"]),
                             (K.wo1[:], io["wo_t"].rearrange("(i p) d -> p i d", p=P)),
                             (K.wib[:], io["wi_b"]), (K.wob[:], io["wo_b"].partition_broadcast(P))):
                sp.dma_start(dst, src).then_inc(K.fin_in, DMA)
            sp.wait_ge(K.fin_in, 7 * DMA)


        @block.vector
        def _(v):
            ch = Chain(v, own)

            def join(b):
                n = slice(b * BT, b * BT + BT)
                v.wait_ge(flipped, b + 1)
                v.wait_ge(x_in[min(b, 1)], DMA if b == 0 else (B - 1) * DMA)
                ch.link(v.tensor_tensor(prod[:], fs[:], K.G0[:, n, :], ALU.mult))
                v.nop().then_inc(flip_read, 1)
                ch.link(v.tensor_tensor(X1[:, n, :], X[:, n, :], prod[:], ALU.add))
                row_stats(v, ch, X1, st, b, 1e-5, var_ready)
                apply_norm(v, ch, X1, XN, st, b, rstd_ready, b + 1)
                v.nop().then_inc(xn_ready, 1)

            lg = ZL[:, :, 0:E]

            def best_gate():
                v.wait_ge(wz_in, 2 * DMA)
                v.wait_ge(z_out, B)
                ch.link(v.tensor_tensor(lg, lg, mid_axis(gb[:], NT), ALU.add))
                ch.link(v.tensor_reduce(col[:, 0, :], lg, AX_X, ALU.max))
                v.tensor_tensor(lg, lg, last_axis(col[:, 0, :], E), ALU.subtract).then_inc(max_sub, 1)

            def route():
                v.wait_ge(exp_ready, 1)
                v.wait_ge(iota_ready, 1)
                ch.link(v.tensor_scalar(r1[:], lg, 1.0, float(E), ALU.is_lt, ALU.mult))
                ch.link(v.tensor_tensor(r1[:], r1[:], io8[:], ALU.add))
                ch.link(v.tensor_reduce(col[:, 1, :], r1[:], AX_X, ALU.min))
                ch.link(v.tensor_tensor(hot[:], io8[:], last_axis(col[:, 1, :], E), ALU.is_equal))
                for r in range(R):
                    ins = v.tensor_tensor(K.ZM[:, :, 0:ER].rearrange("p t (e r) -> p t e r", r=R)[:, :, :, r],
                                          ZL[:, :, E:NZ].rearrange("p t (e r) -> p t e r", r=R)[:, :, :, r], hot[:], ALU.mult)
                ch.link(ins)
                for k in (1, 2):
                    ins = v.tensor_copy(K.ZM[:, :, k * ER:k * ER + ER], K.ZM[:, :, 0:ER])
                ch.link(ins)

            def split_lora():
                v.wait_ge(K.fin_in, 7 * DMA)
                ch.link(v.tensor_copy(K.lb[:], lbf[:]))
                ch.link(v.tensor_tensor(K.lb[ER:2 * ER, :], lbf[ER:2 * ER, :], K.lb[ER:2 * ER, :], ALU.subtract))

            def scans(b):
                lam = LAM[:, b % 2, :]
                v.wait_ge(act_out, 5 * b + 5)
                v.wait_ge(base_ready, 1)
                ch.link(v.tensor_scalar(lam, lam, 0.2, 1.0, ALU.mult, ALU.add))
                ch.link(v.tensor_scalar(lam, lam, base[:, 0:1], 0.0, ALU.mult, ALU.max))
                ch.link(v.tensor_scalar(lam, lam, 0.9995, None, ALU.min))
                for f in range(FE):
                    n = b * FE + f
                    if f == Z_AT + 1:
                        v.wait_ge(z_ready, b + 1)
                        v.tensor_copy(ZL[:, b * BT:b * BT + BT, :], zp).then_inc(z_out, 1)
                    if b == B - 1 and f == Z_AT + 2:
                        best_gate()
                    if b == 1 and f == 0:
                        split_lora()
                    if b == B - 1 and f == Z_AT + 4:
                        route()
                    v.wait_ge(made, 13 * b + 5 + f + 1)
                    if n >= 2:
                        v.wait_ge(scanned, n - 1)
                    v.tensor_tensor(KV[:, n % 2, :], pj[(13 * b + 5 + f) % 2][:], KT[:, b % 2, :],
                                    ALU.mult).then_inc(kv_read, 1)
                    v.wait_ge(kv_read, n + 1)
                    if n >= 2:
                        v.wait_ge(weighed, n - 1)
                    v.tensor_tensor_scan(SC[:, n % 2, :], lam, KV[:, n % 2, :], 0.0, ALU.mult,
                                         ALU.add).then_inc(scanned, 1)

            join(0)
            for b in range(B):
                if b + 1 < B:
                    join(b + 1)
                scans(b)

        @block.gpsimd
        def _(g):
            g.iota(io8[:], pattern=[[0, NT], [1, E]], base=0, channel_multiplier=0,
                   allow_small_or_imprecise_dtypes=True).then_inc(iota_ready, 1)
            g.memset(neg_half[:], -0.5).then_inc(half_ready, 1)
            g.wait_ge(half_ready, 1)

            g.memset(flip[:], 0.0).then_inc(half_ready, 1)
            g.wait_ge(half_ready, 2)
            g.affine_select(out=flip[:], in_=flip[:], compare_op=ALU.not_equal, fill=1.0, base=1 - P,
                            pattern=[[1, P]], channel_multiplier=1).then_inc(flip_ready, 1)

            def rstd(b):
                n = slice(b * BT, b * BT + BT)
                g.wait_ge(var_ready, b + 1)
                g.tensor_tensor(st.rstd[:, n], st.var[:, n], neg_half[:, n], ALU.pow).then_inc(rstd_ready, 1)

            rstd(0)
            for b in range(B):
                if b + 1 < B:
                    rstd(b + 1)
                for f in range(FE):
                    n = b * FE + f
                    g.wait_ge(scanned, n + 1)
                    if n >= 2:
                        g.wait_ge(weighed_used, n - 1)
                    g.tensor_tensor(WT[:, n % 2, :], SC[:, n % 2, :], QT[:, b % 2, :], ALU.mult).then_inc(weighed, 1)

        @block.scalar
        def _(act):
            act.wait_ge(w_in, 7 * DMA)
            act.activation(base[:], base[:], ACT.Sigmoid).then_inc(base_ready, 1)
            for b in range(B):
                for i in range(5):
                    act.wait_ge(made, 13 * b + i + 1)
                    src = pj[(13 * b + i) % 2]
                    if b >= 2 and i == 1:
                        act.wait_ge(weighed, FE * (b - 1))
                        act.wait_ge(scanned, FE * (b - 1))
                    if i == 0:
                        ins = act.copy(XNT[:, b * S:b * S + S], src[:])
                    elif i == 1:
                        ins = act.copy(QT[:, b % 2, :], src[:])
                    elif i == 2:
                        ins = act.copy(KT[:, b % 2, :], src[:])
                    elif i == 3:
                        ins = act.activation(C1[:], src[0:D // 4, :], ACT.Tanh, bias=c1b[:, 0:1])
                    else:
                        ins = act.activation(LAM[:, b % 2, :], src[:], ACT.Sigmoid, bias=c2b[:, 0:1])
                    ins.then_inc(act_out, 1)
                if b == B - 1:
                    act.wait_ge(max_sub, 1)
                    act.activation(ZL[:, :, 0:E], ZL[:, :, 0:E], ACT.Exp).then_inc(exp_ready, 1)
                act.wait_ge(s1_ready, b + 1)
                act.copy(K.S1[:, b * BT:b * BT + BT, :], so[:]).then_inc(s1_out, 1)

        @block.tensor
        def _(pe):
            def halves(dst, lhs, src, m=P):
                for c in range(S // CH):
                    mm = pe.matmul(dst[0:m, c * CH:c * CH + CH], lhs, src[:, c * CH:c * CH + CH], start=True, stop=True)
                mm.then_inc(made, 1)

            def share(b, f):
                n = b * FE + f
                pe.wait_ge(weighed, n + 1)
                if f == 0 and b >= 1:
                    pe.wait_ge(s1_out, b)
                for t in range(BT):
                    mm = pe.matmul(so[:, t, :], WT[:, n % 2, t * P:t * P + P], wo[:, f, :],
                                   start=(f == 0 and t % 4 == 0), stop=(f == FE - 1), skip_group_check=True)
                mm.then_inc(weighed_used, 1)
                if f == FE - 1:
                    pe.wait_ge(weighed_used, n + 1)
                    pe.nop().then_inc(s1_ready, 1)

            def gate_rows(b):
                pe.wait_ge(wz_in, 2 * DMA)
                pe.wait_ge(flip_read, min(b + 2, B))
                for t in range(BT):
                    mm = pe.matmul(zp[:, t, :], XNT[:, (b * BT + t) * P:(b * BT + t + 1) * P], wz[:], start=True, stop=True)
                mm.then_inc(z_ready, 1)

            def unflip(b):
                if b >= 1:
                    pe.wait_ge(flip_read, b)
                if b >= 2:
                    pe.wait_ge(z_out, b - 1)
                for t in range(BT):
                    mm = pe.matmul(fs[:, t, :], flip[:], K.SACC[:, b * BT + t, :], start=True, stop=True)
                mm.then_inc(flipped, 1)

            pe.wait_ge(flip_ready, 1)
            unflip(0)
            for b in range(B):
                if b + 1 < B:
                    unflip(b + 1)
                pe.wait_ge(xn_ready, b + 1)
                if b >= 1:
                    pe.wait_ge(kv_read, FE * b)
                dst = pj[13 * b % 2]
                for t in range(BT):
                    mm = pe.transpose(dst[:, t * P:t * P + P], XN[:, b * BT + t, :], K.ident[:])
                mm.then_inc(made, 1)
                pe.wait_ge(act_out, 5 * b + 1)
                if b == 0:
                    pe.wait_ge(w_in, 7 * DMA)
                x = XNT[:, b * S:b * S + S]
                halves(pj[(13 * b + 1) % 2], wq[:], x)
                halves(pj[(13 * b + 2) % 2], wk[:], x)
                pe.wait_ge(act_out, 5 * b + 2)
                halves(pj[(13 * b + 3) % 2], c1w[:], x, D // 4)
                pe.wait_ge(act_out, 5 * b + 4)
                halves(pj[(13 * b + 4) % 2], c2w[:], C1[:])
                if b == 0:
                    pe.wait_ge(vo_in, 2 * DMA)
                for f in range(FE):
                    if f == Z_AT:
                        gate_rows(b)
                    if f == 1:
                        pe.wait_ge(act_out, 5 * b + 5)
                    if f >= 2:
                        pe.wait_ge(kv_read, FE * b + f - 1)
                    halves(pj[(13 * b + 5 + f) % 2], wv[:, f, :], x)
                    if f >= 2:
                        share(b, f - 2)
                share(b, FE - 2)
                share(b, FE - 1)


def finish(nc, K, io, sb, ps, sem):
    zt_ready, zt_out, h_ready, h_out, o_ready, y_ready = (sem("zt_ready"), sem("zt_out"), sem("fh_ready"),
                                                          sem("fh_out"), sem("fo_ready"), sem("y_ready"))
    g1_ready, mixed, x2_ready, out_wr = sem("g1_ready"), sem("mixed"), sem("x2_ready"), sem("out_wr")
    lb, wi, wo, wib, wob, ZM = K.lb, K.wi, K.wo1, K.wib, K.wob, K.ZM
    ZT = sb("z_t_parts", [3 * ER, B * S], BF16)
    z_up = sem("z_up")
    hT = [sb(f"fhid{i}", [P, FT, CH]) for i in range(2)]
    Y = [sb(f"y{i}", [P, 4, D]) for i in range(2)]
    pb = [ps(f"fin_ps{i}", [P, CH]) for i in range(8)]
    NJ = NT // 4

    with nc.Block() as block:

        @block.sync
        def _(sp):
            for j in range(NJ):
                sp.wait_ge(x2_ready, j + 1)
                b, t = j // 2, 4 * (j % 2)
                sp.dma_start(io["out"][b].rearrange("(t p) d -> p t d", p=P)[:, t:t + 4, :],
                             K.X[:, 4 * j:4 * j + 4, :]).then_inc(out_wr, DMA)
            sp.wait_ge(out_wr, DMA * NJ)

        @block.gpsimd
        def _(g):
            for j in range(NJ):
                g.wait_ge(mixed, j + 1)
                n = slice(4 * j, 4 * j + 4)
                g.tensor_tensor(K.X[:, n, :], K.X[:, n, :], K.S1[:, n, :], ALU.add).then_inc(x2_ready, 1)

        @block.tensor
        def _(pe):
            for j in range(NJ):
                for t in range(4):
                    mm = pe.transpose(pb[j][0:3 * ER, t * P:t * P + P], ZM[:, 4 * j + t, :], K.ident[:])
                mm.then_inc(zt_ready, 1)
            pe.wait_ge(zt_out, NJ)

            def hidden(j):
                for i in range(FT):
                    if j >= 1:
                        pe.wait_ge(h_out, FT * (j - 1) + i + 1)
                    pe.matmul(pb[i][:], wi[:, i * P:i * P + P], K.XNT[:, j * CH:j * CH + CH], start=True, stop=False)
                    pe.matmul(pb[i][:], lb[:, i * P:i * P + P], ZT[:, j * CH:j * CH + CH],
                              start=False, stop=True).then_inc(h_ready, 1)

            def out(j):
                s = j % 2
                o = pb[4 + s]
                if j >= 2:
                    pe.wait_ge(y_ready, j - 1)
                for i in range(FT):
                    pe.wait_ge(h_out, FT * j + i + 1)
                    for c in range(4):
                        mm = pe.matmul(o[:, c * P:c * P + P], hT[s][:, i, c * P:c * P + P], wo[:, i, :],
                                       start=(i == 0 and c == 0), stop=(i == FT - 1), skip_group_check=True)
                mm.then_inc(o_ready, 1)

            hidden(0)
            for j in range(NJ):
                if j + 1 < NJ:
                    hidden(j + 1)
                out(j)

        @block.scalar
        def _(act):
            for j in range(NJ):
                act.wait_ge(zt_ready, j + 1)
                act.copy(ZT[:, j * CH:j * CH + CH], pb[j][0:3 * ER, :]).then_inc(z_up, 1)

            def relu(j):
                for i in range(FT):
                    act.wait_ge(h_ready, FT * j + i + 1)
                    if j >= 2 and i == 0:
                        act.wait_ge(o_ready, j - 1)
                    act.activation(hT[j % 2][:, i, :], pb[i][:], ACT.Relu, bias=wib[:, i:i + 1]).then_inc(h_out, 1)

            def gate(j):
                act.wait_ge(y_ready, j + 1)
                act.activation(Y[j % 2][:], Y[j % 2][:], ACT.Silu).then_inc(g1_ready, 1)

            for j in range(NJ):
                relu(j)
                if j >= 1:
                    gate(j - 1)
            gate(NJ - 1)

        @block.vector
        def _(v):
            low = slice(2 * ER, 3 * ER)
            for j in range(NJ):
                v.wait_ge(z_up, j + 1)
                v.tensor_tensor(ZT[low, j * CH:j * CH + CH], pb[j][low, :], ZT[low, j * CH:j * CH + CH],
                                ALU.subtract).then_inc(zt_out, 1)
            for j in range(NJ):
                s, n = j % 2, slice(4 * j, 4 * j + 4)
                v.wait_ge(o_ready, j + 1)
                if j >= 2:
                    v.wait_ge(mixed, j - 1)
                v.tensor_tensor(Y[s][:], pb[4 + s][:].rearrange("p (t d) -> p t d", d=D), mid_axis(wob[:], 4),
                                ALU.add).then_inc(y_ready, 1)
                v.wait_ge(g1_ready, j + 1)
                v.tensor_tensor(K.S1[:, n, :], K.S1[:, n, :], Y[s][:], ALU.mult).then_inc(mixed, 1)


def program(nc, io):
    with ExitStack() as outer:
        def maker(stack):
            def sb(name, shape, dt=F32):
                return stack.enter_context(nc.sbuf_tensor(name, shape, dt))

            def ps(name, shape, dt=F32):
                return stack.enter_context(nc.psum_tensor(name, shape, dt))
            return sb, ps

        def sem(name):
            return outer.enter_context(nc.semaphore(name))

        sb, _ = maker(outer)
        K = Shared()
        K.ident = sb("ident", [P, P])
        K.G0, K.SACC = sb("g0", [P, NT, D]), sb("s0", [P, NT, D])
        K.disp = nc.dram_tensor("dispatch", [E * CAP, D], F32, kind="Internal").ap()
        K.eout = nc.dram_tensor("expert_rows", [E * CAP, D], F32, kind="Internal").ap()
        K.fscr = nc.dram_tensor("bias_by_distance", [H, FLEN], F32, kind="Internal").ap()
        K.vscr = nc.dram_tensor("v_parts", [NT, P, H, 2 * DH], BF16, kind="Internal").ap()
        K.qkscr = nc.dram_tensor("qk_parts", [B * G, P, 4, S], BF16, kind="Internal").ap()

        def run(block):
            with ExitStack() as own:
                block_sb, block_ps = maker(own)
                block(nc, K, io, block_sb, block_ps, sem)

        K.qk_in, K.tab_in = [[sem(f"{n}_in{s}") for s in range(2)] for n in ("aqk", "at")]
        with ExitStack() as heads:
            sb_in, _ = maker(heads)
            K.QS = [sb_in(f"q_hi_lo{s}", [P, S], BF16) for s in range(2)]
            K.QX = [sb_in(f"q_lo_hi{s}", [P, S], BF16) for s in range(2)]
            K.KS = [sb_in(f"k_hi_hi{s}", [P, S], BF16) for s in range(2)]
            K.KL = [sb_in(f"k_lo_lo{s}", [P, S], BF16) for s in range(2)]
            K.TB = [sb_in(f"bias_tab{s}", [P, TAB]) for s in range(2)]
            with ExitStack() as layer0:
                sb0, _ = maker(layer0)
                K.XNT = sb0("xn_t", [P, B * S])
                K.wv, K.wv_in = sb0("wv", [P, H * DH]), sem("wv_in")
                K.COS, K.SIN = sb0("cos_table", [P, S]), sb0("sin_table", [P, S])
                K.coef_moe, K.gather_idx = sb0("coef_moe", [P, NT]), sb0("gather_idx", [P, NT], U32)
                with ExitStack() as moe:
                    sb_moe, _ = maker(moe)
                    K.XN, K.coef_res = sb_moe("xn", [P, NT, D]), sb_moe("coef_res", [P, NT])
                    K.w1 = [sb_moe(f"w1_{i}", [P, F]) for i in range(RING)]
                    K.w2 = [sb_moe(f"w2_{i}", [P, FT, D]) for i in range(RING)]
                    K.dx = [sb_moe(f"dispatched{i}", [P, CAP // P, D]) for i in range(RING)]
                    K.w_in, K.d_in = [sem(f"w_in{s}") for s in range(RING)], [sem(f"d_in{s}") for s in range(RING)]
                    run(prepare)
                    run(experts)
                K.MOE = sb0("moe_rows", [P, NT, D])
                run(project)
            run(attend)
        K.X = sb("x1", [P, NT, D])
        K.XN, K.XNT, K.S1 = sb("xn1", [P, NT, D]), sb("xn1_t", [P, B * S]), sb("s1", [P, NT, D])
        K.lb, K.wi, K.wo1 = sb("lora_b_parts", [3 * ER, F], BF16), sb("wi", [P, F]), sb("wo_t", [P, FT, D])
        K.wib, K.wob = sb("wi_b", [P, FT]), sb("wo_b", [P, D])
        K.ZM, K.fin_in = sb("z_masked", [P, NT, 3 * ER]), sem("fin_in")
        run(recur)
        run(finish)


def layouts(inp):
    import numpy as np
    a = {k: np.ascontiguousarray(v) for k, v in inp.items()}
    c = np.ascontiguousarray
    qkv = a["L0_attn_qkv_w"].reshape(3, H, DH, D)

    def pair(w):
        return w.reshape(G, P, D).transpose(0, 2, 1)

    def swapped(w):
        return np.concatenate([w[:, DH // 2:], w[:, :DH // 2]], axis=1)
    wqk = np.stack([pair(qkv[0]), pair(swapped(qkv[0])), pair(qkv[1]), pair(swapped(qkv[1]))], axis=2)
    wo = a["L0_attn_out_w"].reshape(D, H, DH).transpose(1, 2, 0)
    wo2 = np.concatenate([wo, wo], axis=1)
    he = a["L1_attn_v_w"].reshape(H, 8, D)
    vrep = np.repeat(he.transpose(2, 1, 0)[:, :, :, None], 8, axis=3).reshape(D, 8, P)
    ow = a["L1_attn_o_w"].reshape(D, H, 8)
    orep = np.repeat(ow.transpose(1, 2, 0)[:, None], 8, axis=1).reshape(P, 8, D)
    cs2 = np.repeat(a["L1_attn_cs_w2"].T[:, :, None], 8, axis=2).reshape(D // 4, P)
    return dict(
        x=a["L0_attn_x"], wqk=c(wqk), wv=c(a["L0_attn_qkv_w"][2 * H * DH:].T), wo2=c(wo2),
        bias_p=a["L0_attn_bias_p"].reshape(H, 1), bias_a=a["L0_attn_bias_a"].reshape(H, 1), freqs=a["L0_attn_rope_freqs"],
        attn_nw=a["L0_ffn_attn_nw"], attn_nb=a["L0_ffn_attn_nb"], wg=a["L0_ffn_wg"], inter_w=a["L0_ffn_inter_w"],
        inter_b=c(a["L0_ffn_inter_b"].reshape(E, FT, P).transpose(2, 0, 1)), output_w=a["L0_ffn_output_w"], output_b=a["L0_ffn_output_b"],
        res_inter_w=a["L0_ffn_res_inter_w"], res_inter_b=c(a["L0_ffn_res_inter_b"].reshape(FT, P).T),
        res_output_w=a["L0_ffn_res_output_w"], res_output_b=a["L0_ffn_res_output_b"], res_coef=a["L0_ffn_res_coef"],
        q_w=c(a["L1_attn_q_w"].T), k_w=c(a["L1_attn_k_w"].T), v_w=c(vrep), o_w=c(orep), cs_w1=c(a["L1_attn_cs_w1"].T),
        cs_b1=a["L1_attn_cs_b1"].reshape(D // 4, 1), cs_w2=c(cs2),
        cs_b2=c(np.repeat(a["L1_attn_cs_b2"], 8).reshape(P, 1)), decay=a["L1_attn_decay_params"].reshape(P, 1),
        wz=c(np.concatenate([a["L1_ffn_gate_W"].T, a["L1_ffn_lora_A"].reshape(E * R, D).T], axis=1)),
        gate_b=a["L1_ffn_gate_b"], wi=c(a["L1_ffn_wi_W"].T), wi_b=c(a["L1_ffn_wi_b"].reshape(FT, P).T), wo_t=c(a["L1_ffn_wo_W"].T),
        wo_b=a["L1_ffn_wo_b"], lora_b=c(a["L1_ffn_lora_B"].transpose(0, 2, 1).reshape(E * R, F)),
    )


def kernel(**inputs):
    import numpy as np
    import concourse.bacc as bacc
    from concourse.bass_utils import run_bass_kernel_spmd

    nc = bacc.Bacc("TRN2", target_bir_lowering=False, num_devices=1)
    arrays, aps = {}, {}
    for name, a in layouts(inputs).items():
        arrays[f"in_{name}"] = a
        aps[name] = nc.dram_tensor(f"in_{name}", a.shape, mybir.dt.from_np(a.dtype), kind="ExternalInput").ap()
    aps["out"] = nc.dram_tensor("out_0", [B, S, D], F32, kind="ExternalOutput").ap()
    program(nc, aps)
    r = run_bass_kernel_spmd(nc, [arrays], core_ids=[0])
    return r.results[0]["out_0"]
```
